# Optimizing a Trainium2 kernel written in Bass

```python
import numpy as np
import jax
import jax.numpy as jnp

def _softmax(x, axis=-1):
    return jax.nn.softmax(x, axis=axis)

def _gelu(x):
    return jax.nn.gelu(x, approximate=True)

def _silu(x):
    return jax.nn.silu(x)

def _sigmoid(x):
    return jax.nn.sigmoid(x)

def _layernorm(x, axis=-1, eps=1e-05):
    m = jnp.mean(x, axis=axis, keepdims=True)
    v = jnp.var(x, axis=axis, keepdims=True)
    return (x - m) / jnp.sqrt(v + eps)

def _scatter_add(tgt, idx, src, axis=0):
    return tgt.at[idx].add(src)

def _segment_sum(src, seg, n):
    return jax.ops.segment_sum(src, seg, n)
kernel_name = 'mk_prb_d2_jaxref_r8_d4d57d'

def setup_inputs(seed: int=0):
    np.random.seed(seed)
    _w = jnp.asarray

    def _L0_attn_setup():
        import jax, jax.numpy as jnp
        import numpy as np
        from jax import lax
        D_OUTER, D, N, K = (128, 256, 16, 4)
        B_SZ, L = (2, 128)

        def _forward(X, ln_g, ln_b, W_up1, conv_w, conv_b, W_ll, b_ll, A_log, W_up2, W_down, b_down):
            X_res = X
            mu = jnp.mean(X, axis=-1, keepdims=True)
            var = jnp.var(X, axis=-1, keepdims=True)
            Xn = (X - mu) * lax.rsqrt(var + 1e-05) * ln_g + ln_b
            X_main = jnp.einsum('bld,ed->ble', Xn, W_up1)
            x_ncl = X_main.transpose(0, 2, 1)
            y = lax.conv_general_dilated(x_ncl, conv_w, window_strides=(1,), padding=[(K - 1, 0)], feature_group_count=D, dimension_numbers=('NCH', 'OIH', 'NCH'))
            X_main = (y + conv_b[None, :, None]).transpose(0, 2, 1)
            X_main = jax.nn.silu(X_main)
            pp = jnp.einsum('bld,ed->ble', X_main, W_ll) + b_ll
            delta = jax.nn.softplus(pp[..., :D])
            Bm = pp[..., D:D + N]
            Cm = pp[..., D + N:]
            A = -jnp.exp(A_log)
            dA = jnp.einsum('bld,dn->bldn', delta, A)
            A_bar = jnp.exp(dA)
            zoh = (A_bar - 1.0) / dA
            B_bar = zoh * (delta[..., None] * Bm[:, :, None, :])
            U = X_main[..., None] * B_bar
            H0 = jnp.zeros((X.shape[0], D, N), jnp.float32)

            def step(H, inp):
                Ab_t, U_t, C_t = inp
                H = Ab_t * H + U_t
                y_t = jnp.einsum('bn,bdn->bd', C_t, H)
                return (H, y_t)
            _, Ys = lax.scan(step, H0, (A_bar.swapaxes(0, 1), U.swapaxes(0, 1), Cm.swapaxes(0, 1)))
            Y_ssm = Ys.swapaxes(0, 1)
            X_gate = jax.nn.silu(jnp.einsum('bld,ed->ble', Xn, W_up2))
            Y = Y_ssm * X_gate
            Y_proj = jnp.einsum('bld,ed->ble', Y, W_down) + b_down
            return X_res + Y_proj
        key = jax.random.key(seed)
        ks = jax.random.split(key, 12)
        s = 0.02
        X = jax.random.normal(ks[0], (B_SZ, L, D_OUTER), jnp.float32)
        ln_g = jnp.ones((D_OUTER,), jnp.float32)
        ln_b = jnp.zeros((D_OUTER,), jnp.float32)
        W_up1 = jax.random.normal(ks[1], (D, D_OUTER), jnp.float32) * s
        conv_w = jax.random.normal(ks[2], (D, 1, K), jnp.float32) * 0.1
        conv_b = jax.random.normal(ks[3], (D,), jnp.float32) * 0.1
        W_ll = jax.random.normal(ks[4], (2 * N + D, D), jnp.float32) * s
        b_ll = jax.random.normal(ks[5], (2 * N + D,), jnp.float32) * 0.1
        A_log = jnp.log(jnp.tile(jnp.arange(1, N + 1, dtype=jnp.float32), (D, 1)))
        W_up2 = jax.random.normal(ks[6], (D, D_OUTER), jnp.float32) * s
        W_down = jax.random.normal(ks[7], (D_OUTER, D), jnp.float32) * s
        b_down = jax.random.normal(ks[8], (D_OUTER,), jnp.float32) * 0.1
        return {'X': X, 'ln_g': ln_g, 'ln_b': ln_b, 'W_up1': W_up1, 'conv_w': conv_w, 'conv_b': conv_b, 'W_ll': W_ll, 'b_ll': b_ll, 'A_log': A_log, 'W_up2': W_up2, 'W_down': W_down, 'b_down': b_down}
    _L0_attn_in = _L0_attn_setup()

    def _L0_ffn_setup():
        import jax, jax.numpy as jnp
        import numpy as np
        from math import ceil
        CAPACITY_FACTOR = 2.0
        MIN_CAPACITY = 4
        key = jax.random.key(seed)
        ks = jax.random.split(key, 4)
        B, S, D, Di, E = (4, 256, 128, 512, 8)
        x = jax.random.normal(ks[0], (B, S, D), dtype=jnp.float32)
        Wr = jax.random.normal(ks[1], (D, E), dtype=jnp.float32) * D ** (-0.5)
        W1 = jax.random.normal(ks[2], (E, D, Di), dtype=jnp.float32) * D ** (-0.5)
        b1 = jnp.zeros((E, Di), dtype=jnp.float32)
        W2 = jax.random.normal(ks[3], (E, Di, D), dtype=jnp.float32) * Di ** (-0.5)
        b2 = jnp.zeros((E, D), dtype=jnp.float32)
        return {'x': x, 'Wr': Wr, 'W1': W1, 'b1': b1, 'W2': W2, 'b2': b2}
    _L0_ffn_in = _L0_ffn_setup()

    def _L1_attn_setup():
        import jax, jax.numpy as jnp
        import numpy as np
        HIDDEN = 128
        HEADS = 8
        HEAD = HIDDEN // HEADS
        EPS = 1e-05

        def _gammas():
            lo = np.log(1.0 / 512.0)
            hi = np.log(1.0 / 32.0)
            lin = np.linspace(lo, hi, HEADS)
            return jnp.asarray(1.0 - np.exp(lin), dtype=jnp.float32)

        def _decay_mask(S, gammas):
            idx = jnp.arange(S)
            diff = idx[:, None] - idx[None, :]
            causal = diff >= 0
            safe = jnp.where(causal, diff, 0).astype(jnp.float32)
            D = jnp.where(causal[None], gammas[:, None, None] ** safe[None], 0.0)
            return D

        def _msr_forward(x, Wq, Wk, Wv, W1, W2, gn_w, gn_b):
            B, S, _ = x.shape
            xh = x.reshape(B, S, HEADS, HEAD)
            q = jnp.einsum('bshd,hde->bshe', xh, Wq)
            k = jnp.einsum('bshd,hde->bshe', xh, Wk)
            v = jnp.einsum('bshd,hde->bshe', xh, Wv)
            D = _decay_mask(S, _gammas())
            scores = jnp.einsum('bnhd,bmhd->bhnm', q, k) * D[None]
            ret = jnp.einsum('bhnm,bmhd->bnhd', scores, v)
            mu = jnp.mean(ret, axis=-1, keepdims=True)
            var = jnp.var(ret, axis=-1, keepdims=True)
            ret = (ret - mu) * jax.lax.rsqrt(var + EPS)
            ret = ret.reshape(B, S, HIDDEN) * gn_w + gn_b
            gated = x @ W1
            out = gated * jax.nn.sigmoid(gated) + ret
            return out @ W2
        key = jax.random.key(seed)
        ks = jax.random.split(key, 7)
        B, S = (2, 256)
        x = jax.random.normal(ks[0], (B, S, HIDDEN), dtype=jnp.float32)
        Wq = jax.random.normal(ks[1], (HEADS, HEAD, HEAD), dtype=jnp.float32) / HEAD
        Wk = jax.random.normal(ks[2], (HEADS, HEAD, HEAD), dtype=jnp.float32) / HEAD
        Wv = jax.random.normal(ks[3], (HEADS, HEAD, HEAD), dtype=jnp.float32) / HEAD
        W1 = jax.random.normal(ks[4], (HIDDEN, HIDDEN), dtype=jnp.float32) / HIDDEN
        W2 = jax.random.normal(ks[5], (HIDDEN, HIDDEN), dtype=jnp.float32) / HIDDEN
        gn_w = jnp.ones((HIDDEN,), dtype=jnp.float32)
        gn_b = jnp.zeros((HIDDEN,), dtype=jnp.float32)
        return {'x': x, 'Wq': Wq, 'Wk': Wk, 'Wv': Wv, 'W1': W1, 'W2': W2, 'gn_w': gn_w, 'gn_b': gn_b}
    _L1_attn_in = _L1_attn_setup()

    def _L1_ffn_setup():
        import jax, jax.numpy as jnp
        import numpy as np
        D_MODEL = 128
        D_HIDDEN = 512
        NUM_BANKS = 16
        NUM_SELECTED = 2
        key = jax.random.key(seed)
        ks = jax.random.split(key, 7)
        s = 0.02
        return {'tensor': jax.random.normal(ks[0], (4, 128, D_MODEL), dtype=jnp.float32), 'Wr': jax.random.normal(ks[1], (D_MODEL, NUM_BANKS), dtype=jnp.float32) * s, 'br': jnp.zeros((NUM_BANKS,), dtype=jnp.float32), 'W1': jax.random.normal(ks[2], (NUM_BANKS, D_MODEL, D_HIDDEN), dtype=jnp.float32) * s, 'b1': jnp.zeros((NUM_BANKS, D_HIDDEN), dtype=jnp.float32), 'W2': jax.random.normal(ks[3], (NUM_BANKS, D_HIDDEN, D_MODEL), dtype=jnp.float32) * s, 'b2': jnp.zeros((NUM_BANKS, D_MODEL), dtype=jnp.float32)}
    _L1_ffn_in = _L1_ffn_setup()
    _d = {'L0_attn_X': _L0_attn_in['X'], 'L0_attn_ln_g': _L0_attn_in['ln_g'], 'L0_attn_ln_b': _L0_attn_in['ln_b'], 'L0_attn_W_up1': _L0_attn_in['W_up1'], 'L0_attn_conv_w': _L0_attn_in['conv_w'], 'L0_attn_conv_b': _L0_attn_in['conv_b'], 'L0_attn_W_ll': _L0_attn_in['W_ll'], 'L0_attn_b_ll': _L0_attn_in['b_ll'], 'L0_attn_A_log': _L0_attn_in['A_log'], 'L0_attn_W_up2': _L0_attn_in['W_up2'], 'L0_attn_W_down': _L0_attn_in['W_down'], 'L0_attn_b_down': _L0_attn_in['b_down'], 'L0_ffn_Wr': _L0_ffn_in['Wr'], 'L0_ffn_W1': _L0_ffn_in['W1'], 'L0_ffn_b1': _L0_ffn_in['b1'], 'L0_ffn_W2': _L0_ffn_in['W2'], 'L0_ffn_b2': _L0_ffn_in['b2'], 'L1_attn_Wq': _L1_attn_in['Wq'], 'L1_attn_Wk': _L1_attn_in['Wk'], 'L1_attn_Wv': _L1_attn_in['Wv'], 'L1_attn_W1': _L1_attn_in['W1'], 'L1_attn_W2': _L1_attn_in['W2'], 'L1_attn_gn_w': _L1_attn_in['gn_w'], 'L1_attn_gn_b': _L1_attn_in['gn_b'], 'L1_ffn_Wr': _L1_ffn_in['Wr'], 'L1_ffn_br': _L1_ffn_in['br'], 'L1_ffn_W1': _L1_ffn_in['W1'], 'L1_ffn_b1': _L1_ffn_in['b1'], 'L1_ffn_W2': _L1_ffn_in['W2'], 'L1_ffn_b2': _L1_ffn_in['b2']}
    _x0 = _d['L0_attn_X']
    _d['L0_attn_X'] = jax.random.normal(jax.random.fold_in(jax.random.key(seed), 1), (8, 256, 128), dtype=_x0.dtype)
    del _x0
    return _d

def reference(L0_attn_X, L0_attn_ln_g, L0_attn_ln_b, L0_attn_W_up1, L0_attn_conv_w, L0_attn_conv_b, L0_attn_W_ll, L0_attn_b_ll, L0_attn_A_log, L0_attn_W_up2, L0_attn_W_down, L0_attn_b_down, L0_ffn_Wr, L0_ffn_W1, L0_ffn_b1, L0_ffn_W2, L0_ffn_b2, L1_attn_Wq, L1_attn_Wk, L1_attn_Wv, L1_attn_W1, L1_attn_W2, L1_attn_gn_w, L1_attn_gn_b, L1_ffn_Wr, L1_ffn_br, L1_ffn_W1, L1_ffn_b1, L1_ffn_W2, L1_ffn_b2):

    def _L0_attn_ref(X, ln_g, ln_b, W_up1, conv_w, conv_b, W_ll, b_ll, A_log, W_up2, W_down, b_down):
        import jax, jax.numpy as jnp
        import numpy as np
        from jax import lax
        D_OUTER, D, N, K = (128, 256, 16, 4)
        B_SZ, L = (2, 128)

        def _forward(X, ln_g, ln_b, W_up1, conv_w, conv_b, W_ll, b_ll, A_log, W_up2, W_down, b_down):
            X_res = X
            mu = jnp.mean(X, axis=-1, keepdims=True)
            var = jnp.var(X, axis=-1, keepdims=True)
            Xn = (X - mu) * lax.rsqrt(var + 1e-05) * ln_g + ln_b
            X_main = jnp.einsum('bld,ed->ble', Xn, W_up1)
            x_ncl = X_main.transpose(0, 2, 1)
            y = lax.conv_general_dilated(x_ncl, conv_w, window_strides=(1,), padding=[(K - 1, 0)], feature_group_count=D, dimension_numbers=('NCH', 'OIH', 'NCH'))
            X_main = (y + conv_b[None, :, None]).transpose(0, 2, 1)
            X_main = jax.nn.silu(X_main)
            pp = jnp.einsum('bld,ed->ble', X_main, W_ll) + b_ll
            delta = jax.nn.softplus(pp[..., :D])
            Bm = pp[..., D:D + N]
            Cm = pp[..., D + N:]
            A = -jnp.exp(A_log)
            dA = jnp.einsum('bld,dn->bldn', delta, A)
            A_bar = jnp.exp(dA)
            zoh = (A_bar - 1.0) / dA
            B_bar = zoh * (delta[..., None] * Bm[:, :, None, :])
            U = X_main[..., None] * B_bar
            H0 = jnp.zeros((X.shape[0], D, N), jnp.float32)

            def step(H, inp):
                Ab_t, U_t, C_t = inp
                H = Ab_t * H + U_t
                y_t = jnp.einsum('bn,bdn->bd', C_t, H)
                return (H, y_t)
            _, Ys = lax.scan(step, H0, (A_bar.swapaxes(0, 1), U.swapaxes(0, 1), Cm.swapaxes(0, 1)))
            Y_ssm = Ys.swapaxes(0, 1)
            X_gate = jax.nn.silu(jnp.einsum('bld,ed->ble', Xn, W_up2))
            Y = Y_ssm * X_gate
            Y_proj = jnp.einsum('bld,ed->ble', Y, W_down) + b_down
            return X_res + Y_proj
        return _forward(X, ln_g, ln_b, W_up1, conv_w, conv_b, W_ll, b_ll, A_log, W_up2, W_down, b_down)

    def _L0_ffn_ref(x, Wr, W1, b1, W2, b2):
        import jax, jax.numpy as jnp
        import numpy as np
        from math import ceil
        CAPACITY_FACTOR = 2.0
        MIN_CAPACITY = 4
        B, S, D = x.shape
        E = Wr.shape[1]
        N = B * S
        k = max(MIN_CAPACITY, ceil(N * CAPACITY_FACTOR / E))
        xt = x.reshape(N, D)
        scores = jax.nn.softmax(xt @ Wr, axis=-1)
        G, idx = jax.lax.top_k(scores.T, k)
        X_in = xt[idx]
        h = jax.nn.gelu(jnp.einsum('ekd,edh->ekh', X_in, W1) + b1[:, None, :], approximate=False)
        X_e = jnp.einsum('ekh,ehd->ekd', h, W2) + b2[:, None, :]
        contrib = (G[..., None] * X_e).reshape(E * k, D)
        out = jnp.zeros((N, D), dtype=x.dtype).at[idx.reshape(-1)].add(contrib)
        return out.reshape(B, S, D)

    def _L1_attn_ref(x, Wq, Wk, Wv, W1, W2, gn_w, gn_b):
        import jax, jax.numpy as jnp
        import numpy as np
        HIDDEN = 128
        HEADS = 8
        HEAD = HIDDEN // HEADS
        EPS = 1e-05

        def _gammas():
            lo = np.log(1.0 / 512.0)
            hi = np.log(1.0 / 32.0)
            lin = np.linspace(lo, hi, HEADS)
            return jnp.asarray(1.0 - np.exp(lin), dtype=jnp.float32)

        def _decay_mask(S, gammas):
            idx = jnp.arange(S)
            diff = idx[:, None] - idx[None, :]
            causal = diff >= 0
            safe = jnp.where(causal, diff, 0).astype(jnp.float32)
            D = jnp.where(causal[None], gammas[:, None, None] ** safe[None], 0.0)
            return D

        def _msr_forward(x, Wq, Wk, Wv, W1, W2, gn_w, gn_b):
            B, S, _ = x.shape
            xh = x.reshape(B, S, HEADS, HEAD)
            q = jnp.einsum('bshd,hde->bshe', xh, Wq)
            k = jnp.einsum('bshd,hde->bshe', xh, Wk)
            v = jnp.einsum('bshd,hde->bshe', xh, Wv)
            D = _decay_mask(S, _gammas())
            scores = jnp.einsum('bnhd,bmhd->bhnm', q, k) * D[None]
            ret = jnp.einsum('bhnm,bmhd->bnhd', scores, v)
            mu = jnp.mean(ret, axis=-1, keepdims=True)
            var = jnp.var(ret, axis=-1, keepdims=True)
            ret = (ret - mu) * jax.lax.rsqrt(var + EPS)
            ret = ret.reshape(B, S, HIDDEN) * gn_w + gn_b
            gated = x @ W1
            out = gated * jax.nn.sigmoid(gated) + ret
            return out @ W2
        return _msr_forward(x, Wq, Wk, Wv, W1, W2, gn_w, gn_b)

    def _L1_ffn_ref(tensor, Wr, br, W1, b1, W2, b2):
        import jax, jax.numpy as jnp
        import numpy as np
        D_MODEL = 128
        D_HIDDEN = 512
        NUM_BANKS = 16
        NUM_SELECTED = 2
        logits = jnp.einsum('bsd,de->bse', tensor, Wr) + br
        probs = jax.nn.softmax(logits, axis=-1)
        topv, topi = jax.lax.top_k(probs, NUM_SELECTED)
        gate = jnp.sum(jax.nn.one_hot(topi, NUM_BANKS, dtype=tensor.dtype) * topv[..., None], axis=-2)
        h = jax.nn.relu(jnp.einsum('bsd,edh->bseh', tensor, W1) + b1)
        y = jnp.einsum('bseh,ehm->bsem', h, W2) + b2
        out = jnp.einsum('bse,bsem->bsm', gate, y)
        return out
    x = L0_attn_X
    xn = _layernorm(x, axis=-1)
    x = x + _L0_attn_ref(xn, L0_attn_ln_g, L0_attn_ln_b, L0_attn_W_up1, L0_attn_conv_w, L0_attn_conv_b, L0_attn_W_ll, L0_attn_b_ll, L0_attn_A_log, L0_attn_W_up2, L0_attn_W_down, L0_attn_b_down) + _L0_ffn_ref(xn, L0_ffn_Wr, L0_ffn_W1, L0_ffn_b1, L0_ffn_W2, L0_ffn_b2)
    xn = _layernorm(x, axis=-1)
    x = x + _L1_attn_ref(xn, L1_attn_Wq, L1_attn_Wk, L1_attn_Wv, L1_attn_W1, L1_attn_W2, L1_attn_gn_w, L1_attn_gn_b) + _L1_ffn_ref(xn, L1_ffn_Wr, L1_ffn_br, L1_ffn_W1, L1_ffn_b1, L1_ffn_W2, L1_ffn_b2)
    return x

_drawn_inputs = setup_inputs


def setup_inputs(seed=0):
    import zlib

    import numpy as np

    out = dict(_drawn_inputs(seed))
    spreads = {'L0_attn_ln_g': (1.0, 0.6),
     'L0_attn_ln_b': (0.0, 0.8),
     'L0_ffn_b1': (0.0, 2.0),
     'L0_ffn_b2': (0.0, 2.0),
     'L1_attn_gn_w': (1.0, 0.6),
     'L1_attn_gn_b': (0.0, 2.0),
     'L1_ffn_br': (0.0, 2.0),
     'L1_ffn_b1': (0.0, 2.0),
     'L1_ffn_b2': (0.0, 2.0)}
    factors = {'L0_attn_W_up1': 8.0,
     'L0_attn_conv_w': 8.0,
     'L0_attn_conv_b': 8.0,
     'L0_attn_W_ll': 8.0,
     'L0_attn_b_ll': 8.0,
     'L0_attn_A_log': 8.0,
     'L0_attn_W_up2': 8.0,
     'L0_attn_W_down': 8.0,
     'L1_attn_W1': 200.0,
     'L1_ffn_Wr': 60.512,
     'L1_ffn_W1': 64.0,
     'L1_ffn_W2': 64.0,
     'L0_attn_b_down': 64.0,
     'L0_ffn_Wr': 8.0,
     'L0_ffn_W1': 8.0,
     'L0_ffn_W2': 8.0,
     'L1_attn_Wq': 64.0,
     'L1_attn_Wk': 64.0,
     'L1_attn_Wv': 64.0,
     'L1_attn_W2': 64.0}
    for name, (base, spread) in spreads.items():
        noise = np.random.default_rng([zlib.crc32(name.encode()), seed]).standard_normal(out[name].shape)
        drawn = base * np.exp(spread * noise) if base else spread * noise
        out[name] = jnp.asarray(drawn.astype(out[name].dtype))
    for name, factor in factors.items():
        out[name] = (out[name] * factor).astype(out[name].dtype)
    return out
```

```python
from contextlib import ExitStack

import concourse.bass as bass
from concourse import mybir

F32 = mybir.dt.float32
BF16 = mybir.dt.bfloat16
I32 = mybir.dt.int32
U32 = mybir.dt.uint32
ALU = mybir.AluOpType
ACT = mybir.ActivationFunctionType
AX = mybir.AxisListType

P = 128
NB, L = 8, 256
T = NB * L
NT = T // P
CH = 512
NC = T // CH
DI, N, K = 256, 16, 4
NH2 = DI // P
LP = L + K
HID = 512
HC = HID // P
E0, KTOP = 8, (T * 2) // 8
E1 = 16
HEADS, HD = 8, 16
SC = 384
EPS = 1e-5
NBITS = 30


class Chain:

    def __init__(self, eng, sem):
        self.eng, self.sem, self.n, self.calls = eng, sem, 0, 0

    def __call__(self, ins):
        ins.then_inc(self.sem, 1)
        self.n = self.n + 1
        self.calls += 1
        self.eng.wait_ge(self.sem, self.n)

    def loop(self, i, per):
        self.start, self.per, self.calls = self.n, per, 0
        self.n = self.start + i * per

    def end(self, count):
        assert self.calls == self.per, self.calls
        self.n = self.start + count * self.per


def layer_pair(nc, x, cf, mask_d, bits_i, bits_f, cols, conv_t, w_up1, w_up2, w_ll, a_log, a_log_t, w_down,
               wr0, w1_0, w2_0, b2_0, wq, wk, wv, wg, wo, wr1, br1, w1_1, w2_1, b2_1, out):
    ctx = ExitStack()
    with ctx:
        def sb(name, shape, dt=F32):
            return ctx.enter_context(nc.sbuf_tensor(name, shape, dt))

        def sem(name):
            return ctx.enter_context(nc.semaphore(name))

        bank = [ctx.enter_context(nc.psum_tensor(f"bank{i}", [P, 512], F32)) for i in range(8)]

        acc = sb("acc", [P, NT, P])
        xn = sb("xn", [P, NT, P])
        xnT = sb("xnT", [P, T])
        hbuf = sb("hbuf", [P, 2, HC, CH])
        z2p = sb("z2p", [P, NB, LP])
        w1b = sb("w1b", [P, 2, HID])
        w2b = sb("w2b", [P, 2, HC, P])
        xm = sb("xm", [P, NH2, T])
        gate = sb("gate", [P, NH2, T])
        delta = sb("delta", [P, NH2, T])
        abar = sb("abar", [P, 8, 2, L])
        zbuf = sb("zbuf", [P, 4, 2, L])
        bd = sb("bd", [P, 2, 2, N, P + 1])
        diag = sb("diag", [P, NH2, N, P])
        hb = hbuf[:, :, :, :].rearrange("p a c t -> p (a c t)")
        xnf = xn[:, :, :].rearrange("p t d -> p (t d)")
        xcur = hb[:, 0:1024].rearrange("p (a h l) -> p a h l", a=2, h=NH2)
        xT = xnf[:, 0:1024].rearrange("p (a c d) -> p a c d", a=2, c=2)
        bcur = sb("bcur", [N, 2, L])
        ccur = sb("ccur", [N, 2, L])
        cres = sb("cres", [N, 2, L])
        cb = sb("cb", [N, 2, L])
        cmid = sb("cmid", [N, L], BF16)
        csp = sb("csp", [P, 2, L], BF16)
        btok = sb("btok", [P, 2, 2, N])
        mcur = hb[:, 1024:2048].rearrange("p (a h l) -> p a h l", a=2, h=NH2)
        yg = xnf[:, 1024:2048].rearrange("p (a h l) -> p a h l", a=2, h=NH2)
        ident = sb("ident", [P, P])
        cfs = sb("cfs", [P, 129 + 128 + 128 + 16])
        bid = cfs[:, 0:129]
        ones_f = cfs[:, 129:257]
        iota_e = cfs[:, 385:401]
        onesb = sb("onesb", [P, P], BF16)
        ltri = sb("ltri", [P, P], BF16)
        selb = sb("selb", [P, N, P], BF16)
        NCOL = cols.shape[1]
        colv = sb("colv", [P, NCOL])
        nega = sb("nega", [P, NH2, N])
        inva = sb("inva", [P, NH2, N])
        invat = sb("invat", [N, DI])
        convb = delta[:, 1, 0:K * DI].rearrange("p (k e) -> p k e", k=K)
        wup1 = delta[:, 0, K * DI:(K + 1) * DI]
        wconv = delta[:, 0, 0:K * DI].rearrange("p (k e) -> p k e", k=K)
        wup2 = delta[:, 0, (K + 1) * DI:(K + 2) * DI]
        wll = sb("wll", [P, NH2, DI + 2 * N])
        wdn = sb("wdn", [P, NH2, P])
        wr0s = sb("wr0s", [P, E0])
        b2s0 = sb("b2s0", [E0, P])
        st = sb("st", [P, 8, NT])
        sc = sb("sc", [P, NT, E1])
        gt = sb("gt", [P, E1, NT])
        gtT = zbuf[0:E1, :, :, :].rearrange("e a b l -> e (a b l)").rearrange("e (t p) -> e t p", p=P)
        sm = sb("sm", [P, 4, NT])
        cmpb = sb("cmpb", [P, NT, E0], BF16)
        eqb = sb("eqb", [P, NT, E0], BF16)
        tmp8 = xT[:, :, :, :].rearrange("p a b l -> p (a b l)")[:, 0:3 * NT * E0].rearrange("p (a t e) -> p a t e", a=3, e=E0)
        thr = sb("thr", [P, E0], I32)
        cand = sb("cand", [P, E0], I32)
        inc = sb("inc", [P, E0], I32)
        cnt = sb("cnt", [P, E0])
        need = sb("need", [P, E0])
        bis = sb("bis", [P, NBITS, E0], I32)
        bfs = sb("bfs", [P, NBITS, E0])
        mx8 = sb("mx8", [P, NT, 8])
        ix8 = sb("ix8", [P, NT, 8], U32)
        ixf = sb("ixf", [P, 2, NT])
        maskd = delta[:, :, :].rearrange("p h t -> p (h t)")[:, 0:HEADS * SC].rearrange("p (h c) -> p h c", h=HEADS)
        wqs = abar[:, 0, :, :].rearrange("p a b -> p (a b)")[:, 0:2 * P].rearrange("p (g e) -> p g e", g=2)
        wks = abar[:, 1, :, :].rearrange("p a b -> p (a b)")[:, 0:2 * P].rearrange("p (g e) -> p g e", g=2)
        wvs = abar[:, 2, 0, 0:P]
        wgs = abar[:, 2, 1, 0:P]
        wos = abar[:, 3, 0, 0:P]
        wr1s = abar[:, 3, 1, 0:E1]
        br1s = abar[0:1, 3, 1, 32:32 + E1]
        b2s1 = abar[0:E1, 4, 0, 0:P]
        qcur = zbuf[:, 0:2, 0, :]
        kcur = zbuf[:, 0:2, 1, :]
        pbuf = hbuf[:, 1, :, 0:SC]
        ret = xm[:, 0, :].rearrange("p (t d) -> p t d", t=NT)
        ret2 = xm[:, 1, :].rearrange("p (t d) -> p t d", t=NT)
        vtok = gate[:, 0, :].rearrange("p (t d) -> p t d", t=NT)
        oT = gate[:, 1, :]
        retT = hbuf[:, 0, :, :].rearrange("p c t -> p (c t)")
        gst = st

        C_LNG, C_LNB, C_CB, C_BD, C_BB, C_BC, C_DN, C_B10, C_B11, C_GW, C_GB = 0, 1, 2, 4, 6, 7, 8, 9, 41, 105, 106

        names = ("act_past pe_past pool_past "
                 "ld_x ld_c ld_w ld_w2 ld_late pe_done dve_done act_done pool_done act_link dve_link pool_link "
                 "ps_ready ps_free psd_ready psd_free ab_ready ab_free dw_ready cbc_ready p_ready p_free "
                 "y_ready y_free xcur_ready pro_x pro_xe pro_bt pro_bte bd_ready csp_hi csp_r csp_mid csp_r2 csp_lo "
                 "cb_ready m_ready m_evac xm_ready yg_ready yg_used dn_ready dn_evac "
                 "u_ready h_ready d_ready w_ready0 w_ready1 f_acc layer0 "
                 "ee abs_r exp_r ln_r w_r cnt_in cnt_out st_out "
                 "qk_ps qk_sb s_ready s_free pm_ready pm_free r_free").split()
        S = {n: sem(n) for n in names}

        block = ctx.enter_context(nc.Block())

        FFN = {0: dict(E=E0, e0=0, func=ACT.Gelu, col=C_B10), 1: dict(E=E1, e0=E0, func=ACT.Relu, col=C_B11)}

        def dve_ffn(dve, lay):
            f = FFN[lay]
            with dve.Fori(0, f["E"] // 2) as i:
                for k in range(2 * NC):
                    g = (i * 2 + f["e0"]) * NC + k
                    j = k % NC
                    dve.wait_ge(S["d_ready"], g + 6)
                    for tt in range(4):
                        t = 4 * j + tt
                        m = nc.vector.scalar_tensor_tensor(
                            out=acc[:, t, :], in0=bank[4 + k % 2][:, tt * P:(tt + 1) * P],
                            scalar=gt[:, :, t:t + 1].rearrange("p e o -> p (e o)")[:, bass.ds(i * 2 + k // NC, 1)],
                            in1=acc[:, t, :], op0=ALU.mult, op1=ALU.add)
                        if tt == 3:
                            m.then_inc(S["f_acc"], 1)
                    dve.wait_ge(S["f_acc"], g + 3)

        dve_at = {}

        @block.vector
        def _(dve):
            link = Chain(dve, S["dve_link"])
            V = nc.vector

            def bc(ap, n):
                return ap[:, :, None].broadcast_to([P, NT, n])

            sq = hbuf[:, 1, :, :].rearrange("p c (q d) -> p (c q) d", d=P)

            def layer_norm(dst, source, nth):
                link(V.tensor_reduce(st[:, 0, :], source, AX.X, ALU.add))
                link(V.tensor_scalar(st[:, 1, :], st[:, 0, :], 1.0 / P, None, ALU.mult))
                link(V.tensor_tensor(dst, source, bc(st[:, 1, :], P), ALU.subtract))
                link(V.tensor_tensor(sq, dst, dst, ALU.mult))
                link(V.tensor_reduce(st[:, 0, :], sq, AX.X, ALU.add))
                link(V.tensor_scalar(st[:, 2, :], st[:, 0, :], 1.0 / P, EPS, ALU.mult, ALU.add))
                dve_at[nth] = link.n
                dve.wait_ge(S["abs_r"], {0: 1, 1: 2, 2: 3 + 2 * NC}[nth])
                link(V.reciprocal(st[:, 4, :], st[:, 3, :]))
                V.tensor_tensor(dst, dst, bc(st[:, 4, :], P), ALU.mult).then_inc(S["dve_link"], 1)
                link.n += 1
                dve.wait_ge(S["dve_link"], link.n)

            dve.wait_ge(S["ld_x"], 64)
            layer_norm(xn[:, :, :], acc[:, :, :], 0)
            dve.sem_inc(S["dve_done"], 1)
            z2 = hbuf[:, 0, :, :].rearrange("p c (q d) -> p (c q) d", d=P)
            layer_norm(z2, xn[:, :, :], 1)
            dve.sem_inc(S["dve_done"], 1)
            link(V.tensor_tensor(acc[:, :, :], acc[:, :, :], xn[:, :, :], ALU.add))
            dve.wait_ge(S["ld_c"], 64)
            for q in range(4):
                dve.wait_ge(S["ps_ready"], q + 1)
                V.tensor_copy(xnT[:, q * CH:(q + 1) * CH], bank[q % 2][:, :]).then_inc(S["ps_free"], 1)
            for q in range(4):
                dve.wait_ge(S["ps_ready"], q + 5)
                V.tensor_scalar(z2p[:, 2 * q:2 * q + 2, K - 1:K - 1 + L], bank[q % 2][:, :].rearrange("p (b l) -> p b l", b=2),
                                colv[:, C_LNG:C_LNG + 1], colv[:, C_LNB:C_LNB + 1], ALU.mult, ALU.add).then_inc(S["ps_free"], 1)
            dve.wait_ge(S["act_link"], 2)
            link(V.tensor_scalar(nega[:, :, :], nega[:, :, :], -1.0, None, ALU.mult))
            link(V.tensor_scalar(invat[:, :], invat[:, :], -1.0, None, ALU.mult))
            link(V.reciprocal(inva[:, :, :], nega[:, :, :]))
            link(V.reciprocal(invat[:, :], invat[:, :]))
            dve_at["inva"] = link.n
            with dve.Fori(0, NC) as j:
                link.loop(j, 5 * NH2)
                for h in range(NH2):
                    d = delta[:, h, bass.ts(j, CH)]
                    dve.wait_ge(S["abs_r"], j * 2 + (2 + h + 1))
                    link(V.tensor_scalar(d, bank[h][:, :], colv[:, C_BD + h:C_BD + h + 1], 0.0, ALU.add, ALU.max))
                    dve.wait_ge(S["exp_r"], j * 2 + h + 1)
                    link(V.tensor_scalar(hbuf[:, h, 3, :], hbuf[:, h, 1, :], 1.0, None, ALU.add))
                    link(V.scalar_tensor_tensor(out=hbuf[:, h, 3, :], in0=hbuf[:, h, 3, :], scalar=-1.0, in1=hbuf[:, h, 1, :],
                                                op0=ALU.add, op1=ALU.subtract))
                    link(V.tensor_tensor(d, d, hbuf[:, h, 3, :], ALU.subtract))
                    dve.wait_ge(S["ln_r"], j * 2 + h + 1)
                    link(V.tensor_tensor(d, d, hbuf[:, h, 2, :], ALU.add))
                    dve.sem_inc(S["psd_free"], 1)
                    dve.sem_inc(S["w_r"], 1)
            link.end(NC)
            dve_at["delta"] = link.n
            dve.wait_ge(S["psd_free"], 4 + 4 * NC)
            dve.sem_inc(S["xm_ready"], 1)

            def mult(b, s):
                n2, h = s // 2, s % 2
                dve.wait_ge(S["cbc_ready"], b * 8 + n2 + 1)
                dve.wait_ge(S["ab_free"], b * 16 + (s + 9))
                z = zbuf[:, s % 4, :, :].rearrange("p n t -> p (n t)")
                V.tensor_tensor(z, z, bank[2 + n2 % 2][:, :], ALU.mult).then_inc(S["p_ready"], 1)

            def main(b, par):
                for s in range(16):
                    h = s % 2
                    dve.wait_ge(S["ab_ready"], b * 16 + s + 1)
                    dve.wait_ge(S["dw_ready"], b * 16 + s + 1)
                    dve.wait_ge(S["p_free"], b * 16 + s + 1)
                    for r in range(2):
                        m = V.tensor_tensor_scan(zbuf[:, s % 4, r, :], bank[s % 2][:, r * L:(r + 1) * L], abar[:, s % 8, r, :],
                                                 0.0, ALU.add, ALU.mult)
                    m.then_inc(S["ab_free"], 1)
                    if s >= 1:
                        mult(b, s - 1)
                mult(b, 15)
                dve.wait_ge(S["m_evac"], b + 1)
                if not (isinstance(b, int) and b < 2):
                    dve.wait_ge(S["dn_ready"], b - 1)
                link(V.tensor_tensor(yg[:, par, :, :], xcur[:, par, :, :], mcur[:, par, :, :], ALU.mult))
                dve.wait_ge(S["p_free"], b * 16 + (16 + 4))
                for h in range(NH2):
                    link(V.tensor_tensor(yg[:, par, h, :], bank[4 + h][:, 0:L], yg[:, par, h, :], ALU.subtract))
                    dve.sem_inc(S["y_free"], 1)
                V.tensor_tensor(yg[:, par, :, :], yg[:, par, :, :], gate[:, :, bass.ds(b * L, L)], ALU.mult).then_inc(S["yg_ready"], 1)

            main(0, 0)
            with dve.Fori(0, 3) as i:
                link.loop(i, 6)
                main(i * 2 + 1, 1)
                main(i * 2 + 2, 0)
            link.end(3)
            main(7, 1)
            dve.wait_ge(S["p_free"], 8 * 16 + 4)
            dve.sem_inc(S["dve_done"], 1)
            for q in range(4):
                dve.wait_ge(S["pe_done"], q + 1)
                t = acc[:, 4 * q:4 * q + 4, :].rearrange("p t d -> p (t d)")
                V.tensor_tensor(t, t, bank[q % 2][:, :], ALU.add).then_inc(S["dve_done"], 1)

            def softmax(E, ready, at, nth):
                s = sc[:, :, 0:E]
                dve.wait_ge(S["pe_done"], ready)
                ps = at[:, 0:NT * E].rearrange("p (t e) -> p t e", t=NT)
                link(V.tensor_reduce(sm[:, 0, :], ps, AX.X, ALU.max))
                link(V.tensor_tensor(s, ps, bc(sm[:, 0, :], E), ALU.subtract))
                dve_at[nth] = link.n
                dve.wait_ge(S["exp_r"], 2 * NC + (1 if E == E0 else 2))
                link(V.tensor_reduce(sm[:, 1, :], s, AX.X, ALU.add))
                link(V.reciprocal(sm[:, 2, :], sm[:, 1, :]))
                link(V.tensor_tensor(s, s, bc(sm[:, 2, :], E), ALU.mult))

            softmax(E0, 5, bank[2], "smax0")
            s0 = sc[:, :, 0:E0]

            def per_e(ap):
                return ap[:, None, :].broadcast_to([P, NT, E0])

            tot = bank[3][:, 0:P].rearrange("p (t e) -> p t e", t=NT)
            link(V.memset(thr[:, :], 0))
            with dve.Fori(0, NBITS) as i:
                link.loop(i, 5)
                link(V.tensor_tensor(cand[:, :], thr[:, :], bis[:, bass.ds(i, 1), :].rearrange("p a e -> p (a e)"), ALU.bitwise_or))
                link(V.tensor_tensor(cmpb[:, :, :], s0, per_e(cand[:, :].bitcast(F32)), ALU.is_ge))
                dve.sem_inc(S["cnt_in"], 1)
                dve.wait_ge(S["cnt_out"], i + 1)
                link(V.tensor_reduce(cnt[:, :], tot.rearrange("p t e -> p e t"), AX.X, ALU.add))
                link(V.scalar_tensor_tensor(out=inc[:, :], in0=cnt[:, :], scalar=float(KTOP),
                                            in1=bfs[:, bass.ds(i, 1), :].rearrange("p a e -> p (a e)"),
                                            op0=ALU.is_ge, op1=ALU.mult))
                link(V.tensor_tensor(thr[:, :], thr[:, :], inc[:, :], ALU.bitwise_or))
            link.end(NBITS)
            thf = thr[:, :].bitcast(F32)
            link(V.tensor_tensor(cmpb[:, :, :], s0, per_e(thf), ALU.is_gt))
            dve.sem_inc(S["cnt_in"], 1)
            link(V.tensor_tensor(eqb[:, :, :], s0, per_e(thf), ALU.is_equal))
            dve.wait_ge(S["cnt_out"], NBITS + 1)
            link(V.tensor_reduce(cnt[:, :], tot.rearrange("p t e -> p e t"), AX.X, ALU.add))
            dve.sem_inc(S["cnt_in"], 1)
            link(V.tensor_scalar(need[:, :], cnt[:, :], -1.0, float(KTOP), ALU.mult, ALU.add))
            dve.wait_ge(S["cnt_out"], NBITS + 2)
            link(V.memset(tmp8[:, 0, 0:1, :], 0.0))
            link(V.tensor_copy(tmp8[:, 0, 1:NT, :], tot[:, 0:NT - 1, :]))
            cur = 0
            for d in (1, 2, 4, 8):
                V.tensor_copy(tmp8[:, 1 - cur, 0:d, :], tmp8[:, cur, 0:d, :]).then_inc(S["dve_link"], 1)
                link.n += 1
                link(V.tensor_tensor(tmp8[:, 1 - cur, d:NT, :], tmp8[:, cur, d:NT, :], tmp8[:, cur, 0:NT - d, :], ALU.add))
                cur = 1 - cur
            rank = tmp8[:, 2, :, :]
            link(V.tensor_tensor(rank, tmp8[:, cur, :, :], bank[2][:, 0:P].rearrange("p (t e) -> p t e", t=NT), ALU.add))
            link(V.tensor_tensor(rank, rank, per_e(need[:, :]), ALU.is_lt))
            link(V.tensor_tensor(rank, rank, eqb[:, :, :], ALU.mult))
            link(V.tensor_tensor(rank, rank, cmpb[:, :, :], ALU.add))
            V.tensor_tensor(gt[:, 0:E0, :].rearrange("p e t -> p t e"), rank, s0, ALU.mult).then_inc(S["dve_link"], 1)
            link.n += 1
            dve.wait_ge(S["dve_link"], link.n)
            dve.sem_inc(S["dve_done"], 1)

            def bias_rows(first):
                for q in range(4):
                    dve.wait_ge(S["pe_done"], first + q + 1)
                    t = acc[:, 4 * q:4 * q + 4, :].rearrange("p t d -> p (t d)")
                    V.tensor_tensor(t, t, bank[6 + q % 2][:, :], ALU.add).then_inc(S["dve_done"], 1)

            bias_rows(9)
            dve.wait_ge(S["dve_done"], 12)
            dve_ffn(dve, 0)
            dve.sem_inc(S["layer0"], 1)
            layer_norm(xn[:, :, :], acc[:, :, :], 2)
            dve.sem_inc(S["dve_done"], 1)
            for q in range(4):
                dve.wait_ge(S["ps_ready"], q + 9)
                V.tensor_copy(xnT[:, q * CH:(q + 1) * CH], bank[q % 2][:, :]).then_inc(S["ps_free"], 1)
            softmax(E1, 18, bank[4], "smax1")
            dve.sem_inc(S["dve_done"], 1)
            for t in range(NT):
                V.max(mx8[:, t, :], sc[:, t, :]).then_inc(S["dve_link"], 1)
                link.n += 1
            dve.wait_ge(S["dve_link"], link.n)
            for t in range(NT):
                V.max_index(ix8[:, t, :], mx8[:, t, :], sc[:, t, :]).then_inc(S["dve_link"], 1)
                link.n += 1
            dve.wait_ge(S["dve_link"], link.n)
            oh = [hbuf[:, 0, w, 0:NT * E1].rearrange("p (t e) -> p t e", t=NT) for w in range(2)]
            for w in range(2):
                link(V.tensor_copy(ixf[:, w, :], ix8[:, :, w]))
                link(V.tensor_tensor(oh[w], iota_e[:, None, :].broadcast_to([P, NT, E1]),
                                     ixf[:, w, :, None].broadcast_to([P, NT, E1]), ALU.is_equal))
            link(V.tensor_tensor(oh[0], oh[0], oh[1], ALU.add))
            link(V.tensor_tensor(gt[:, :, :].rearrange("p e t -> p t e"), oh[0], sc[:, :, :], ALU.mult))
            dve.wait_ge(S["act_link"], 6)
            dve.sem_inc(S["dve_done"], 1)
            dve.wait_ge(S["ld_late"], 9 * 16)
            with dve.Fori(0, NB) as b:
                for h in range(HEADS):
                    dve.wait_ge(S["s_ready"], b * 8 + (h + 1))
                    if h >= 4:
                        dve.wait_ge(S["pm_free"], b * 8 + (h + 5))
                    else:
                        dve.wait_ge(S["pm_free"], b * 8 + 8)
                    V.tensor_tensor(pbuf[:, h % 4, :], bank[h % 4][:, 0:SC], maskd[:, h, :], ALU.mult).then_inc(S["pm_ready"], 1)
                    if h >= 1:
                        dve.wait_ge(S["pm_ready"], b * 8 + h)
                        dve.sem_inc(S["s_free"], 1)
                dve.wait_ge(S["pm_ready"], b * 8 + 8)
                dve.sem_inc(S["s_free"], 1)
            dve.wait_ge(S["r_free"], NB + 1)
            r4 = ret.rearrange("p t (h d) -> p (t h) d", h=HEADS)
            q4 = ret2.rearrange("p t (h d) -> p (t h) d", h=HEADS)
            G = NT * HEADS
            g0, g1, g2 = (hbuf[:, 1, k, 0:G] for k in range(3))

            def gb(ap):
                return ap[:, :, None].broadcast_to([P, G, HD])

            link(V.tensor_reduce(g0, r4, AX.X, ALU.add))
            link(V.tensor_scalar(g1, g0, 1.0 / HD, None, ALU.mult))
            link(V.tensor_tensor(r4, r4, gb(g1), ALU.subtract))
            link(V.tensor_tensor(q4, r4, r4, ALU.mult))
            link(V.tensor_reduce(g2, q4, AX.X, ALU.add))
            link(V.tensor_scalar(g0, g2, 1.0 / HD, EPS, ALU.mult, ALU.add))
            dve_at["gn"] = link.n
            dve.wait_ge(S["abs_r"], 4 + 2 * NC)
            link(V.reciprocal(g2, g1))
            link(V.tensor_tensor(r4, r4, gb(g2), ALU.mult))
            dve.sem_inc(S["dve_done"], 1)
            for q in range(4):
                dve.wait_ge(S["ps_ready"], 13 + q)
                link(V.tensor_scalar(retT[:, q * CH:(q + 1) * CH], bank[0][:, :], colv[:, C_GW:C_GW + 1], colv[:, C_GB:C_GB + 1],
                                     ALU.mult, ALU.add))
                dve.sem_inc(S["ps_free"], 1)
                dve.wait_ge(S["ps_free"], 14 + 2 * q)
                V.tensor_tensor(oT[:, q * CH:(q + 1) * CH], oT[:, q * CH:(q + 1) * CH], retT[:, q * CH:(q + 1) * CH], ALU.add
                                ).then_inc(S["dve_done"], 1)
            for q in range(4):
                dve.wait_ge(S["pe_done"], 19 + q)
                t = acc[:, 4 * q:4 * q + 4, :].rearrange("p t d -> p (t d)")
                V.tensor_tensor(t, t, bank[2 + q][:, :], ALU.add).then_inc(S["dve_done"], 1)
            dve.sem_inc(S["dve_done"], 1)
            bias_rows(26)
            dve.wait_ge(S["dve_done"], 29)
            dve_ffn(dve, 1)

        @block.sync
        def _(sp):
            xv = x.rearrange("(t p) d -> p t d", p=P)
            for q in range(4):
                sp.dma_start(acc[:, 4 * q:4 * q + 4, :], xv[:, 4 * q:4 * q + 4, :]).then_inc(S["ld_x"], 16)
            for dst, src in ((ident[:, :], cf[:, 0:P]), (colv[:, :], cols), (cfs[:, :], cf[:, P:P + 401]),
                             (abar[:, 0:4, :, :].rearrange("p a b l -> p (a b l)"), cf[:, P + 401:])):
                sp.dma_start(dst, src).then_inc(S["ld_c"], 16)
            for k in range(K):
                sp.dma_start(convb[:, k, :], conv_t[k, :].partition_broadcast(P)).then_inc(S["ld_w"], 16)
            for dst, src in ((wup1, w_up1), (wup2, w_up2),
                             (wll[:, :, :], w_ll.rearrange("(h p) e -> p h e", p=P)),
                             (wdn[:, :, :], w_down.rearrange("(h p) e -> p h e", p=P)),
                             (nega[:, :, :], a_log.rearrange("(h p) n -> p h n", p=P)),
                             (invat[:, :], a_log_t), (wr0s[:, :], wr0), (b2s0[:, :], b2_0),
                             (bis[:, :, :], bits_i), (bfs[:, :, :], bits_f)):
                sp.dma_start(dst, src).then_inc(S["ld_w"], 16)
            with sp.Fori(0, E0 // 2) as i:
                for par in range(2):
                    e = i * 2 + par
                    sp.wait_ge(S["d_ready"], e * NC + 1)
                    sp.dma_start(w1b[:, par, :], w1_0[bass.ds(e, 1), :, :].rearrange("a p h -> p (a h)")).then_inc(S[f"w_ready{par}"], 16)
                    sp.dma_start(w2b[:, par, :, :].rearrange("p c d -> p (c d)"),
                                 w2_0[bass.ds(e, 1), :, :].rearrange("a p h -> p (a h)")).then_inc(S[f"w_ready{par}"], 16)
            sp.wait_ge(S["layer0"], 1)
            for dst, src in ((maskd, mask_d), (wqs, wq), (wks, wk), (wvs, wv), (wgs, wg), (wos, wo),
                             (wr1s, wr1), (br1s, br1), (b2s1, b2_1)):
                sp.dma_start(dst, src).then_inc(S["ld_late"], 16)
            with sp.Fori(0, E1 // 2) as i:
                for par in range(2):
                    e = i * 2 + par
                    sp.wait_ge(S["d_ready"], e * NC + (E0 * NC + 1))
                    sp.dma_start(w1b[:, par, :], w1_1[bass.ds(e, 1), :, :].rearrange("a p h -> p (a h)")).then_inc(S[f"w_ready{par}"], 16)
                    sp.dma_start(w2b[:, par, :, :].rearrange("p c d -> p (c d)"),
                                 w2_1[bass.ds(e, 1), :, :].rearrange("a p h -> p (a h)")).then_inc(S[f"w_ready{par}"], 16)
            sp.wait_ge(S["f_acc"], (E0 + E1) * NC + 2)
            sp.dma_start(out.rearrange("(t p) d -> p t d", p=P), acc[:, :, :]).then_inc(S["st_out"], 16)
            sp.wait_ge(S["st_out"], 16)


        def pe_ffn(pe, lay):
            f = FFN[lay]
            with pe.Fori(0, f["E"] // 2) as i:
                def up(k):
                    g = (i * 2 + f["e0"]) * NC + k
                    par = k // NC
                    if k % NC == 0:
                        pe.wait_ge(S[f"w_ready{par}"], i * 32 + (16 * f["e0"] + 32))
                    for c in range(HC):
                        pe.wait_ge(S["h_ready"], g * HC + c + 1)
                        pe.matmul(bank[c][:, :], w1b[:, par, c * P:(c + 1) * P], xnT[:, (k % NC) * CH:(k % NC + 1) * CH],
                                  start=True, stop=True).then_inc(S["u_ready"], 1)

                def down(k):
                    g = (i * 2 + f["e0"]) * NC + k
                    par = k // NC
                    pe.wait_ge(S["h_ready"], g * HC + 2 * HC)
                    pe.wait_ge(S["f_acc"], g + 1)
                    for tt in range(4):
                        for c in range(HC):
                            m = pe.matmul(bank[4 + k % 2][:, tt * P:(tt + 1) * P], hbuf[:, k % 2, c, tt * P:(tt + 1) * P],
                                          w2b[:, par, c, :], start=(c == 0), stop=(c == HC - 1))
                    m.then_inc(S["d_ready"], 1)

                for k in range(2 * NC):
                    up(k)
                    if k:
                        down(k - 1)
                down(2 * NC - 1)

        def act_ffn(act, lay):
            f = FFN[lay]
            with act.Fori(0, f["E"] // 2) as i:
                for k in range(2 * NC):
                    g = (i * 2 + f["e0"]) * NC + k
                    act.wait_ge(S["d_ready"], g + 4)
                    for c in range(HC):
                        act.wait_ge(S["u_ready"], g * HC + c + 1)
                        act.sem_inc(S["act_past"], 1)
                        nc.scalar.activation(hbuf[:, k % 2, c, :], bank[c][:, :], f["func"],
                                             bias=colv[:, bass.ds(i * (2 * HC) + (f["col"] + (k // NC) * HC + c), 1)]
                                             ).then_inc(S["h_ready"], 1)

        @block.tensor
        def _(pe):
            pe.wait_ge(S["ld_c"], 64)

            def transpose_norm(ready, free):
                for q in range(4):
                    pe.wait_ge(*ready)
                    if free(q):
                        pe.wait_ge(S["ps_free"], free(q))
                    for r in range(4):
                        m = pe.transpose(bank[q % 2][:, r * P:(r + 1) * P], src(4 * q + r), ident[:, :])
                    m.then_inc(S["ps_ready"], 1)

            z2 = hbuf[:, 0, :, :].rearrange("p c (q d) -> p (c q) d", d=P)
            src = lambda t: xn[:, t, :]
            transpose_norm((S["dve_done"], 1), lambda q: q - 1 if q > 1 else 0)
            src = lambda t: z2[:, t, :]
            transpose_norm((S["dve_done"], 2), lambda q: q + 3)

            pe.wait_ge(S["ld_w"], 14 * 16)
            pe.wait_ge(S["pool_done"], 1)
            pe.wait_ge(S["ps_free"], 8)
            with pe.Fori(0, NC) as j:
                for q in range(4):
                    pe.wait_ge(S["psd_free"], j * 4 + q + 1)
                    h = q % 2
                    if q < 2:
                        for k in range(K):
                            m = pe.matmul(bank[q][:, :], wconv[:, k, h * P:(h + 1) * P],
                                          z2p[:, bass.ds(j * 2, 2), k:k + L], start=(k == 0), stop=(k == K - 1))
                    else:
                        m = pe.matmul(bank[q][:, :], wup2[:, h * P:(h + 1) * P],
                                      z2p[:, bass.ds(j * 2, 2), K - 1:K - 1 + L], start=True, stop=True)
                    m.then_inc(S["psd_ready"], 1)
            pe.wait_ge(S["psd_free"], 4 * NC + 4)
            with pe.Fori(0, NC) as j:
                for h in range(NH2):
                    pe.wait_ge(S["psd_free"], j * 2 + (4 * NC + 4 + h - 1))
                    for kh in range(NH2):
                        m = pe.matmul(bank[h][:, :], wll[:, kh, h * P:(h + 1) * P], xm[:, kh, bass.ts(j, CH)],
                                      start=(kh == 0), stop=(kh == NH2 - 1))
                    m.then_inc(S["psd_ready"], 1)
            pe.wait_ge(S["psd_free"], 4 * NC + 4 + 2 * NC)

            DW, CB_, Y, M0, M1 = bank[0:2], bank[2:4], bank[4:6], bank[6], bank[7]

            def pro1(b, par):
                pe.wait_ge(S["xcur_ready"], b + 1)
                if not (isinstance(b, int) and b == 0):
                    pe.wait_ge(S["m_evac"], b)
                    pe.wait_ge(S["pro_bte"], b)
                    pe.wait_ge(S["dn_evac"], b - 1) if not (isinstance(b, int) and b == 1) else None
                for c in range(2):
                    for h in range(NH2):
                        pe.transpose(M0[:, c * DI + h * P:c * DI + (h + 1) * P], xcur[:, par, h, c * P:(c + 1) * P], ident[:, :])
                for w in range(2):
                    for h in range(NH2):
                        m = pe.matmul(M1[0:N, w * L:(w + 1) * L], wll[:, h, DI + w * N:DI + (w + 1) * N],
                                      xcur[:, par, h, :], start=(h == 0), stop=(h == NH2 - 1))
                m.then_inc(S["pro_x"], 1)

            def pro2(b, par):
                pe.wait_ge(S["pro_xe"], b + 1)
                pe.sem_inc(S["pe_past"], 1)
                for c in range(2):
                    m = pe.transpose(M0[:, c * N:(c + 1) * N], bcur[:, par, c * P:(c + 1) * P], ident[0:N, 0:N])
                m.then_inc(S["pro_bt"], 1)

            def pro3(b, par):
                pe.wait_ge(S["cb_ready"], b + 1)
                for h in range(NH2):
                    m = pe.matmul(M1[:, h * L:(h + 1) * L], invat[:, h * P:(h + 1) * P], cb[:, par, :], start=True, stop=True)
                m.then_inc(S["m_ready"], 1)

            def down(b, par):
                pe.wait_ge(S["yg_ready"], b + 1)
                pe.wait_ge(S["pro_bte"], b + 2)
                for h in range(NH2):
                    m = pe.matmul(M0[:, 0:L], wdn[:, h, :], yg[:, par, h, :], start=(h == 0), stop=(h == NH2 - 1))
                m.then_inc(S["dn_ready"], 1)

            def y_sum(b, s):
                n2, h = s // 2, s % 2
                pe.wait_ge(S["p_ready"], b * 16 + s + 3)
                if n2 == 0:
                    pe.wait_ge(S["y_free"], b * 2 + h + 1)
                for r in range(2):
                    m = pe.matmul(Y[h][:, 0:L], diag[:, h, 2 * n2 + r, :], zbuf[:, s % 4, r, :],
                                  start=(n2 == 0 and r == 0), stop=(n2 == 7 and r == 1))
                m.then_inc(S["p_free"], 1)

            def main(b, par, more):
                first = isinstance(b, int) and b == 0
                pe.wait_ge(S["bd_ready"], b + 1)
                pe.wait_ge(S["csp_lo"], b + 1)
                for s in range(16):
                    n2, h = s // 2, s % 2
                    if h == 0:
                        pe.wait_ge(S["p_ready"], b * 16 + 2 * n2)
                        for r in range(2):
                            m = pe.matmul(CB_[n2 % 2][:, r * L:(r + 1) * L], selb[:, 2 * n2 + r, :], csp[:, par, :],
                                          start=True, stop=True)
                        m.then_inc(S["cbc_ready"], 1)
                    pe.wait_ge(S["ab_free"], b * 16 + s + 7)
                    o = DW[s % 2][:, :].rearrange("p (n t) -> p n t", n=2)
                    pe.matmul(o[:, :, 0:P + 1], xT[:, par, 0, h * P:(h + 1) * P], bd[:, par, 0, 2 * n2:2 * n2 + 2, :],
                              start=True, stop=False, skip_group_check=True)
                    pe.matmul(o[:, :, P:L], xT[:, par, 1, h * P:(h + 1) * P], bd[:, par, 1, 2 * n2:2 * n2 + 2, 0:P],
                              start=False, stop=True, skip_group_check=True).then_inc(S["dw_ready"], 1)
                    if s >= 2:
                        y_sum(b, s - 2)
                    if s == 3 and not first:
                        down(b - 1, 1 - par)
                    if more:
                        if s == 5:
                            pro1(b + 1, 1 - par)
                        if s == 8:
                            pro2(b + 1, 1 - par)
                        if s == 11:
                            pro3(b + 1, 1 - par)
                y_sum(b, 14)
                y_sum(b, 15)
                m = None

            pe.wait_ge(S["pool_done"], 2)
            pe.wait_ge(S["act_done"], 2)
            pro1(0, 0)
            pro2(0, 0)
            pro3(0, 0)
            main(0, 0, True)
            with pe.Fori(0, 3) as i:
                main(i * 2 + 1, 1, True)
                main(i * 2 + 2, 0, True)
            main(7, 1, False)
            pe.wait_ge(S["dn_evac"], 7)
            pe.wait_ge(S["yg_ready"], 8)
            for h in range(NH2):
                m = pe.matmul(M0[:, 0:L], wdn[:, h, :], yg[:, 1, h, :], start=(h == 0), stop=(h == NH2 - 1))
            m.then_inc(S["dn_ready"], 1)
            pe.wait_ge(S["dn_evac"], 8)
            ymt = z2p[:, :, :].rearrange("p b l -> p (b l)")
            for q in range(4):
                pe.wait_ge(S["dve_done"], 3 if q < 2 else 2 + q)
                for r in range(4):
                    t = 4 * q + r
                    m = pe.transpose(bank[q % 2][:, r * P:(r + 1) * P], ymt[:, t * P:(t + 1) * P], ident[:, :])
                m.then_inc(S["pe_done"], 1)
            pe.wait_ge(S["dve_done"], 7)
            for t in range(NT):
                m = pe.matmul(bank[2][:, t * E0:(t + 1) * E0], xnT[:, t * P:(t + 1) * P], wr0s[:, :], start=True, stop=True)
            m.then_inc(S["pe_done"], 1)
            with pe.Fori(0, NBITS + 1) as i:
                pe.wait_ge(S["cnt_in"], i + 1)
                pe.matmul(bank[3][:, 0:P], onesb[:, :], cmpb[:, :, :], start=True, stop=True).then_inc(S["cnt_out"], 1)
            pe.wait_ge(S["cnt_in"], NBITS + 2)
            pe.matmul(bank[3][:, 0:P], onesb[:, :], eqb[:, :, :], start=True, stop=True)
            pe.matmul(bank[2][:, 0:P], ltri[:, :], eqb[:, :, :], start=True, stop=True).then_inc(S["cnt_out"], 1)
            pe.wait_ge(S["dve_done"], 8)

            def bias_rows(E, b2, done):
                for q in range(4):
                    if q:
                        pe.wait_ge(S["act_done"], done + q)
                    for r in range(4):
                        t = 4 * q + r
                        m = pe.transpose(bank[6][0:E, r * P:(r + 1) * P], gt[:, 0:E, t], ident[:, :])
                    m.then_inc(S["pe_done"], 1)
                pe.wait_ge(S["act_done"], done + 4)
                for q in range(4):
                    if q > 1:
                        pe.wait_ge(S["dve_done"], bd0 + q - 1)
                    for r in range(4):
                        t = 4 * q + r
                        m = pe.matmul(bank[6 + q % 2][:, r * P:(r + 1) * P], gtT[0:E, t, :], b2, start=True, stop=True)
                    m.then_inc(S["pe_done"], 1)

            bd0 = 8
            bias_rows(E0, b2s0[:, :], 2)
            pe_ffn(pe, 0)

            src = lambda t: xn[:, t, :]
            transpose_norm((S["dve_done"], 13), lambda q: 8 + (q - 1 if q > 1 else 0))
            pe.wait_ge(S["ps_free"], 12)
            pe.wait_ge(S["ld_late"], 9 * 16)
            for q in range(4):
                for r in range(4):
                    t = 4 * q + r
                    m = pe.matmul(bank[q][:, r * P:(r + 1) * P], xnT[:, t * P:(t + 1) * P], wvs, start=True, stop=True)
                m.then_inc(S["pe_done"], 1)
            for t in range(NT):
                pe.matmul(bank[4][:, t * E1:(t + 1) * E1], xnT[:, t * P:(t + 1) * P], wr1s, start=True, stop=False)
                m = pe.matmul(bank[4][:, t * E1:(t + 1) * E1], ones_f[0:1, :], br1s, start=False, stop=True)
            m.then_inc(S["pe_done"], 1)
            pe.wait_ge(S["dve_done"], 15)
            with pe.Fori(0, NB) as b:
                pe.wait_ge(S["qk_sb"], b + 1)
                for g in range(2):
                    for w, o in ((wqs, 0), (wks, L)):
                        m = pe.matmul(bank[4 + g][:, o:o + L], w[:, g, :], xnT[:, bass.ts(b, L)], start=True, stop=True)
                m.then_inc(S["qk_ps"], 1)
                pe.wait_ge(S["qk_sb"], b + 2)
                for g in range(2):
                    for hh in range(4):
                        pe.wait_ge(S["s_free"], b * 8 + (4 * g + hh + 1))
                        o = slice(32 * hh, 32 * hh + 32)
                        pe.matmul(bank[hh][:, 0:L], kcur[o, g, 0:P], qcur[o, g, :], start=True, stop=True)
                        pe.matmul(bank[hh][:, L:SC], kcur[o, g, P:L], qcur[o, g, P:L], start=True, stop=True
                                  ).then_inc(S["s_ready"], 1)
                    if g == 0:
                        pe.wait_ge(S["r_free"], b + 1)
                    for hh in range(4):
                        h = 4 * g + hh
                        pe.wait_ge(S["pm_ready"], b * 8 + (h + 1))
                        v0 = vtok[:, bass.ds(b * 2, 1), h * HD:(h + 1) * HD]
                        v1 = vtok[:, bass.ds(b * 2 + 1, 1), h * HD:(h + 1) * HD]
                        pe.matmul(bank[6][:, h * HD:(h + 1) * HD], pbuf[:, hh, 0:P], v0, start=True, stop=True)
                        pe.matmul(bank[6][:, P + h * HD:P + (h + 1) * HD], pbuf[:, hh, P:L], v0, start=True, stop=False)
                        m = pe.matmul(bank[6][:, P + h * HD:P + (h + 1) * HD], pbuf[:, hh, L:SC], v1, start=False, stop=True)
                        m.then_inc(S["pm_free"], 1)
            pe.wait_ge(S["dve_done"], 16)
            for q in range(4):
                if q:
                    pe.wait_ge(S["ps_free"], 12 + 2 * q)
                for r in range(4):
                    t = 4 * q + r
                    pe.transpose(bank[0][:, r * P:(r + 1) * P], ret[:, t, :], ident[:, :])
                pe.matmul(bank[1][:, :], wgs, xnT[:, q * CH:(q + 1) * CH], start=True, stop=True).then_inc(S["ps_ready"], 1)
            for q in range(4):
                pe.wait_ge(S["dve_done"], 17 + q)
                for r in range(4):
                    t = 4 * q + r
                    m = pe.matmul(bank[2 + q][:, r * P:(r + 1) * P], oT[:, t * P:(t + 1) * P], wos, start=True, stop=True)
                m.then_inc(S["pe_done"], 1)
            pe.wait_ge(S["dve_done"], 25)
            bd0 = 25
            bias_rows(E1, b2s1, 6)
            pe.wait_ge(S["dve_done"], 29)
            pe_ffn(pe, 1)

        @block.scalar
        def _(act):
            link = Chain(act, S["act_link"])
            act.wait_ge(S["ld_w"], 14 * 16)
            act.wait_ge(S["ld_c"], 64)
            nc.scalar.activation(nega[:, :, :], nega[:, :, :], ACT.Exp).then_inc(S["act_link"], 1)
            link.n += 1
            link(nc.scalar.activation(invat[:, :], invat[:, :], ACT.Exp))
            nc.scalar.activation(onesb[:, :], ones_f, ACT.Copy).then_inc(S["act_link"], 1)
            nc.scalar.activation(ltri[:, :], cfs[:, 257:385], ACT.Copy).then_inc(S["act_link"], 1)
            nc.scalar.activation(selb[:, :, :].rearrange("p n m -> p (n m)"), abar[:, 0:4, :, :].rearrange("p a b l -> p (a b l)"), ACT.Copy
                                 ).then_inc(S["act_link"], 1)
            link.n += 3
            act.wait_ge(S["act_link"], link.n)

            def norm_sqrt(k):
                act.wait_ge(S["dve_link"], dve_at[k])
                nc.scalar.activation(st[:, 3, :], st[:, 2, :], ACT.Sqrt).then_inc(S["abs_r"], 1)

            norm_sqrt(0)
            norm_sqrt(1)
            with act.Fori(0, NC) as j:
                for q in range(4):
                    h = q % 2
                    act.wait_ge(S["psd_ready"], j * 4 + q + 1)
                    act.sem_inc(S["act_past"], 1)
                    if q < 2:
                        nc.scalar.activation(xm[:, h, bass.ts(j, CH)], bank[q][:, :], ACT.Silu,
                                             bias=colv[:, C_CB + h:C_CB + h + 1]).then_inc(S["psd_free"], 1)
                    else:
                        nc.scalar.activation(gate[:, h, bass.ts(j, CH)], bank[q][:, :], ACT.Silu).then_inc(S["psd_free"], 1)
            sp_t = hbuf
            with act.Fori(0, NC) as j:
                for h in range(NH2):
                    act.wait_ge(S["psd_ready"], j * 2 + (4 * NC + h + 1))
                    act.wait_ge(S["w_r"], j * 2 + h + 1)
                    nc.scalar.activation(sp_t[:, h, 0, :], bank[h][:, :], ACT.Abs, bias=colv[:, C_BD + h:C_BD + h + 1]
                                         ).then_inc(S["abs_r"], 1)
                    act.wait_ge(S["abs_r"], j * 2 + (2 + h + 1))
                    nc.scalar.activation(sp_t[:, h, 1, :], sp_t[:, h, 0, :], ACT.Exp, scale=-1.0).then_inc(S["exp_r"], 1)
                    act.wait_ge(S["exp_r"], j * 2 + h + 1)
                    nc.scalar.activation(sp_t[:, h, 2, :], sp_t[:, h, 1, :], ACT.Ln, bias=1.0).then_inc(S["ln_r"], 1)

            def pro_a(b, par):
                act.wait_ge(S["pro_x"], b + 1)
                if not (isinstance(b, int) and b < 2):
                    act.wait_ge(S["dw_ready"], b * 16 - 16)
                    act.wait_ge(S["cb_ready"], b - 1)
                nc.scalar.activation(xT[:, par, :, :].rearrange("p c d -> p (c d)"), bank[6][:, :], ACT.Copy).then_inc(S["ee"], 1)
                nc.scalar.activation(bcur[:, par, :], bank[7][0:N, 0:L], ACT.Identity, bias=colv[0:N, C_BB:C_BB + 1]
                                     ).then_inc(S["ee"], 1)
                nc.scalar.activation(ccur[:, par, :], bank[7][0:N, L:2 * L], ACT.Identity, bias=colv[0:N, C_BC:C_BC + 1]
                                     ).then_inc(S["ee"], 1)
                act.wait_ge(S["ee"], b * 3 + 3)
                nc.scalar.activation(csp[0:N, par, :], ccur[:, par, :], ACT.Copy).then_inc(S["pro_xe"], 1)
                act.wait_ge(S["pro_xe"], b + 1)
                act.sem_inc(S["csp_hi"], 1)

            def pro_b(b, par):
                act.wait_ge(S["pro_bt"], b + 1)
                if not (isinstance(b, int) and b < 2):
                    act.wait_ge(S["bd_ready"], b - 1)
                nc.scalar.activation(btok[:, par, :, :].rearrange("p c n -> p (c n)"), bank[6][:, 0:2 * N], ACT.Copy
                                     ).then_inc(S["pro_bte"], 1)
                act.wait_ge(S["csp_r"], b + 1)
                nc.scalar.activation(csp[32:32 + N, par, :], cres[:, 0, :], ACT.Copy).then_inc(S["csp_mid"], 1)
                act.wait_ge(S["csp_r2"], b + 1)
                nc.scalar.activation(csp[64:64 + N, par, :], cres[:, 1, :], ACT.Copy).then_inc(S["csp_lo"], 1)

            def pro_c(b, par):
                act.wait_ge(S["m_ready"], b + 1)
                if not (isinstance(b, int) and b < 2):
                    act.wait_ge(S["yg_ready"], b - 1)
                nc.scalar.activation(mcur[:, par, :, :].rearrange("p h l -> p (h l)"), bank[7][:, :], ACT.Copy
                                     ).then_inc(S["m_evac"], 1)

            ymt = z2p[:, :, :].rearrange("p b l -> p (b l)")

            def down_a(b, par):
                act.wait_ge(S["dn_ready"], b + 1)
                act.sem_inc(S["act_past"], 1)
                nc.scalar.activation(ymt[:, bass.ds(b * L, L)], bank[6][:, 0:L], ACT.Identity,
                                     bias=colv[:, C_DN:C_DN + 1]).then_inc(S["dn_evac"], 1)

            def main(b, par, more):
                for s in range(16):
                    n2, h = s // 2, s % 2
                    act.wait_ge(S["ab_free"], b * 16 + s + 1)
                    act.sem_inc(S["act_past"], 1)
                    for r in range(2):
                        n = 2 * n2 + r
                        m = nc.scalar.activation(abar[:, s % 8, r, :], delta[:, h, bass.ds(b * L, L)], ACT.Exp,
                                                 scale=negs[:, h, n:n + 1])
                    m.then_inc(S["ab_ready"], 1)
                    if s == 7 and not (isinstance(b, int) and b == 0):
                        down_a(b - 1, 1 - par)
                    if more:
                        if s == 9:
                            pro_a(b + 1, 1 - par)
                        if s == 12:
                            pro_b(b + 1, 1 - par)
                        if s == 14:
                            pro_c(b + 1, 1 - par)

            negs = nega
            act.wait_ge(S["pool_done"], 2)
            act.sem_inc(S["act_done"], 2)
            pro_a(0, 0)
            pro_b(0, 0)
            pro_c(0, 0)
            act.wait_ge(S["dve_link"], dve_at["delta"])
            main(0, 0, True)
            with act.Fori(0, 3) as i:
                main(i * 2 + 1, 1, True)
                main(i * 2 + 2, 0, True)
            main(7, 1, False)
            down_a(7, 1)
            act.wait_ge(S["dve_link"], dve_at["smax0"])
            nc.scalar.activation(sc[:, :, 0:E0], sc[:, :, 0:E0], ACT.Exp).then_inc(S["exp_r"], 1)

            def gate_rows(E, first):
                for q in range(4):
                    act.wait_ge(S["pe_done"], first + q + 1)
                    nc.scalar.activation(gtT[0:E, 4 * q:4 * q + 4, :].rearrange("e t p -> e (t p)"), bank[6][0:E, :], ACT.Copy
                                         ).then_inc(S["act_done"], 1)

            gate_rows(E0, 5)
            act_ffn(act, 0)
            norm_sqrt(2)
            for q in range(4):
                act.wait_ge(S["pe_done"], 14 + q)
                m = nc.scalar.activation(vtok[:, 4 * q:4 * q + 4, :].rearrange("p t d -> p (t d)"), bank[q][:, :], ACT.Copy)
            m.then_inc(S["act_link"], 1)
            act.wait_ge(S["dve_link"], dve_at["smax1"])
            nc.scalar.activation(sc[:, :, :], sc[:, :, :], ACT.Exp).then_inc(S["exp_r"], 1)
            act.sem_inc(S["qk_sb"], 1)
            with act.Fori(0, NB) as b:
                act.wait_ge(S["qk_ps"], b + 1)
                act.wait_ge(S["pm_free"], b * 8 + 8)
                for g in range(2):
                    nc.scalar.activation(qcur[:, g, :], bank[4 + g][:, 0:L], ACT.Copy)
                    m = nc.scalar.activation(kcur[:, g, :], bank[4 + g][:, L:2 * L], ACT.Copy)
                m.then_inc(S["qk_sb"], 1)
                act.wait_ge(S["pm_free"], b * 8 + 16)
                act.sem_inc(S["act_past"], 1)
                nc.scalar.activation(ret[:, bass.ds(b * 2, 2), :], bank[6][:, 0:2 * P].rearrange("p (t d) -> p t d", t=2), ACT.Copy
                                     ).then_inc(S["r_free"], 1)
            act.wait_ge(S["dve_link"], dve_at["gn"])
            nc.scalar.activation(hbuf[:, 1, 1, 0:NT * HEADS], hbuf[:, 1, 0, 0:NT * HEADS], ACT.Sqrt).then_inc(S["abs_r"], 1)
            for q in range(4):
                act.wait_ge(S["ps_ready"], 13 + q)
                nc.scalar.activation(oT[:, q * CH:(q + 1) * CH], bank[1][:, :], ACT.Silu).then_inc(S["ps_free"], 1)
            gate_rows(E1, 22)
            act_ffn(act, 1)

        @block.gpsimd
        def _(pool):
            link = Chain(pool, S["pool_link"])
            for name, n in (("psd_free", 4), ("ab_free", 8), ("p_ready", 2), ("y_free", 2), ("p_free", 4),
                            ("h_ready", HC), ("d_ready", 5), ("pm_free", 8), ("f_acc", 2), ("w_r", 2), ("s_free", 4),
                            ("r_free", 1)):
                pool.sem_inc(S[name], n)
            link(nc.gpsimd.memset(z2p[:, :, 0:K - 1], 0.0))
            link(nc.gpsimd.memset(csp[:, :, :], 0.0))
            pool.wait_ge(S["ld_w"], 14 * 16)
            for k in range(K):
                m = nc.gpsimd.tensor_tensor(wconv[:, k, :], wup1, convb[:, k, :], ALU.mult)
            m.then_inc(S["pool_done"], 1)
            pool.wait_ge(S["dve_link"], dve_at["inva"])
            for h in range(NH2):
                link(nc.gpsimd.tensor_tensor(diag[:, h, :, :], ident[:, None, :].broadcast_to([P, N, P]),
                                             inva[:, h, :, None].broadcast_to([P, N, P]), ALU.mult))
            pool.sem_inc(S["pool_done"], 1)

            pool.wait_ge(S["xm_ready"], 1)

            def pro(b, par):
                if not (isinstance(b, int) and b < 2):
                    pool.wait_ge(S["yg_ready"], b - 1)
                    pool.wait_ge(S["pro_x"], b - 1)
                pool.sem_inc(S["pool_past"], 1)
                nc.gpsimd.tensor_copy(xcur[:, par, :, :], xm[:, :, bass.ds(b * L, L)]).then_inc(S["xcur_ready"], 1)
                pool.wait_ge(S["csp_hi"], b + 1)
                if not (isinstance(b, int) and b == 0):
                    pool.wait_ge(S["csp_lo"], b)
                nc.gpsimd.tensor_tensor(cres[:, 0, :], ccur[:, par, :], csp[0:N, par, :], ALU.subtract).then_inc(S["csp_r"], 1)
                if not (isinstance(b, int) and b == 0):
                    pool.wait_ge(S["m_ready"], b)
                nc.gpsimd.tensor_tensor(cb[:, par, :], ccur[:, par, :], bcur[:, par, :], ALU.mult).then_inc(S["cb_ready"], 1)
                pool.wait_ge(S["csp_mid"], b + 1)
                pool.sem_inc(S["pool_past"], 1)
                nc.gpsimd.tensor_copy(cmid[:, :], cres[:, 0, :]).then_inc(S["pool_link"], 1)
                pool.wait_ge(S["pool_link"], b + link.n + 1)
                nc.gpsimd.tensor_tensor(cres[:, 1, :], cres[:, 0, :], cmid[:, :], ALU.subtract).then_inc(S["csp_r2"], 1)
                pool.wait_ge(S["pro_bte"], b + 1)
                if not (isinstance(b, int) and b < 2):
                    pool.wait_ge(S["dw_ready"], b * 16 - 16)
                for c in range(2):
                    m = nc.gpsimd.tensor_tensor(bd[:, par, c, :, :], bid[:, None, :].broadcast_to([P, N, P + 1]),
                                                btok[:, par, c, :, None].broadcast_to([P, N, P + 1]), ALU.mult)
                m.then_inc(S["bd_ready"], 1)

            pro(0, 0)
            pro(1, 1)
            with pool.Fori(0, 3) as i:
                pro(i * 2 + 2, 0)
                pro(i * 2 + 3, 1)



def kernel(**inputs):
    import numpy as np
    import concourse.bacc as bacc
    from concourse.bass_utils import run_bass_kernel_spmd as run

    a = {k: np.asarray(v) for k, v in inputs.items()}
    f = np.float32
    r = np.arange(P)
    ident = np.eye(P, dtype=f)
    bid = np.zeros((P, P + 1), f)
    bid[r, r] = 1
    bid[r, r + 1] = -1
    sel = np.zeros((P, N, P), f)
    for part in range(3):
        sel[32 * part + np.arange(N), np.arange(N), :] = 1
    cf = np.concatenate([ident, bid, np.ones((P, P), f), np.triu(np.ones((P, P), f), 1),
                         np.tile(np.arange(E1, dtype=f), (P, 1)), sel.reshape(P, -1)], axis=1)
    gam = (1.0 - np.exp(np.linspace(np.log(1.0 / 512.0), np.log(1.0 / 32.0), HEADS))).astype(f)
    diff = np.arange(L)[None, :] - np.arange(L)[:, None]
    dec = np.where(diff >= 0, gam[:, None, None] ** np.where(diff >= 0, diff, 0).astype(f), 0).astype(f)
    mask = np.concatenate([dec[:, 0:P, :], dec[:, P:L, P:L]], axis=2).transpose(1, 0, 2)
    bits = np.tile((1 << np.arange(NBITS - 1, -1, -1))[None, :, None], (P, 1, E0))
    z = lambda v, n: np.ascontiguousarray(v.reshape(n, P).T)
    col = np.zeros((P, 107), f)
    col[:, 0] = a["L0_attn_ln_g"]
    col[:, 1] = a["L0_attn_ln_b"]
    col[:, 2:4] = z(a["L0_attn_conv_b"], 2)
    col[:, 4:6] = z(a["L0_attn_b_ll"][0:DI], 2)
    col[0:N, 6] = a["L0_attn_b_ll"][DI:DI + N]
    col[0:N, 7] = a["L0_attn_b_ll"][DI + N:]
    col[:, 8] = a["L0_attn_b_down"]
    col[:, 9:41] = z(a["L0_ffn_b1"], E0 * HC)
    col[:, 41:105] = z(a["L1_ffn_b1"], E1 * HC)
    col[:, 105] = a["L1_attn_gn_w"]
    col[:, 106] = a["L1_attn_gn_b"]

    def padded(w):
        o = np.zeros((P, 2, 4, 32), f)
        for h in range(HEADS):
            o[h * HD:(h + 1) * HD, h // 4, h % 4, 0:HD] = w[h]
        return o.reshape(P, 2, P)

    wv = np.zeros((P, P), f)
    for h in range(HEADS):
        wv[h * HD:(h + 1) * HD, h * HD:(h + 1) * HD] = a["L1_attn_Wv"][h]
    down = lambda w, e: w.reshape(e, HC, P, P).transpose(0, 2, 1, 3).reshape(e, P, HC * P)
    arrays = dict(
        x=a["L0_attn_X"].reshape(T, P), cf=cf, mask_d=mask, bits_i=bits.astype(np.int32), bits_f=bits.astype(f),
        cols=col, conv_t=a["L0_attn_conv_w"].reshape(DI, K).T,
        w_up1=a["L0_attn_W_up1"].T, w_up2=a["L0_attn_W_up2"].T, w_ll=a["L0_attn_W_ll"].T, a_log=a["L0_attn_A_log"],
        a_log_t=a["L0_attn_A_log"].T, w_down=a["L0_attn_W_down"].T, wr0=a["L0_ffn_Wr"], w1_0=a["L0_ffn_W1"],
        w2_0=down(a["L0_ffn_W2"], E0), b2_0=a["L0_ffn_b2"], wq=padded(a["L1_attn_Wq"]), wk=padded(a["L1_attn_Wk"]),
        wv=wv, wg=a["L1_attn_W1"], wo=a["L1_attn_W2"], wr1=a["L1_ffn_Wr"], br1=a["L1_ffn_br"].reshape(1, E1),
        w1_1=a["L1_ffn_W1"], w2_1=down(a["L1_ffn_W2"], E1), b2_1=a["L1_ffn_b2"])
    arrays = {k: np.ascontiguousarray(v) for k, v in arrays.items()}
    nc = bacc.Bacc("TRN2", target_bir_lowering=False, num_devices=1)
    ins = {k: nc.dram_tensor(f"in_{k}", v.shape, mybir.dt.from_np(v.dtype), kind="ExternalInput").ap()
           for k, v in arrays.items()}
    out = nc.dram_tensor("out_x", [T, P], F32, kind="ExternalOutput").ap()
    layer_pair(nc, out=out, **{k: v for k, v in ins.items() if k != "rows"})
    res = run(nc, [{f"in_{k}": v for k, v in arrays.items()}], core_ids=[0])
    return res.results[0]["out_x"].reshape(NB, L, P)
```

```python
from contextlib import ExitStack

import concourse.bass as bass
from concourse import mybir

F32 = mybir.dt.float32
BF16 = mybir.dt.bfloat16
I32 = mybir.dt.int32
U32 = mybir.dt.uint32
ALU = mybir.AluOpType
ACT = mybir.ActivationFunctionType
AX = mybir.AxisListType

P = 128
NB, L = 8, 256
T = NB * L
NT = T // P
CH = 512
NC = T // CH
DI, N, K = 256, 16, 4
NH2 = DI // P
LP = L + K
HID = 512
HC = HID // P
E0, KTOP = 8, (T * 2) // 8
E1 = 16
SLOTT = 48
SLOTS = SLOTT * P
YLAG = 6
LAG = 3
HEADS, HD = 8, 16
SC = 384
EPS = 1e-5
ROW1 = P + 2
ROW = P + E0
PB = HID + P
ROUNDS = 16


class Chain:

    def __init__(self, eng, sem):
        self.eng, self.sem, self.n, self.calls = eng, sem, 0, 0

    def __call__(self, ins):
        ins.then_inc(self.sem, 1)
        self.n = self.n + 1
        self.calls += 1
        self.eng.wait_ge(self.sem, self.n)

    def more(self, ins):
        ins.then_inc(self.sem, 1)
        self.n = self.n + 1
        self.calls += 1

    def loop(self, i, per):
        self.start, self.per, self.calls = self.n, per, 0
        self.n = self.start + i * per

    def end(self, count):
        assert self.calls == self.per, self.calls
        self.n = self.start + count * self.per


def layer_pair(nc, x, cf, mask_d, bits_i, bits_f, cols, conv_t, w_up1, w_up2, w_ll, a_log, a_log_t, w_down,
               wr0, w1_0, w2_0, b2_0, wq, wk, wv, wg, wo, wr1, br1, w1_1, w2_1, b_1, out):
    ctx = ExitStack()
    with ctx:
        def sb(name, shape, dt=F32):
            return ctx.enter_context(nc.sbuf_tensor(name, shape, dt))

        def sem(name):
            return ctx.enter_context(nc.semaphore(name))

        bank = [ctx.enter_context(nc.psum_tensor(f"bank{i}", [P, 512], F32)) for i in range(8)]

        acc = sb("acc", [P, NT, P])
        xnw = sb("xnw", [P, NT, ROW1])
        xn = xnw[:, :, 0:P]
        xnT = sb("xnT", [P, T])
        hbuf = sb("hbuf", [P, 2, HC, CH])
        z2p = sb("z2p", [P, NB, LP])
        w1b = sb("w1b", [P, 2, HID])
        w2b = sb("w2b", [P, 2, HC, P])
        xm = sb("xm", [P, NH2, T])
        gate = sb("gate", [P, NH2, T])
        delta = sb("delta", [P, NH2, T])
        zbuf = sb("zbuf", [P, 4, 2, L])
        arena = sb("arena", [P, E1 * HID])
        abar = arena[:, 0:4096].rearrange("p (a b l) -> p a b l", a=8, b=2)
        bd = sb("bd", [P, 2, 2, N, P + 1])
        zb = arena[:, 4096:8192].rearrange("p (a b l) -> p a b l", a=8, b=2)
        hb = hbuf[:, :, :, :].rearrange("p a c t -> p (a c t)")
        xnf = xnw[:, :, :].rearrange("p t d -> p (t d)")
        xcur = hb[:, 0:1024].rearrange("p (a h l) -> p a h l", a=2, h=NH2)
        xT = xnf[:, 0:1024].rearrange("p (a c d) -> p a c d", a=2, c=2)
        bcur = sb("bcur", [N, 2, L])
        ccur = sb("ccur", [N, 2, L])
        cres = sb("cres", [N, 2, L])
        cb = sb("cb", [N, 2, L])
        cmid = sb("cmid", [N, L], BF16)
        csp = sb("csp", [P, 2, L], BF16)
        btok = sb("btok", [P, 2, 2, N])
        mcur = hb[:, 1024:2048].rearrange("p (a h l) -> p a h l", a=2, h=NH2)
        yg = xnf[:, 1024:2048].rearrange("p (a h l) -> p a h l", a=2, h=NH2)
        ident = sb("ident", [P, P])
        cfs = sb("cfs", [P, 129 + 128 + 128 + 128 + 1])
        iota_p = cfs[:, 385:513]
        iota_k = iota_p[:, 0:SLOTT]
        own_p = cfs[:, 513:514]
        bid = cfs[:, 0:129]
        ones_f = cfs[:, 129:257]
        iota_e = iota_p[:, 0:E1]
        onesb = sb("onesb", [P, P], BF16)
        ltri = sb("ltri", [P, P], BF16)
        selb = sb("selb", [P, N, P], BF16)
        NCOL = cols.shape[1]
        colv = sb("colv", [P, NCOL])
        nega = sb("nega", [P, NH2, N])
        inva = sb("inva", [P, NH2, N])
        invat = sb("invat", [N, DI])
        convb = delta[:, 1, 0:K * DI].rearrange("p (k e) -> p k e", k=K)
        wup1 = delta[:, 0, K * DI:(K + 1) * DI]
        wconv = delta[:, 0, 0:K * DI].rearrange("p (k e) -> p k e", k=K)
        wup2 = delta[:, 0, (K + 1) * DI:(K + 2) * DI]
        wll = sb("wll", [P, NH2, DI + 2 * N])
        wdn = sb("wdn", [P, NH2, P])
        wr0s = sb("wr0s", [P, E0])
        bn = sb("bn", [P, NT, 11])
        sc = sb("sc", [P, NT, E1])
        gts = sb("gts", [P, NT, E0])
        sm = sb("sm", [P, 4, NT])
        early = bd[:, 1, :, :, :].rearrange("p c n t -> p (c n t)")
        bis = early[:, 0:3 * ROUNDS * E0].bitcast(I32).rearrange("p (r c e) -> p r c e", c=3, e=E0)
        bfs = early[:, 512:512 + 3 * ROUNDS * E0].rearrange("p (r c e) -> p r c e", c=3, e=E0)
        cmp3 = early[:, 1024:1024 + 3 * P // 2].bitcast(BF16).rearrange("p (c t e) -> p c t e", c=3, e=E0)
        eqb = early[:, 1280:1280 + P // 2].bitcast(BF16).rearrange("p (t e) -> p t e", e=E0)
        cmpb = cmp3[:, 0, :, :]
        tmp8 = xT[:, :, :, :].rearrange("p a b l -> p (a b l)")[:, 0:3 * NT * E0].rearrange("p (a t e) -> p a t e", a=3, e=E0)
        thr = sb("thr", [P, E0], I32)
        cand = sb("cand", [P, 3, E0], I32)
        inc = sb("inc", [P, 3, E0], I32)
        cnt = sb("cnt", [P, 3, E0])
        need = sb("need", [P, E0])
        mx8 = sb("mx8", [P, NT, 8])
        ix8 = sb("ix8", [P, NT, 8], U32)
        ixf = sb("ixf", [P, 2, NT])
        choice, posn, quot, four = (early[:, 1536 + 128 * k:1664 + 128 * k] for k in (0, 1, 2, 3))
        four = early[:, 2048:2560].rearrange("p (m q) -> p m q", q=4)
        choice, posn, quot = (v.rearrange("p (t e) -> p t e", e=E0) for v in (choice, posn, quot))
        posi, quoi, modi = (early[:, 2560 + 128 * k:2688 + 128 * k].bitcast(I32) for k in range(3))
        chb = cmp3[:, 1, :, :]
        zf = zbuf[:, :, :, :].rearrange("p a b l -> p (a b l)")
        place = zf[:, 0:P].rearrange("p (t e) -> p t e", e=E0)
        tokp = zf[:, 128:640].bitcast(BF16).rearrange("p (t e q c) -> p t e q c", t=NT, e=E0, q=4)
        b2b = zf[:, 640:640 + 2 * P].rearrange("p (a d) -> p a d", a=2)
        idx = zf[:, 1024:1024 + 4 * E0].bitcast(I32)
        idxf = zf[:, 1024 + 4 * E0:1028 + 4 * E0]
        xmf = xm[:, :, :].rearrange("p h t -> p (h t)")
        xg = xmf[:, 0:4 * 4 * ROW].rearrange("p (a q r) -> p a q r", a=4, q=4)
        xgT = xmf[:, 4096 - 1024:4096].rearrange("p (a s) -> p a s", a=2)
        hot = gate[:, 0, :].bitcast(BF16).rearrange("p (a t r) -> p a t r", a=2, t=NT)
        ye = gate[:, 1, 0:1024].rearrange("p (a q d) -> p a q d", a=2, q=4)
        rows = nc.dram_tensor("token_rows", [T, ROW], F32, kind="Internal").ap()
        moe = nc.dram_tensor("expert_sums", [T, P], F32, kind="Internal").ap()
        latef = delta[:, :, :].rearrange("p h t -> p (h t)")
        maskd = latef[:, 0:HEADS * SC].rearrange("p (h c) -> p h c", h=HEADS)
        centre = latef[:, HEADS * SC:HEADS * SC + P]
        average = latef[:, HEADS * SC + P:HEADS * SC + 2 * P]
        zs = z2p[:, :, :].rearrange("p b l -> p (b l)")
        wqs, wks, wvs, wgs, wos = (zs[:, k * P:(k + 1) * P] for k in (0, 1, 4, 5, 6))
        wr1s = zs[:, 7 * P:7 * P + E1]
        br1s = zs[0:1, 7 * P + 32:7 * P + 32 + E1]
        w1r = bd[:, :, :, :, :].rearrange("p a c n t -> p (a c n t)")[:, 0:E1 * HID].rearrange("p (e h) -> p e h", e=E1)
        w2r = arena[:, :].rearrange("p (e c d) -> p e c d", e=E1, c=HC)
        w1f = w1b[:, :, :].rearrange("p a h -> p (a h)")
        w2f = w2b[:, :, :, :].rearrange("p a c d -> p (a c d)")
        xs = xnT[:, 0:8 * ROW1].rearrange("p (k r) -> p k r", k=8)
        ys = w1f[:, 4 * P:8 * P].rearrange("p (k d) -> p k d", k=4)
        xsT = sb("xsT", [P, 2, P])
        hs = hbuf[:, 0, :, :].rearrange("p (a b) t -> p a (b t)", a=2)[:, :, 0:HID]
        hT = hbuf[:, 1, :, :].rearrange("p (a b) t -> p a (b t)", a=2)[:, :, 0:HID]
        bias1 = w2f[0:E1, 0:PB]
        bhi = w2f[0:E1, PB:PB + PB // 2].bitcast(BF16)
        bres = latef[0:E1, HEADS * SC + 2 * P:HEADS * SC + 2 * P + PB]
        bmid = bcur[:, :, :].rearrange("n a l -> n (a l)")[:, 0:PB // 2].bitcast(BF16)
        blo = ccur[:, :, :].rearrange("n a l -> n (a l)")[:, 0:PB // 2].bitcast(BF16)
        b1p = delta[0:3, :, :].rearrange("p h t -> p (h t)").bitcast(BF16).rearrange("p (e h) -> p e h", e=E1)
        b2p = zbuf[0:3, 0:2, :, :].rearrange("p a b l -> p (a b l)").bitcast(BF16).rearrange("p (e d) -> p e d", e=E1)
        inc8 = sb("inc8", [P, 1, E1], I32)
        ekf = sb("ekf", [P, SLOTT])
        mkb = sb("mkb", [P, NT, E1], BF16)
        slot = sb("slot", [P, 2, NT], I32)
        eidx = sb("eidx", [P, SLOTT], I32)
        esm = sb("esm", [P, 5, E1])
        xd = nc.dram_tensor("slots_in", [SLOTS, ROW1], F32, kind="Internal").ap()
        kT = w1f[:, 0:2 * L].rearrange("p (a l) -> p a l", a=2)
        qm = xm[:, :, :].rearrange("p a (h l) -> p a h l", h=HEADS)
        vmf = [zf, gate[:, 0, :]]
        vm = [v.rearrange("p (t h d) -> p t h d", t=2, h=HEADS) for v in vmf]
        pbuf = hbuf[:, 1, :, 0:SC]
        vtok = gate[:, 1, :].rearrange("p (t d) -> p t d", t=NT)
        oT = gate[:, 1, :]
        retT = hbuf[:, 0, :, :].rearrange("p c t -> p (c t)")

        C_LNG, C_LNB, C_CB, C_BD, C_BB, C_BC, C_DN, C_B10, C_B11, C_GW, C_GB, C_EPS, C_HEAD = 0, 1, 2, 4, 6, 7, 8, 9, 41, 105, 106, 107, 108

        names = ("act_past pe_past pool_past "
                 "ld_x0 ld_x1 ld_x2 ld_x3 sum_ready norm_ready norm_root ld_c ld_w ld_w2 ld_late pe_done dve_done act_done pool_done wconv_ready act_link dve_link pool_link "
                 "ps_ready ps_free psd_ready psd_free ab_ready ab_free dw_ready cbc_ready p_ready q_ready p_free "
                 "y_ready y_free xcur_ready pro_x pro_xe pro_bt pro_bte bd_ready csp_hi csp_r csp_mid csp_r2 csp_lo "
                 "cb_ready m_ready m_evac xm_ready yg_ready yg_used dn_ready dn_evac "
                 "u_ready h_ready d_ready w1_in0 w1_in1 w2_in0 w2_in1 layer0 rows_x gates_ready rows_g moe_zero hot_ready cp_ready id_ready "
                 "xg_in0 xg_in1 xg_in2 xg_in3 xg_ps xg_sb ye_ready added moe_in0 moe_in1 moe_in2 moe_in3 "
                 "ee abs_r exp_r sm_exp ln_r w_r cnt_in cnt_out st_out "
                 "ld_w1 ld_b ld_bp b_split scattered xs_in0 xs_in1 xs_in2 xs_in3 xs_in4 xs_in5 xs_in6 xs_in7 xT_ps xT_sb h_ps h_sb hT_ps hT_sb y_ps y_sb "
                 "sum_out added1 "
                 "qk_ps qk_sb s_ready pm_ready pm_free r_free vm_zero gc_ready gsq_ready gv_ready groot gate_ps gate_sb").split()
        S = {n: sem(n) for n in names}

        block = ctx.enter_context(nc.Block())

        def expert_steps(stages):
            for s in range(E0 + 3):
                for lag, f in stages:
                    if 0 <= s - lag < E0:
                        f(s - lag)

        def slot_steps(eng, stages):
            def step(t, u):
                for lag, f in stages:
                    k = t - lag
                    if not isinstance(k, int) or 0 <= k < SLOTT:
                        f(k, (u - lag) % 8)

            for t in range(8):
                step(t, t)
            with eng.Fori(0, SLOTT // 8 - 1) as i:
                for u in range(8):
                    step(i * 8 + (8 + u), u)
            for t in range(SLOTT, SLOTT + 5):
                step(t, t % 8)

        def later(k, n):
            return not isinstance(k, int) or k >= n

        dve_at = {}

        @block.vector
        def _(dve):
            link = Chain(dve, S["dve_link"])
            V = nc.vector

            def bc(ap, n):
                return ap[:, :, None].broadcast_to([P, NT, n])

            def norm_stats(source, nth, q):
                for t in range(4 * q, 4 * q + 4):
                    link.more(V.bn_stats(bn[:, t, 0:6], source[:, t, :]))
                dve.wait_ge(S["dve_link"], link.n)
                for t in range(4 * q, 4 * q + 4):
                    link.more(V.bn_aggr(bn[:, t, 6:8], bn[:, t, 0:6]))
                dve.wait_ge(S["dve_link"], link.n)
                link(V.tensor_scalar(bn[:, 4 * q:4 * q + 4, 8], bn[:, 4 * q:4 * q + 4, 7], EPS, None, ALU.add))
                dve_at[nth, q] = link.n

            def normalize(dst, source, nth, q):
                dve.wait_ge(S["norm_root"], 4 * nth + q + 1)
                link(V.reciprocal(bn[:, 4 * q:4 * q + 4, 10], bn[:, 4 * q:4 * q + 4, 9]))
                for t in range(4 * q, 4 * q + 4):
                    link.more(V.tensor_scalar(dst[:, t, :], source[:, t, :], bn[:, t, 6:7], bn[:, t, 10:11],
                                              ALU.subtract, ALU.mult))
                dve.wait_ge(S["dve_link"], link.n)
                dve.sem_inc(S["norm_ready"], 1)

            z2 = hbuf[:, 0, :, :].rearrange("p c (q d) -> p (c q) d", d=P)
            norms = {0: (xn, acc), 1: (z2, xn)}
            for nth, q, part in ((0, 0, 0), (0, 1, 0), (0, 0, 1), (0, 2, 0), (0, 1, 1), (0, 3, 0), (0, 2, 1), (1, 0, 0),
                                 (0, 3, 1), (1, 1, 0), (1, 0, 1), (1, 2, 0), (1, 1, 1), (1, 3, 0), (1, 2, 1), (1, 3, 1)):
                dst, source = norms[nth]
                if part:
                    normalize(dst, source, nth, q)
                else:
                    if nth == 0:
                        dve.wait_ge(S[f"ld_x{q}"], 16)
                    norm_stats(source, nth, q)
            dve.sem_inc(S["dve_done"], 2)
            dve.wait_ge(S["act_link"], 2)
            link(V.tensor_scalar(nega[:, :, :], nega[:, :, :], -1.0, None, ALU.mult))
            link(V.tensor_scalar(invat[:, :], invat[:, :], -1.0, None, ALU.mult))
            link(V.reciprocal(inva[:, :, :], nega[:, :, :]))
            link(V.reciprocal(invat[:, :], invat[:, :]))
            dve_at["inva"] = link.n
            def softmax(E, ready, at, nth):
                s = sc[:, :, 0:E]
                dve.wait_ge(S["pe_done"], ready)
                ps = at[:, 0:NT * E].rearrange("p (t e) -> p t e", t=NT)
                link(V.tensor_reduce(sm[:, 0, :], ps, AX.X, ALU.max))
                link(V.tensor_tensor(s, ps, bc(sm[:, 0, :], E), ALU.subtract))
                dve_at[nth] = link.n
                dve.wait_ge(S["sm_exp"], 1 if E == E0 else 2)
                link(V.tensor_reduce(sm[:, 1, :], s, AX.X, ALU.add))
                link(V.reciprocal(sm[:, 2, :], sm[:, 1, :]))
                link(V.tensor_tensor(s, s, bc(sm[:, 2, :], E), ALU.mult))

            softmax(E0, 1, bank[4], "smax0")
            s0 = sc[:, :, 0:E0]

            def per_e(ap):
                return ap[:, None, :].broadcast_to([P, NT, E0])

            tot = bank[5][:, 0:P].rearrange("p (t e) -> p t e", t=NT)
            tot3 = bank[5][:, 0:3 * P].rearrange("p (c t e) -> p c t e", c=3, t=NT)
            link(V.memset(thr[:, :], 0))
            with dve.Fori(0, ROUNDS // 4) as j:
                link.loop(j, 28)
                for r in range(4):
                    i = j * 4 + r
                    link(V.tensor_tensor(cand[:, :, :], thr[:, None, :].broadcast_to([P, 3, E0]),
                                         bis[:, bass.ds(i, 1), :, :].rearrange("p a c e -> p (a c) e"), ALU.bitwise_or))
                    link(V.tensor_tensor(cmp3[:, :, :, :], s0[:, None, :, :].broadcast_to([P, 3, NT, E0]),
                                         cand[:, :, None, :].bitcast(F32).broadcast_to([P, 3, NT, E0]), ALU.is_ge))
                    dve.sem_inc(S["cnt_in"], 1)
                    dve.wait_ge(S["cnt_out"], i + 1)
                    link(V.tensor_reduce(cnt[:, :, :], tot3.rearrange("p c t e -> p c e t"), AX.X, ALU.add))
                    link(V.scalar_tensor_tensor(out=inc[:, :, :], in0=cnt[:, :, :], scalar=float(KTOP),
                                                in1=bfs[:, bass.ds(i, 1), :, :].rearrange("p a c e -> p (a c) e"),
                                                op0=ALU.is_ge, op1=ALU.mult))
                    for c in range(3):
                        link(V.tensor_tensor(thr[:, :], thr[:, :], inc[:, c, :], ALU.bitwise_xor))
            link.end(ROUNDS // 4)
            thf = thr[:, :].bitcast(F32)
            link(V.tensor_tensor(cmpb, s0, per_e(thf), ALU.is_gt))
            dve.sem_inc(S["cnt_in"], 1)
            link(V.tensor_tensor(eqb[:, :, :], s0, per_e(thf), ALU.is_equal))
            dve.wait_ge(S["cnt_out"], ROUNDS + 1)
            link(V.tensor_reduce(cnt[:, 0, :], tot.rearrange("p t e -> p e t"), AX.X, ALU.add))
            dve.sem_inc(S["cnt_in"], 1)
            link(V.tensor_scalar(need[:, :], cnt[:, 0, :], -1.0, float(KTOP), ALU.mult, ALU.add))
            dve.wait_ge(S["cnt_out"], ROUNDS + 2)
            dve.wait_ge(S["rows_x"], 16)
            dve.wait_ge(S["sum_ready"], 1)

            def running(out_, total, within):
                link(V.memset(tmp8[:, 0, 0:1, :], 0.0))
                link(V.tensor_copy(tmp8[:, 0, 1:NT, :], total[:, 0:NT - 1, :]))
                cur = 0
                for d in (1, 2, 4, 8):
                    V.tensor_copy(tmp8[:, 1 - cur, 0:d, :], tmp8[:, cur, 0:d, :]).then_inc(S["dve_link"], 1)
                    link.n += 1
                    link(V.tensor_tensor(tmp8[:, 1 - cur, d:NT, :], tmp8[:, cur, d:NT, :], tmp8[:, cur, 0:NT - d, :], ALU.add))
                    cur = 1 - cur
                link(V.tensor_tensor(out_, tmp8[:, cur, :, :], within, ALU.add))

            own = bank[6][:, 0:P].rearrange("p (t e) -> p t e", t=NT)
            rank = tmp8[:, 2, :, :]
            running(rank, tot, own)
            link(V.tensor_tensor(rank, rank, per_e(need[:, :]), ALU.is_lt))
            link(V.tensor_tensor(rank, rank, eqb[:, :, :], ALU.mult))
            link(V.tensor_tensor(choice, rank, cmpb, ALU.add))
            link(V.tensor_copy(chb, choice))
            dve.sem_inc(S["cnt_in"], 1)
            link(V.tensor_tensor(gts[:, :, :], choice, s0, ALU.mult))
            dve.sem_inc(S["gates_ready"], 1)
            dve.wait_ge(S["cnt_out"], ROUNDS + 3)
            running(posn, tot, own)
            flat = "p t e -> p (t e)"
            link(V.tensor_copy(posi, posn.rearrange(flat)))
            link(V.tensor_scalar(quoi, posi, 7, None, ALU.logical_shift_right))
            link(V.tensor_scalar(modi, posi, P - 1, None, ALU.bitwise_and))
            link(V.tensor_copy(quot.rearrange(flat), quoi))
            link(V.tensor_copy(place.rearrange(flat), modi))
            link(V.tensor_tensor(four, iota_p[:, None, 0:4].broadcast_to([P, P, 4]),
                                 quot.rearrange(flat)[:, :, None].broadcast_to([P, P, 4]), ALU.is_equal))
            link(V.tensor_tensor(four, four, choice.rearrange(flat)[:, :, None].broadcast_to([P, P, 4]), ALU.mult))
            link(V.scalar_tensor_tensor(out=tokp[:, :, :, :, 0].rearrange("p t e q -> p t (e q)"),
                                        in0=four.rearrange("p (t e) q -> p t (e q)", t=NT), scalar=float(P),
                                        in1=iota_e[:, :, None].broadcast_to([P, NT, 4 * E0]), op0=ALU.mult, op1=ALU.mult))
            link(V.tensor_scalar(tokp[:, :, :, :, 1].rearrange("p t e q -> p (t e q)"), four.rearrange("p m q -> p (m q)"), own_p, None, ALU.mult))
            with dve.Fori(0, NC) as j:
                link.loop(j, 5 * NH2)
                for h in range(NH2):
                    d = delta[:, h, bass.ts(j, CH)]
                    dve.wait_ge(S["abs_r"], j * 2 + (h + 1))
                    link(V.tensor_scalar(d, bank[h][:, :], colv[:, C_BD + h:C_BD + h + 1], 0.0, ALU.add, ALU.max))
                    dve.wait_ge(S["exp_r"], j * 2 + h + 1)
                    link(V.tensor_scalar(hbuf[:, h, 3, :], hbuf[:, h, 1, :], 1.0, None, ALU.add))
                    link(V.scalar_tensor_tensor(out=hbuf[:, h, 3, :], in0=hbuf[:, h, 3, :], scalar=-1.0, in1=hbuf[:, h, 1, :],
                                                op0=ALU.add, op1=ALU.subtract))
                    link(V.tensor_tensor(d, d, hbuf[:, h, 3, :], ALU.subtract))
                    dve.wait_ge(S["ln_r"], j * 2 + h + 1)
                    link(V.tensor_tensor(d, d, hbuf[:, h, 2, :], ALU.add))
                    dve.sem_inc(S["psd_free"], 1)
                    dve.sem_inc(S["w_r"], 1)
            link.end(NC)
            dve_at["delta"] = link.n
            dve.wait_ge(S["psd_free"], 4 + 4 * NC)
            dve.sem_inc(S["xm_ready"], 1)

            def mult(b, s):
                n2, h = s // 2, s % 2
                dve.wait_ge(S["cbc_ready"], b * 8 + n2 + 1)
                dve.wait_ge(S["ab_free"], b * 16 + (s + 9))
                for r in range(2):
                    n = 2 * n2 + r
                    m = V.scalar_tensor_tensor(out=zb[:, s % 8, r, :], in0=zb[:, s % 8, r, :], scalar=inva[:, h, n:n + 1],
                                               in1=bank[4][:, r * L:(r + 1) * L], op0=ALU.mult, op1=ALU.mult)
                m.then_inc(S["p_ready"], 1)

            def finish(b, par):
                dve.wait_ge(S["m_evac"], b + 1)
                if later(b, 2):
                    dve.wait_ge(S["dn_ready"], b + 1)
                link(V.tensor_tensor(yg[:, par, :, :], xm[:, :, bass.ds(b * L, L)], mcur[:, par, :, :], ALU.mult))
                dve.wait_ge(S["p_free"], b * 16 + (16 + 8))
                yf = yg[:, par, :, :].rearrange("p h l -> p (h l)")
                link(V.tensor_tensor(yf, bank[5][:, :], yf, ALU.subtract))
                dve.sem_inc(S["y_free"], 1)
                V.tensor_tensor(yg[:, par, :, :], yg[:, par, :, :], gate[:, :, bass.ds(b * L, L)], ALU.mult).then_inc(S["yg_ready"], 1)

            def main(b, par):
                for s in range(16):
                    dve.wait_ge(S["ab_ready"], b * 16 + s + 1)
                    dve.wait_ge(S["dw_ready"], b * 16 + s + 1)
                    dve.wait_ge(S["p_free"], b * 16 + s + 1)
                    for r in range(2):
                        m = V.tensor_tensor_scan(zb[:, s % 8, r, :], bank[s % 4][:, r * L:(r + 1) * L], abar[:, s % 8, r, :],
                                                 0.0, ALU.add, ALU.mult)
                    m.then_inc(S["ab_free"], 1)
                    if s >= 1:
                        mult(b, s - 1)
                    elif later(b, 1):
                        mult(b - 1, 15)
                    if s == 4 and later(b, 1):
                        finish(b - 1, 1 - par)

            main(0, 0)
            with dve.Fori(0, 3) as i:
                link.loop(i, 4)
                main(i * 2 + 1, 1)
                main(i * 2 + 2, 0)
            link.end(3)
            main(7, 1)
            mult(7, 15)
            finish(7, 1)
            dve.sem_inc(S["dve_done"], 1)
            for q in range(4):
                dve.wait_ge(S["pe_done"], q + 2)
                t = acc[:, 4 * q:4 * q + 4, :].rearrange("p t d -> p (t d)")
                V.tensor_tensor(t, t, bank[q % 2][:, :], ALU.add).then_inc(S["dve_done"], 1)


            def one_hot(e):
                if e > 1:
                    dve.wait_ge(S["cp_ready"], e - 1)
                V.tensor_tensor(hot[:, e % 2, :, :], iota_p[:, None, :].broadcast_to([P, NT, P]),
                                place[:, :, e:e + 1].broadcast_to([P, NT, P]), ALU.is_equal).then_inc(S["hot_ready"], 1)

            def indices(e):
                dve.wait_ge(S["cp_ready"], e + 1)
                pair = bank[7][:, 0:8].rearrange("p (q c) -> p q c", c=2)
                link(V.tensor_reduce(idxf, pair, AX.X, ALU.add))
                V.tensor_copy(idx[:, 4 * e:4 * e + 4], idxf).then_inc(S["id_ready"], 1)

            def gated(e):
                dve.wait_ge(S["d_ready"], e + 1)
                if e > 1:
                    dve.wait_ge(S["added"], 64 * (e - 1))
                y = ye[:, e % 2, :, :]
                link(V.tensor_tensor(y, bank[4 + e % 2][:, :].rearrange("p (q d) -> p q d", q=4),
                                     b2b[:, e % 2, None, :].broadcast_to([P, 4, P]), ALU.add))
                V.tensor_tensor(y, y, xg[:, e % 4, :, P + e:P + e + 1].broadcast_to([P, 4, P]), ALU.mult).then_inc(S["ye_ready"], 1)

            expert_steps(((0, one_hot), (0, indices), (3, gated)))
            dve.sem_inc(S["layer0"], 1)

            def layer0_sum(q):
                dve.wait_ge(S[f"moe_in{q}"], 16)
                link(V.tensor_tensor(acc[:, 4 * q:4 * q + 4, :], acc[:, 4 * q:4 * q + 4, :], xn[:, 4 * q:4 * q + 4, :], ALU.add))

            for q in range(5):
                if q < 4:
                    layer0_sum(q)
                    norm_stats(acc, 2, q)
                if q:
                    normalize(xn, acc, 2, q - 1)
            link(V.tensor_scalar(xnw[:, :, P].bitcast(I32), iota_e, float(P), own_p, ALU.mult, ALU.add))
            dve.sem_inc(S["dve_done"], 1)
            softmax(E1, 10, bank[4], "smax1")
            dve.sem_inc(S["dve_done"], 1)
            for t in range(NT):
                V.max(mx8[:, t, :], sc[:, t, :]).then_inc(S["dve_link"], 1)
                link.n += 1
            dve.wait_ge(S["dve_link"], link.n)
            for t in range(NT):
                V.max_index(ix8[:, t, :], mx8[:, t, :], sc[:, t, :]).then_inc(S["dve_link"], 1)
                link.n += 1
            dve.wait_ge(S["dve_link"], link.n)
            oh = [hbuf[:, 0, w, 0:NT * E1].rearrange("p (t e) -> p t e", t=NT) for w in range(2)]
            pre = [hbuf[:, 1, w, 0:NT * E1].rearrange("p (t e) -> p t e", t=NT) for w in range(2)]
            ek = hbuf[:, 1, 2:4, :].rearrange("p a t -> p (a t)")[:, 0:SLOTT * E1].rearrange("p (k e) -> p k e", e=E1)
            for w in range(2):
                link(V.tensor_copy(ixf[:, w, :], ix8[:, :, w]))
                link(V.tensor_tensor(oh[w], iota_e[:, None, :].broadcast_to([P, NT, E1]),
                                     ixf[:, w, :, None].broadcast_to([P, NT, E1]), ALU.is_equal))
            link(V.tensor_tensor(mkb[:, :, :], oh[0], oh[1], ALU.add))
            dve.sem_inc(S["dve_done"], 1)
            dve.wait_ge(S["pe_done"], 11)
            within = bank[7][:, 0:NT * E1].rearrange("p (t e) -> p t e", t=NT)
            total = bank[7][:, NT * E1:2 * NT * E1].rearrange("p (t e) -> p t e", t=NT)
            link(V.memset(pre[0][:, 0:1, :], 0.0))
            link(V.tensor_copy(pre[0][:, 1:NT, :], total[:, 0:NT - 1, :]))
            cur = 0
            for d in (1, 2, 4, 8):
                link(V.tensor_copy(pre[1 - cur][:, 0:d, :], pre[cur][:, 0:d, :]))
                link(V.tensor_tensor(pre[1 - cur][:, d:NT, :], pre[cur][:, d:NT, :], pre[cur][:, 0:NT - d, :], ALU.add))
                cur = 1 - cur
            ti = inc8[:, 0, :]
            link(V.tensor_tensor(esm[:, 0, :], pre[cur][:, NT - 1, :], total[:, NT - 1, :], ALU.add))
            link(V.tensor_scalar(ti, esm[:, 0, :], float(P - 1), None, ALU.add))
            link(V.tensor_scalar(ti, ti, 7, None, ALU.logical_shift_right))
            link(V.tensor_copy(esm[:, 1, :], ti))
            link(V.memset(esm[:, 2, :], 1.0))
            link(V.tensor_tensor_scan(esm[:, 3, :], esm[:, 2, :], esm[:, 1, :], 0.0, ALU.mult, ALU.add))
            link(V.tensor_tensor(esm[:, 4, :], esm[:, 3, :], esm[:, 1, :], ALU.subtract))
            link(V.tensor_scalar(esm[:, 4, :], esm[:, 4, :], float(P), None, ALU.mult))
            link(V.tensor_tensor(pre[cur], pre[cur], within, ALU.add))
            link(V.tensor_tensor(pre[cur], pre[cur], esm[:, 4, None, :].broadcast_to([P, NT, E1]), ALU.add))
            for w in range(2):
                link(V.tensor_tensor(oh[w], oh[w], pre[cur], ALU.mult))
                link(V.tensor_reduce(ixf[:, w, :], oh[w], AX.X, ALU.add))
                link(V.tensor_copy(slot[:, w, :], ixf[:, w, :]))
            link(V.tensor_tensor(ek, iota_k[:, :, None].broadcast_to([P, SLOTT, E1]),
                                 esm[:, 3, None, :].broadcast_to([P, SLOTT, E1]), ALU.is_ge))
            link(V.tensor_reduce(ekf[:, :], ek, AX.X, ALU.add))
            link(V.tensor_scalar(eidx[:, :], ekf[:, :], float(E1 - 1), None, ALU.min))
            dve.wait_ge(S["act_link"], 6)
            dve.sem_inc(S["dve_done"], 1)
            dve.wait_ge(S["ld_late"], 8 * 16)
            with dve.Fori(0, NB) as b:
                for h in range(HEADS):
                    dve.wait_ge(S["s_ready"], b * 8 + (h + 1))
                    dve.wait_ge(S["pm_free"], b * 8 + (h + 5))
                    V.tensor_tensor(pbuf[:, h % 4, :], bank[h % 4][:, 0:SC], maskd[:, h, :], ALU.mult).then_inc(S["pm_ready"], 1)
            dve.sem_inc(S["dve_done"], 1)
            for q in range(4):
                o = slice(q * CH, (q + 1) * CH)
                rt = hbuf[:, 1, 2 + q % 2, :]
                dve.wait_ge(S["gate_sb"], q + 1)
                link.more(V.tensor_scalar(oT[:, o], oT[:, o], colv[:, C_GB:C_GB + 1], None, ALU.add))
                dve.wait_ge(S["groot"], q + 1)
                link(V.reciprocal(rt, rt))
                link(V.tensor_tensor(rt, bank[q][:, :], rt, ALU.mult))
                V.scalar_tensor_tensor(out=oT[:, o], in0=rt, scalar=colv[:, C_GW:C_GW + 1], in1=oT[:, o],
                                       op0=ALU.mult, op1=ALU.add).then_inc(S["dve_done"], 1)
            for q in range(4):
                dve.wait_ge(S["pe_done"], 12 + q)
                t = acc[:, 4 * q:4 * q + 4, :].rearrange("p t d -> p (t d)")
                V.tensor_tensor(t, t, bank[q][:, :], ALU.add).then_inc(S["dve_done"], 1)

            def h_out(k, u):
                dve.wait_ge(S["hT_ps"], k + 1)
                if later(k, 2):
                    dve.wait_ge(S["y_ps"], k - 1)
                V.tensor_copy(hT[:, u % 2, :], bank[2 + u % 2][:, :]).then_inc(S["hT_sb"], 1)

            def y_out(k, u):
                dve.wait_ge(S["y_ps"], k + 1)
                if later(k, 4):
                    dve.wait_ge(S["added1"], k * 16 - 48)
                V.tensor_scalar(ys[:, u % 4, :], bank[6 + u % 2][:, 0:P], xs[:, u, P + 1:P + 2], None, ALU.mult).then_inc(S["y_sb"], 1)

            slot_steps(dve, ((2, h_out), (LAG, y_out)))

        @block.sync
        def _(sp):
            xv = x.rearrange("(t p) d -> p t d", p=P)
            for q in range(4):
                sp.dma_start(acc[:, 4 * q:4 * q + 4, :], xv[:, 4 * q:4 * q + 4, :]).then_inc(S[f"ld_x{q}"], 16)
            for dst, src in ((ident[:, :], cf[:, 0:P]), (colv[:, :], cols), (cfs[:, :], cf[:, P:P + 514]),
                             (abar[:, 0:4, :, :].rearrange("p a b l -> p (a b l)"), cf[:, P + 514:])):
                sp.dma_start(dst, src).then_inc(S["ld_c"], 16)
            for k in range(K):
                sp.dma_start(convb[:, k, :], conv_t[k, :].partition_broadcast(P)).then_inc(S["ld_w"], 16)
            for dst, src in ((wup1, w_up1), (wup2, w_up2),
                             (wll[:, :, :], w_ll.rearrange("(h p) e -> p h e", p=P)),
                             (wdn[:, :, :], w_down.rearrange("(h p) e -> p h e", p=P)),
                             (nega[:, :, :], a_log.rearrange("(h p) n -> p h n", p=P)),
                             (invat[:, :], a_log_t), (wr0s[:, :], wr0),
                             (bis[:, :, :, :], bits_i), (bfs[:, :, :, :], bits_f)):
                sp.dma_start(dst, src).then_inc(S["ld_w"], 16)
            def weights1(e):
                if e > 1:
                    sp.wait_ge(S["u_ready"], (e - 1) * HC)
                sp.dma_start(w1b[:, e % 2, :], w1_0[e, :, :]).then_inc(S[f"w1_in{e % 2}"], 16)

            def weights2(e):
                if e > 1:
                    sp.wait_ge(S["ye_ready"], e - 1)
                for dst, src in ((w2b[:, e % 2, :, :].rearrange("p c d -> p (c d)"), w2_0[e, :, :]),
                                 (b2b[:, e % 2, :], b2_0[e, :].partition_broadcast(P))):
                    sp.dma_start(dst, src).then_inc(S[f"w2_in{e % 2}"], 16)

            for e in range(2):
                weights1(e)
                weights2(e)
            sp.wait_ge(S["norm_ready"], 4)
            sp.dma_start(rows.rearrange("(t p) r -> p t r", p=P)[:, :, 0:P], xn[:, :, :]).then_inc(S["rows_x"], 16)
            sp.wait_ge(S["gates_ready"], 1)
            sp.dma_start(rows.rearrange("(t p) r -> p t r", p=P)[:, :, P:ROW], gts[:, :, :]).then_inc(S["rows_g"], 16)
            sp.wait_ge(S["dve_done"], 7)
            for dst, src in ((latef[:, 0:HEADS * SC + 2 * P], mask_d), (wqs, wq), (wks, wk), (wvs, wv), (wgs, wg), (wos, wo),
                             (wr1s, wr1), (br1s, br1)):
                sp.dma_start(dst, src).then_inc(S["ld_late"], 16)

            def resident(q):
                e = slice(4 * q, 4 * q + 4)
                sp.dma_start(w1r[:, e, :], w1_1.rearrange("e p h -> p e h")[:, e, :]).then_inc(S["ld_w1"], 16)
                sp.dma_start(w2r[:, e, :, :].rearrange("p e c d -> p e (c d)"),
                             w2_1.rearrange("e p h -> p e h")[:, e, :]).then_inc(S["ld_w1"], 16)

            weights1(2)
            for e in range(2, E0):
                if e + 1 < E0:
                    weights1(e + 1)
                weights2(e)
                if e < 6:
                    resident(e - 2)
            sp.wait_ge(S["added"], 64 * E0)
            for q in range(4):
                sp.dma_start(xn[:, 4 * q:4 * q + 4, :], moe.rearrange("(t p) d -> p t d", p=P)[:, 4 * q:4 * q + 4, :]
                             ).then_inc(S[f"moe_in{q}"], 16)
            sp.wait_ge(S["layer0"], 1)
            sp.dma_start(bias1, b_1).then_inc(S["ld_b"], 16)
            sp.wait_ge(S["b_split"], 1)
            sp.wait_ge(S["gv_ready"], 4)
            for part, src in enumerate((bhi, bmid, blo)):
                sp.dma_start(b1p[part:part + 1, :, :], src[:, 0:HID]).then_inc(S["ld_bp"], 16)
                sp.dma_start(b2p[part:part + 1, :, :], src[:, HID:PB]).then_inc(S["ld_bp"], 16)
            sp.wait_ge(S["scattered"], 33 * 16)

            sp.wait_ge(S["gate_ps"], 4)

            def load(k, u):
                if not isinstance(k, int):
                    sp.wait_ge(S["added1"], k * 16 - 112)
                sp.dma_start(xs[:, u, :], xd[bass.ds(k * P, P), :]).then_inc(S[f"xs_in{u}"], 16)

            for u in range(8):
                load(u, u)
            for q in range(4):
                sp.wait_ge(S["dve_done"], 17 + q)
                sp.dma_start(out.rearrange("(t p) d -> p t d", p=P)[:, 4 * q:4 * q + 4, :], acc[:, 4 * q:4 * q + 4, :]
                             ).then_inc(S["sum_out"], 16)
            with sp.Fori(0, SLOTT // 8 - 1) as i:
                for u in range(8):
                    load(i * 8 + (8 + u), u)
            sp.wait_ge(S["added1"], SLOTT * 16)
            sp.wait_ge(S["sum_out"], 64)

        @block.tensor
        def _(pe):
            pe.wait_ge(S["ld_c"], 64)

            def transpose_norm(src, ready, first):
                for q in range(4):
                    pe.wait_ge(S["norm_ready"], ready + q + 1)
                    for r in range(4):
                        m = pe.transpose(bank[first + q][:, r * P:(r + 1) * P], src[:, 4 * q + r, :], ident[:, :])
                    m.then_inc(S["ps_ready"], 1)

            transpose_norm(xn, 0, 0)
            transpose_norm(hbuf[:, 0, :, :].rearrange("p c (q d) -> p (c q) d", d=P), 4, 4)

            pe.wait_ge(S["ld_w"], 13 * 16)
            pe.wait_ge(S["wconv_ready"], 1)
            pe.wait_ge(S["ps_free"], 8)
            for t in range(NT):
                m = pe.matmul(bank[4][:, t * E0:(t + 1) * E0], xnT[:, t * P:(t + 1) * P], wr0s[:, :], start=True, stop=True)
            m.then_inc(S["pe_done"], 1)

            def count(i):
                pe.wait_ge(S["cnt_in"], i + 1)
                pe.matmul(bank[5][:, 0:3 * P], onesb[:, :], cmp3[:, :, :, :].rearrange("p c t e -> p (c t e)"),
                          start=True, stop=True).then_inc(S["cnt_out"], 1)

            def count_ties():
                pe.wait_ge(S["cnt_in"], ROUNDS + 1)
                pe.matmul(bank[5][:, 0:P], onesb[:, :], cmpb, start=True, stop=True).then_inc(S["cnt_out"], 1)
                pe.wait_ge(S["cnt_in"], ROUNDS + 2)
                pe.matmul(bank[5][:, 0:P], onesb[:, :], eqb[:, :, :], start=True, stop=True)
                pe.matmul(bank[6][:, 0:P], ltri[:, :], eqb[:, :, :], start=True, stop=True).then_inc(S["cnt_out"], 1)
                pe.wait_ge(S["cnt_in"], ROUNDS + 3)
                pe.matmul(bank[5][:, 0:P], onesb[:, :], chb, start=True, stop=True)
                pe.matmul(bank[6][:, 0:P], ltri[:, :], chb, start=True, stop=True).then_inc(S["cnt_out"], 1)

            with pe.Fori(0, NC) as j:
                for q in range(4):
                    pe.wait_ge(S["psd_free"], j * 4 + q + 1)
                    h = q % 2
                    if q < 2:
                        for k in range(K):
                            if q == 0 and k == 3 or q == 1 and k in (1, 3):
                                count(j * 4 + (0 if q == 0 else (k + 1) // 2))
                            m = pe.matmul(bank[q][:, :], wconv[:, k, h * P:(h + 1) * P],
                                          z2p[:, bass.ds(j * 2, 2), k:k + L], start=(k == 0), stop=(k == K - 1))
                    else:
                        m = pe.matmul(bank[q][:, :], wup2[:, h * P:(h + 1) * P],
                                      z2p[:, bass.ds(j * 2, 2), K - 1:K - 1 + L], start=True, stop=True)
                    m.then_inc(S["psd_ready"], 1)
                    if q == 3:
                        count(j * 4 + 3)
            count_ties()
            pe.wait_ge(S["psd_free"], 4 * NC + 4)
            with pe.Fori(0, NC) as j:
                for h in range(NH2):
                    pe.wait_ge(S["psd_free"], j * 2 + (4 * NC + 4 + h - 1))
                    for kh in range(NH2):
                        m = pe.matmul(bank[h][:, :], wll[:, kh, h * P:(h + 1) * P], xm[:, kh, bass.ts(j, CH)],
                                      start=(kh == 0), stop=(kh == NH2 - 1))
                    m.then_inc(S["psd_ready"], 1)
            pe.wait_ge(S["psd_free"], 4 * NC + 4 + 2 * NC)

            DW, CB_, Y, M0, M1 = bank[0:4], bank[4], bank[5], bank[6], bank[7]

            def pro1(b, par):
                pe.wait_ge(S["xcur_ready"], b + 1)
                if not (isinstance(b, int) and b == 0):
                    pe.wait_ge(S["m_evac"], b)
                    pe.wait_ge(S["pro_bte"], b)
                    pe.wait_ge(S["dn_evac"], b - 1) if not (isinstance(b, int) and b == 1) else None
                for c in range(2):
                    for h in range(NH2):
                        pe.transpose(M0[:, c * DI + h * P:c * DI + (h + 1) * P], xcur[:, par, h, c * P:(c + 1) * P], ident[:, :])
                for w in range(2):
                    for h in range(NH2):
                        m = pe.matmul(M1[0:N, w * L:(w + 1) * L], wll[:, h, DI + w * N:DI + (w + 1) * N],
                                      xcur[:, par, h, :], start=(h == 0), stop=(h == NH2 - 1))
                m.then_inc(S["pro_x"], 1)

            def pro2(b, par):
                pe.wait_ge(S["pro_xe"], b + 1)
                pe.sem_inc(S["pe_past"], 1)
                for c in range(2):
                    m = pe.transpose(M0[:, c * N:(c + 1) * N], bcur[:, par, c * P:(c + 1) * P], ident[0:N, 0:N])
                m.then_inc(S["pro_bt"], 1)

            def pro3(b, par):
                pe.wait_ge(S["cb_ready"], b + 1)
                for h in range(NH2):
                    m = pe.matmul(M1[:, h * L:(h + 1) * L], invat[:, h * P:(h + 1) * P], cb[:, par, :], start=True, stop=True)
                m.then_inc(S["m_ready"], 1)

            def down(b, par, last):
                pe.wait_ge(S["yg_ready"], b + 1)
                pe.wait_ge(S["pro_bte"], 8 if last else b + 3)
                for h in range(NH2):
                    m = pe.matmul(M0[:, 0:L], wdn[:, h, :], yg[:, par, h, :], start=(h == 0), stop=(h == NH2 - 1))
                m.then_inc(S["dn_ready"], 1)

            def y_sum(b, s):
                n2, h = s // 2, s % 2
                pe.wait_ge(S["q_ready"], b * 16 + s + 1)
                if s == 0:
                    pe.wait_ge(S["y_free"], b + 1)
                pe.matmul(Y[:, h * L:(h + 1) * L], ident[:, :], zb[:, s % 8, 0, :], start=(s == 0), stop=(s == 15),
                          skip_group_check=True).then_inc(S["p_free"], 1)

            def c_rows(b, par, n2):
                pe.wait_ge(S["p_ready"], b * 16 + 2 * n2 + 2)
                for r in range(2):
                    m = pe.matmul(CB_[:, r * L:(r + 1) * L], selb[:, 2 * n2 + r, :], csp[:, par, :], start=True, stop=True)
                m.then_inc(S["cbc_ready"], 1)

            def main(b, par, more):
                first = isinstance(b, int) and b == 0
                pe.wait_ge(S["csp_lo"], b + 1)
                for s in range(16):
                    n2, h = s // 2, s % 2
                    if h == 0:
                        pe.wait_ge(S["bd_ready"], b * 8 + n2 + 1)
                    pe.wait_ge(S["ab_free"], b * 16 + s + 5)
                    o = DW[s % 4][:, :].rearrange("p (n t) -> p n t", n=2)
                    pe.matmul(o[:, :, 0:P + 1], xT[:, par, 0, h * P:(h + 1) * P], bd[:, par, 0, 2 * n2:2 * n2 + 2, :],
                              start=True, stop=False, skip_group_check=True)
                    pe.matmul(o[:, :, P:L], xT[:, par, 1, h * P:(h + 1) * P], bd[:, par, 1, 2 * n2:2 * n2 + 2, 0:P],
                              start=False, stop=True, skip_group_check=True).then_inc(S["dw_ready"], 1)
                    if h == 1 and s > 1:
                        c_rows(b, par, n2 - 1)
                    elif h == 1 and not first:
                        c_rows(b - 1, 1 - par, 7)
                    if s >= YLAG:
                        y_sum(b, s - YLAG)
                    elif not first:
                        y_sum(b - 1, s + 16 - YLAG)
                    if more:
                        if s == 1:
                            pro1(b + 1, 1 - par)
                        if s == 4:
                            pro2(b + 1, 1 - par)
                        if s == 8:
                            pro3(b + 1, 1 - par)
                    if s == 10 and not first:
                        down(b - 1, 1 - par, not more)

            pe.wait_ge(S["pool_done"], 1)
            pe.wait_ge(S["act_done"], 2)
            pro1(0, 0)
            pro2(0, 0)
            pro3(0, 0)
            main(0, 0, True)
            with pe.Fori(0, 3) as i:
                main(i * 2 + 1, 1, True)
                main(i * 2 + 2, 0, True)
            main(7, 1, False)
            c_rows(7, 1, 7)
            for s in range(16 - YLAG, 16):
                y_sum(7, s)
            pe.wait_ge(S["dn_evac"], 8)
            pe.wait_ge(S["yg_ready"], 8)
            for h in range(NH2):
                m = pe.matmul(M0[:, 0:L], wdn[:, h, :], yg[:, 1, h, :], start=(h == 0), stop=(h == NH2 - 1))
            m.then_inc(S["dn_ready"], 1)
            pe.wait_ge(S["dn_evac"], 9)
            ymt = z2p[:, :, :].rearrange("p b l -> p (b l)")
            for q in range(4):
                pe.wait_ge(S["dve_done"], 3 if q < 2 else 2 + q)
                for r in range(4):
                    t = 4 * q + r
                    m = pe.transpose(bank[q % 2][:, r * P:(r + 1) * P], ymt[:, t * P:(t + 1) * P], ident[:, :])
                m.then_inc(S["pe_done"], 1)

            def compact(e):
                pe.wait_ge(S["hot_ready"], e + 1)
                if e:
                    pe.wait_ge(S["id_ready"], e)
                else:
                    pe.wait_ge(S["dn_evac"], 9)
                for t in range(NT):
                    m = pe.matmul(bank[7][:, 0:8], hot[:, e % 2, t, :], tokp[:, t, e, :, :], start=(t == 0), stop=(t == NT - 1))
                m.then_inc(S["cp_ready"], 1)

            def turn_rows(e):
                pe.wait_ge(S[f"xg_in{e % 4}"], 64 * (e // 4 + 1))
                if e:
                    pe.wait_ge(S["xg_sb"], e)
                for q in range(4):
                    m = pe.transpose(bank[6][:, q * P:(q + 1) * P], xg[:, e % 4, q, 0:P], ident[:, :])
                m.then_inc(S["xg_ps"], 1)

            def up0(e):
                pe.wait_ge(S[f"w1_in{e % 2}"], 16 * (e // 2 + 1))
                pe.wait_ge(S["xg_sb"], e + 1)
                for c in range(HC):
                    if e:
                        pe.wait_ge(S["h_ready"], (e - 1) * HC + c + 1)
                    else:
                        pe.wait_ge(S["dve_done"], 7)
                    pe.matmul(bank[c][:, :], w1b[:, e % 2, c * P:(c + 1) * P], xgT[:, e % 2, :], start=True, stop=True
                              ).then_inc(S["u_ready"], 1)

            def down0(e):
                pe.wait_ge(S[f"w2_in{e % 2}"], 32 * (e // 2 + 1))
                pe.wait_ge(S["h_ready"], (e + 1) * HC)
                if e > 1:
                    pe.wait_ge(S["ye_ready"], e - 1)
                for q in range(4):
                    for c in range(HC):
                        m = pe.matmul(bank[4 + e % 2][:, q * P:(q + 1) * P], hbuf[:, e % 2, c, q * P:(q + 1) * P],
                                      w2b[:, e % 2, c, :], start=(c == 0), stop=(c == HC - 1))
                m.then_inc(S["d_ready"], 1)

            expert_steps(((2, up0), (0, compact), (1, turn_rows), (3, down0)))

            transpose_norm(xn, 8, 0)
            pe.wait_ge(S["ps_free"], 12)
            pe.wait_ge(S["ld_late"], 8 * 16)
            for t in range(NT):
                pe.matmul(bank[4][:, t * E1:(t + 1) * E1], xnT[:, t * P:(t + 1) * P], wr1s, start=True, stop=False)
                m = pe.matmul(bank[4][:, t * E1:(t + 1) * E1], ones_f[0:1, :], br1s, start=False, stop=True)
            m.then_inc(S["pe_done"], 1)
            for q in range(4):
                for r in range(4):
                    t = 4 * q + r
                    m = pe.matmul(bank[q][:, r * P:(r + 1) * P], xnT[:, t * P:(t + 1) * P], wvs, start=True, stop=True)
                m.then_inc(S["pe_done"], 1)
            pe.wait_ge(S["dve_done"], 10)
            pe.matmul(bank[7][:, 0:NT * E1], ltri[:, :], mkb[:, :, :], start=True, stop=True)
            pe.matmul(bank[7][:, NT * E1:2 * NT * E1], onesb[:, :], mkb[:, :, :], start=True, stop=True
                      ).then_inc(S["pe_done"], 1)
            pe.wait_ge(S["dve_done"], 11)

            def project(b, par):
                if not (isinstance(b, int) and b == 0):
                    pe.wait_ge(S["qk_sb"], b)
                pe.sem_inc(S["pe_past"], 1)
                for w, o in ((wqs, 0), (wks, L)):
                    m = pe.matmul(bank[4][:, o:o + L], w, xnT[:, bass.ds(b * L, L)], start=True, stop=True)
                m.then_inc(S["qk_ps"], 1)

            def scores(b, par, h):
                if h == 0:
                    pe.wait_ge(S["qk_sb"], b + 1)
                pe.wait_ge(S["pm_ready"], b * 8 + (h + 1))
                pe.matmul(bank[h % 4][:, 0:L], kT[:, par, 0:P], qm[:, par, h, :], start=True, stop=True)
                pe.matmul(bank[h % 4][:, L:SC], kT[:, par, P:L], qm[:, par, h, P:L], start=True, stop=True
                          ).then_inc(S["s_ready"], 1)

            def retain(b, par, h):
                if h == 0:
                    pe.wait_ge(S["r_free"], b + 1)
                pe.wait_ge(S["pm_ready"], b * 8 + (h + 5))
                o = bank[6 + par]
                pe.matmul(o[:, 0:L], vm[par][:, 0, h, :], pbuf[:, h % 4, 0:L], start=(h == 0), stop=False, skip_group_check=True)
                pe.matmul(o[:, P:L], vm[par][:, 1, h, :], pbuf[:, h % 4, L:SC], start=False, stop=(h == HEADS - 1),
                          skip_group_check=True).then_inc(S["pm_free"], 1)

            def attend(b, par, more):
                for h in range(HEADS):
                    scores(b, par, h)
                    if h >= 3:
                        retain(b, par, h - 3)
                    elif not (isinstance(b, int) and b == 0):
                        retain(b - 1, 1 - par, h + 5)
                    if h == 4 and more:
                        project(b + 1, 1 - par)

            project(0, 0)
            attend(0, 0, True)
            with pe.Fori(0, 3) as i:
                attend(i * 2 + 1, 1, True)
                attend(i * 2 + 2, 0, True)
            attend(7, 1, False)
            for h in range(5, HEADS):
                retain(7, 1, h)
            def gate_in(q):
                if q > 1:
                    pe.wait_ge(S["gate_sb"], q - 1)
                else:
                    pe.wait_ge(S["r_free"], NB + 2)
                pe.matmul(bank[6 + q % 2][:, :], wgs, xnT[:, q * CH:(q + 1) * CH], start=True, stop=True).then_inc(S["gate_ps"], 1)

            def variance(q):
                pe.wait_ge(S["gsq_ready"], q + 1)
                if q > 1:
                    pe.wait_ge(S["groot"], q - 1)
                pe.matmul(bank[4 + q % 2][:, :], average, hbuf[:, 1, q % 2, :], start=True, stop=True).then_inc(S["gv_ready"], 1)

            gate_in(0)
            gate_in(1)
            for q in range(4):
                pe.matmul(bank[q][:, :], centre, retT[:, q * CH:(q + 1) * CH], start=True, stop=True).then_inc(S["gc_ready"], 1)
            gate_in(2)
            gate_in(3)
            for q in range(4):
                variance(q)
            for q in range(4):
                pe.wait_ge(S["dve_done"], 13 + q)
                for r in range(4):
                    t = 4 * q + r
                    m = pe.matmul(bank[q][:, r * P:(r + 1) * P], oT[:, t * P:(t + 1) * P], wos, start=True, stop=True)
                m.then_inc(S["pe_done"], 1)
            pe.wait_ge(S["dve_done"], 20)
            pe.wait_ge(S["ld_w1"], 8 * 16)
            pe.wait_ge(S["ld_bp"], 6 * 16)

            def expert(k):
                return pe.value_load(eidx[0:1, bass.ds(k, 1)], min_val=0, max_val=E1 - 1)

            def turn_x(k, u):
                pe.wait_ge(S[f"xs_in{u}"], (k - u) * 2 + 16)
                if later(k, 2):
                    pe.wait_ge(S["xT_sb"], k - 1)
                pe.transpose(bank[4 + u % 2][:, 0:P], xs[:, u, 0:P], ident[:, :]).then_inc(S["xT_ps"], 1)

            held = {}

            def fetch(k, u):
                held["up"] = expert(k)

            def up(k, u):
                e = held["up"]
                if later(k, 2):
                    pe.wait_ge(S["h_sb"], k - 1)
                pe.wait_ge(S["xT_sb"], k + 1)
                pe.sem_inc(S["pe_past"], 1)
                pe.matmul(bank[u % 2][:, :], onesb[0:3, :], b1p[:, bass.ds(e, 1), :], start=True, stop=False)
                pe.matmul(bank[u % 2][:, :], xsT[:, u % 2, :], w1r[:, bass.ds(e, 1), :], start=False, stop=True
                          ).then_inc(S["h_ps"], 1)

            def turn_h(k, u):
                pe.wait_ge(S["h_sb"], k + 1)
                if later(k, 2):
                    pe.wait_ge(S["hT_sb"], k - 1)
                for c in range(HC):
                    m = pe.transpose(bank[2 + u % 2][:, c * P:(c + 1) * P], hs[:, u % 2, c * P:(c + 1) * P], ident[:, :])
                m.then_inc(S["hT_ps"], 1)

            def down(k, u):
                e = expert(k)
                if later(k, 2):
                    pe.wait_ge(S["y_sb"], k - 1)
                pe.wait_ge(S["hT_sb"], k + 1)
                pe.sem_inc(S["pe_past"], 1)
                pe.matmul(bank[6 + u % 2][:, 0:P], onesb[0:3, :], b2p[:, bass.ds(e, 1), :], start=True, stop=False)
                for c in range(HC):
                    m = pe.matmul(bank[6 + u % 2][:, 0:P], hT[:, u % 2, c * P:(c + 1) * P], w2r[:, bass.ds(e, 1), c, :],
                                  start=False, stop=(c == HC - 1))
                m.then_inc(S["y_ps"], 1)

            slot_steps(pe, ((1, fetch), (0, turn_x), (1, up), (2, turn_h), (LAG, down)))

        @block.scalar
        def _(act):
            link = Chain(act, S["act_link"])
            act.wait_ge(S["ld_c"], 64)

            def norm_root(nth, q):
                act.wait_ge(S["dve_link"], dve_at[nth, q])
                nc.scalar.activation(bn[:, 4 * q:4 * q + 4, 9], bn[:, 4 * q:4 * q + 4, 8], ACT.Sqrt).then_inc(S["norm_root"], 1)

            def turned_out(q, first):
                act.wait_ge(S["ps_ready"], first + q + 1)
                nc.scalar.activation(xnT[:, q * CH:(q + 1) * CH], bank[q][:, :], ACT.Copy).then_inc(S["ps_free"], 1)

            def turned2_out(q):
                act.wait_ge(S["ps_ready"], 4 + q + 1)
                nc.scalar.activation(z2p[:, 2 * q:2 * q + 2, K - 1:K - 1 + L], bank[4 + q][:, :].rearrange("p (b l) -> p b l", b=2),
                                     ACT.Identity, scale=colv[:, C_LNG:C_LNG + 1], bias=colv[:, C_LNB:C_LNB + 1]
                                     ).then_inc(S["ps_free"], 1)

            for q in range(4):
                norm_root(0, q)
            for q in range(2):
                turned_out(q, 0)
            for q in range(4):
                norm_root(1, q)
                if q < 2:
                    turned_out(q + 2, 0)
            for q in range(4):
                turned2_out(q)
            act.wait_ge(S["ld_w"], 13 * 16)
            act.wait_ge(S["ld_c"], 64)
            nc.scalar.activation(nega[:, :, :], nega[:, :, :], ACT.Exp).then_inc(S["act_link"], 1)
            link.n += 1
            link(nc.scalar.activation(invat[:, :], invat[:, :], ACT.Exp))
            nc.scalar.activation(onesb[:, :], ones_f, ACT.Copy).then_inc(S["act_link"], 1)
            nc.scalar.activation(ltri[:, :], cfs[:, 257:385], ACT.Copy).then_inc(S["act_link"], 1)
            nc.scalar.activation(selb[:, :, :].rearrange("p n m -> p (n m)"), abar[:, 0:4, :, :].rearrange("p a b l -> p (a b l)"), ACT.Copy
                                 ).then_inc(S["act_link"], 1)
            link.n += 3
            act.wait_ge(S["act_link"], link.n)
            act.wait_ge(S["dve_link"], dve_at["smax0"])
            nc.scalar.activation(sc[:, :, 0:E0], sc[:, :, 0:E0], ACT.Exp).then_inc(S["sm_exp"], 1)
            with act.Fori(0, NC) as j:
                for q in range(4):
                    h = q % 2
                    act.wait_ge(S["psd_ready"], j * 4 + q + 1)
                    act.sem_inc(S["act_past"], 1)
                    if q < 2:
                        nc.scalar.activation(xm[:, h, bass.ts(j, CH)], bank[q][:, :], ACT.Silu,
                                             bias=colv[:, C_CB + h:C_CB + h + 1]).then_inc(S["psd_free"], 1)
                    else:
                        nc.scalar.activation(gate[:, h, bass.ts(j, CH)], bank[q][:, :], ACT.Silu).then_inc(S["psd_free"], 1)
            sp_t = hbuf
            with act.Fori(0, NC) as j:
                for h in range(NH2):
                    act.wait_ge(S["psd_ready"], j * 2 + (4 * NC + h + 1))
                    act.wait_ge(S["w_r"], j * 2 + h + 1)
                    nc.scalar.activation(sp_t[:, h, 0, :], bank[h][:, :], ACT.Abs, bias=colv[:, C_BD + h:C_BD + h + 1]
                                         ).then_inc(S["abs_r"], 1)
                    act.wait_ge(S["abs_r"], j * 2 + (h + 1))
                    nc.scalar.activation(sp_t[:, h, 1, :], sp_t[:, h, 0, :], ACT.Exp, scale=-1.0).then_inc(S["exp_r"], 1)
                    act.wait_ge(S["exp_r"], j * 2 + h + 1)
                    nc.scalar.activation(sp_t[:, h, 2, :], sp_t[:, h, 1, :], ACT.Ln, bias=1.0).then_inc(S["ln_r"], 1)

            def pro_a(b, par):
                act.wait_ge(S["pro_x"], b + 1)
                if not (isinstance(b, int) and b < 2):
                    act.wait_ge(S["dw_ready"], b * 16 - 16)
                    act.wait_ge(S["cb_ready"], b - 1)
                    act.wait_ge(S["cbc_ready"], b * 8 - 8)
                nc.scalar.activation(xT[:, par, :, :].rearrange("p c d -> p (c d)"), bank[6][:, :], ACT.Copy).then_inc(S["ee"], 1)
                nc.scalar.activation(bcur[:, par, :], bank[7][0:N, 0:L], ACT.Identity, bias=colv[0:N, C_BB:C_BB + 1]
                                     ).then_inc(S["ee"], 1)
                nc.scalar.activation(ccur[:, par, :], bank[7][0:N, L:2 * L], ACT.Identity, bias=colv[0:N, C_BC:C_BC + 1]
                                     ).then_inc(S["ee"], 1)
                act.wait_ge(S["ee"], b * 3 + 3)
                nc.scalar.activation(csp[0:N, par, :], ccur[:, par, :], ACT.Copy).then_inc(S["pro_xe"], 1)
                act.wait_ge(S["pro_xe"], b + 1)
                act.sem_inc(S["csp_hi"], 1)

            def pro_b(b, par):
                act.wait_ge(S["pro_bt"], b + 1)
                if not (isinstance(b, int) and b < 2):
                    act.wait_ge(S["bd_ready"], b * 8 - 8)
                nc.scalar.activation(btok[:, par, :, :].rearrange("p c n -> p (c n)"), bank[6][:, 0:2 * N], ACT.Copy
                                     ).then_inc(S["pro_bte"], 1)
                act.wait_ge(S["csp_r"], b + 1)
                nc.scalar.activation(csp[32:32 + N, par, :], cres[:, 0, :], ACT.Copy).then_inc(S["csp_mid"], 1)
                act.wait_ge(S["csp_r2"], b + 1)
                nc.scalar.activation(csp[64:64 + N, par, :], cres[:, 1, :], ACT.Copy).then_inc(S["csp_lo"], 1)

            def pro_c(b, par):
                act.wait_ge(S["m_ready"], b + 1)
                if not (isinstance(b, int) and b < 2):
                    act.wait_ge(S["yg_ready"], b - 1)
                nc.scalar.activation(mcur[:, par, :, :].rearrange("p h l -> p (h l)"), bank[7][:, :], ACT.Copy
                                     ).then_inc(S["m_evac"], 1)

            ymt = z2p[:, :, :].rearrange("p b l -> p (b l)")

            def down_a(b, par):
                act.wait_ge(S["dn_ready"], b + 3)
                act.sem_inc(S["act_past"], 1)
                nc.scalar.activation(ymt[:, bass.ds(b * L, L)], bank[6][:, 0:L], ACT.Identity,
                                     bias=colv[:, C_DN:C_DN + 1]).then_inc(S["dn_evac"], 1)

            def main(b, par, more):
                for s in range(16):
                    n2, h = s // 2, s % 2
                    act.wait_ge(S["ab_free"], b * 16 + s + 1)
                    act.sem_inc(S["act_past"], 1)
                    for r in range(2):
                        n = 2 * n2 + r
                        m = nc.scalar.activation(abar[:, s % 8, r, :], delta[:, h, bass.ds(b * L, L)], ACT.Exp,
                                                 scale=negs[:, h, n:n + 1])
                    m.then_inc(S["ab_ready"], 1)
                    if s == 13 and not (isinstance(b, int) and b == 0):
                        down_a(b - 1, 1 - par)
                    if more:
                        if s == 4:
                            pro_a(b + 1, 1 - par)
                        if s == 9:
                            pro_b(b + 1, 1 - par)
                        if s == 12:
                            pro_c(b + 1, 1 - par)

            negs = nega
            act.wait_ge(S["pool_done"], 1)
            act.sem_inc(S["act_done"], 2)
            pro_a(0, 0)
            pro_b(0, 0)
            pro_c(0, 0)
            act.wait_ge(S["dve_link"], dve_at["delta"])
            main(0, 0, True)
            with act.Fori(0, 3) as i:
                main(i * 2 + 1, 1, True)
                main(i * 2 + 2, 0, True)
            main(7, 1, False)
            down_a(7, 1)


            def gelus(e):
                if e > 1:
                    act.wait_ge(S["d_ready"], e - 1)
                for c in range(HC):
                    act.wait_ge(S["u_ready"], e * HC + c + 1)
                    k = C_B10 + e * HC + c
                    nc.scalar.activation(hbuf[:, e % 2, c, :], bank[c][:, :], ACT.Gelu, bias=colv[:, k:k + 1]
                                         ).then_inc(S["h_ready"], 1)

            def rows_out(e):
                act.wait_ge(S["xg_ps"], e + 1)
                if e > 1:
                    act.wait_ge(S["u_ready"], (e - 1) * HC)
                nc.scalar.activation(xgT[:, e % 2, :], bank[6][:, :], ACT.Copy).then_inc(S["xg_sb"], 1)

            expert_steps(((2, gelus), (1, rows_out)))
            for q in range(4):
                norm_root(2, q)
            for q in range(4):
                turned_out(q, 8)
            for q in range(4):
                act.wait_ge(S["pe_done"], 7 + q)
                m = nc.scalar.activation(vtok[:, 4 * q:4 * q + 4, :].rearrange("p t d -> p (t d)"), bank[q][:, :], ACT.Copy)
            m.then_inc(S["act_link"], 1)
            act.wait_ge(S["dve_link"], dve_at["smax1"])
            nc.scalar.activation(sc[:, :, :], sc[:, :, :], ACT.Exp).then_inc(S["sm_exp"], 1)

            def qk_out(b, par):
                act.wait_ge(S["qk_ps"], b + 1)
                if not (isinstance(b, int) and b < 2):
                    act.wait_ge(S["pm_free"], b * 8)
                act.sem_inc(S["act_past"], 1)
                nc.scalar.activation(kT[:, par, :], bank[4][:, L:2 * L], ACT.Copy)
                for h in range(HEADS):
                    nc.scalar.activation(qm[:, par, h, :], bank[4][:, 0:L], ACT.Copy, scale=colv[:, C_HEAD + h:C_HEAD + h + 1])
                v4 = vtok[:, bass.ds(b * 2, 2), :].rearrange("p t (h d) -> p t h d", h=HEADS)
                out4 = vmf[par].rearrange("p (t r) -> p t r", t=2)
                step = P + HD
                nc.scalar.activation(out4[:, :, 0:7 * step].rearrange("p t (h r) -> p t h r", r=step)[:, :, :, 0:HD],
                                     v4[:, :, 0:7, :], ACT.Copy)
                nc.scalar.activation(out4[:, :, 7 * step:7 * step + HD], v4[:, :, 7, :], ACT.Copy).then_inc(S["qk_sb"], 1)

            def ret_out(b, par):
                act.wait_ge(S["pm_free"], b * 8 + 16)
                act.sem_inc(S["act_past"], 1)
                nc.scalar.activation(retT[:, bass.ds(b * L, L)], bank[6 + par][:, 0:L], ACT.Copy).then_inc(S["r_free"], 1)

            act.wait_ge(S["vm_zero"], 1)
            qk_out(0, 0)
            qk_out(1, 1)
            with act.Fori(0, 3) as i:
                ret_out(i * 2, 0)
                qk_out(i * 2 + 2, 0)
                ret_out(i * 2 + 1, 1)
                qk_out(i * 2 + 3, 1)
            ret_out(6, 0)
            ret_out(7, 1)
            for q in range(4):
                act.wait_ge(S["gate_ps"], q + 1)
                nc.scalar.activation(oT[:, q * CH:(q + 1) * CH], bank[6 + q % 2][:, :], ACT.Silu).then_inc(S["gate_sb"], 1)

            def square(q):
                act.wait_ge(S["gc_ready"], q + 1)
                if q > 1:
                    act.wait_ge(S["gv_ready"], q - 1)
                nc.scalar.activation(hbuf[:, 1, q % 2, :], bank[q][:, :], ACT.Square).then_inc(S["gsq_ready"], 1)

            def root(q):
                act.wait_ge(S["gv_ready"], q + 1)
                if q > 1:
                    act.wait_ge(S["dve_done"], 11 + q)
                nc.scalar.activation(hbuf[:, 1, 2 + q % 2, :], bank[4 + q % 2][:, :], ACT.Sqrt, bias=colv[:, C_EPS:C_EPS + 1]
                                     ).then_inc(S["groot"], 1)

            square(0)
            square(1)
            for q in range(4):
                root(q)
                if q < 2:
                    square(q + 2)

            def x_out(k, u):
                act.wait_ge(S["xT_ps"], k + 1)
                if later(k, 2):
                    act.wait_ge(S["h_ps"], k - 1)
                nc.scalar.activation(xsT[:, u % 2, :], bank[4 + u % 2][:, 0:P], ACT.Copy).then_inc(S["xT_sb"], 1)

            def relu(k, u):
                act.wait_ge(S["h_ps"], k + 1)
                if later(k, 2):
                    act.wait_ge(S["hT_ps"], k - 1)
                nc.scalar.activation(hs[:, u % 2, :], bank[u % 2][:, :], ACT.Relu).then_inc(S["h_sb"], 1)

            slot_steps(act, ((0, x_out), (1, relu)))

        @block.gpsimd
        def _(pool):
            link = Chain(pool, S["pool_link"])
            for name, n in (("psd_free", 4), ("ab_free", 8), ("p_ready", 2), ("y_free", 1), ("p_free", 8), ("dn_evac", 1), ("dn_ready", 2),
                            ("pm_free", 8), ("w_r", 2), ("pm_ready", 4),
                            ("r_free", 2)):
                pool.sem_inc(S[name], n)
            link(nc.gpsimd.memset(z2p[:, :, 0:K - 1], 0.0))
            link(nc.gpsimd.memset(csp[:, :, :], 0.0))
            blank = bd[:, 0, 0, :, :].rearrange("p n t -> p (n t)")
            link(nc.gpsimd.memset(blank[:, 0:ROW1], 0.0))
            link(nc.gpsimd.memset(blank[:, P:P + 1].bitcast(I32), T))
            nc.gpsimd.dma_start(xd.rearrange("(p k) d -> p k d", p=P), blank[:, None, 0:ROW1].broadcast_to([P, SLOTT, ROW1])
                                ).then_inc(S["scattered"], 16)
            nc.gpsimd.dma_start(moe.rearrange("(p k) d -> p k d", p=P), blank[:, None, 0:P].broadcast_to([P, NT, P])
                                ).then_inc(S["moe_zero"], 16)
            pool.wait_ge(S["ld_w"], 13 * 16)
            for k in range(K):
                m = nc.gpsimd.tensor_tensor(wconv[:, k, :], wup1, convb[:, k, :], ALU.mult)
            m.then_inc(S["wconv_ready"], 1)
            pool.wait_ge(S["norm_ready"], 4)
            nc.gpsimd.tensor_tensor(acc[:, :, :], acc[:, :, :], xn[:, :, :], ALU.add).then_inc(S["sum_ready"], 1)
            pool.wait_ge(S["dve_link"], dve_at["inva"])
            pool.sem_inc(S["pool_done"], 1)

            pool.wait_ge(S["xm_ready"], 1)
            pool.wait_ge(S["scattered"], 16)
            pool.wait_ge(S["moe_zero"], 16)

            def pro_x(b, par):
                if not (isinstance(b, int) and b < 2):
                    pool.wait_ge(S["pro_x"], b - 1)
                pool.sem_inc(S["pool_past"], 1)
                nc.gpsimd.tensor_copy(xcur[:, par, :, :], xm[:, :, bass.ds(b * L, L)]).then_inc(S["xcur_ready"], 1)

            def pro_c(b, par):
                pool.wait_ge(S["csp_hi"], b + 1)
                if not (isinstance(b, int) and b == 0):
                    pool.wait_ge(S["csp_lo"], b)
                nc.gpsimd.tensor_tensor(cres[:, 0, :], ccur[:, par, :], csp[0:N, par, :], ALU.subtract).then_inc(S["csp_r"], 1)
                if not (isinstance(b, int) and b == 0):
                    pool.wait_ge(S["m_ready"], b)
                nc.gpsimd.tensor_tensor(cb[:, par, :], ccur[:, par, :], bcur[:, par, :], ALU.mult).then_inc(S["cb_ready"], 1)

            def pro_m(b, par):
                pool.wait_ge(S["csp_mid"], b + 1)
                pool.sem_inc(S["pool_past"], 1)
                nc.gpsimd.tensor_copy(cmid[:, :], cres[:, 0, :]).then_inc(S["pool_link"], 1)
                pool.wait_ge(S["pool_link"], b + link.n + 1)
                nc.gpsimd.tensor_tensor(cres[:, 1, :], cres[:, 0, :], cmid[:, :], ALU.subtract).then_inc(S["csp_r2"], 1)

            def pro_bd(b, par, n2):
                if n2 == 0:
                    pool.wait_ge(S["pro_bte"], b + 1)
                    if not (isinstance(b, int) and b < 2):
                        pool.wait_ge(S["dw_ready"], b * 16 - 16)
                n = slice(2 * n2, 2 * n2 + 2)
                for c in range(2):
                    m = nc.gpsimd.tensor_tensor(bd[:, par, c, n, :], bid[:, None, :].broadcast_to([P, 2, P + 1]),
                                                btok[:, par, c, n, None].broadcast_to([P, 2, P + 1]), ALU.mult)
                m.then_inc(S["bd_ready"], 1)

            def main(b, par, more):
                for s in range(16):
                    pool.wait_ge(S["p_ready"], b * 16 + s + 3)
                    nc.gpsimd.tensor_tensor(zb[:, s % 8, 0, :], zb[:, s % 8, 0, :], zb[:, s % 8, 1, :], ALU.add
                                            ).then_inc(S["q_ready"], 1)
                    if more:
                        if s == 3:
                            pro_c(b + 1, 1 - par)
                        if s == 5:
                            pro_m(b + 1, 1 - par)
                        if s == 8 and not (isinstance(b, int) and b == 6):
                            pro_x(b + 2, par)
                        if s >= 7 and s % 2:
                            pro_bd(b + 1, 1 - par, (s - 7) // 2)
                    if s in (1, 3, 5):
                        pro_bd(b, par, 5 + s // 2)

            pro_x(0, 0)
            pro_x(1, 1)
            pro_c(0, 0)
            pro_m(0, 0)
            for n2 in range(5):
                pro_bd(0, 0, n2)
            main(0, 0, True)
            with pool.Fori(0, 2) as i:
                main(i * 2 + 1, 1, True)
                main(i * 2 + 2, 0, True)
            main(5, 1, True)
            main(6, 0, True)
            main(7, 1, False)

            pool.wait_ge(S["rows_g"], 16)

            def gather(e):
                pool.wait_ge(S["id_ready"], e + 1)
                if e > 3:
                    pool.wait_ge(S["ye_ready"], e - 3)
                for q in range(4):
                    nc.gpsimd.indirect_dma_start(
                        out=xg[:, e % 4, q, :], out_offset=None, in_=rows,
                        in_offset=bass.IndirectOffsetOnAxis(ap=idx[:, 4 * e + q:4 * e + q + 1], axis=0)
                        ).then_inc(S[f"xg_in{e % 4}"], 16)

            def add(e):
                pool.wait_ge(S["ye_ready"], e + 1)
                if e:
                    pool.wait_ge(S["added"], 64 * e)
                for q in range(4):
                    nc.gpsimd.indirect_dma_start(
                        out=moe, out_offset=bass.IndirectOffsetOnAxis(ap=idx[:, 4 * e + q:4 * e + q + 1], axis=0),
                        in_=ye[:, e % 2, q, :], in_offset=None, compute_op=ALU.add).then_inc(S["added"], 16)

            expert_steps(((0, gather), (3, add)))
            pool.wait_ge(S["added"], 64 * E0)
            for v in vmf:
                m = nc.gpsimd.memset(v, 0.0)
            m.then_inc(S["vm_zero"], 1)
            pool.wait_ge(S["ld_b"], 16)
            pool.wait_ge(S["dve_done"], 11)
            link.n = link.n + NB
            link(nc.gpsimd.tensor_copy(bhi, bias1))
            link(nc.gpsimd.tensor_tensor(bres, bias1, bhi, ALU.subtract))
            link(nc.gpsimd.tensor_copy(bmid, bres))
            link(nc.gpsimd.tensor_tensor(bres, bres, bmid, ALU.subtract))
            link(nc.gpsimd.tensor_copy(blo, bres))
            pool.sem_inc(S["b_split"], 1)
            pool.wait_ge(S["scattered"], 16)
            for w in range(2):
                pool.wait_ge(S["scattered"], (1 + w * NT) * 16)
                link(nc.gpsimd.tensor_copy(xnw[:, :, P + 1], mx8[:, :, w]))
                for t in range(NT):
                    nc.gpsimd.indirect_dma_start(
                        out=xd, out_offset=bass.IndirectOffsetOnAxis(ap=slot[:, w, t:t + 1], axis=0),
                        in_=xnw[:, t, :], in_offset=None).then_inc(S["scattered"], 16)

            def add1(k, u):
                pool.wait_ge(S["y_sb"], k + 1)
                if later(k, 1):
                    pool.wait_ge(S["added1"], k * 16)
                pool.sem_inc(S["pool_past"], 1)
                nc.gpsimd.indirect_dma_start(
                    out=out, out_offset=bass.IndirectOffsetOnAxis(ap=xs[:, u, P:P + 1].bitcast(I32), axis=0),
                    in_=ys[:, u % 4, :], in_offset=None, compute_op=ALU.add, bounds_check=T - 1, oob_is_err=False
                    ).then_inc(S["added1"], 16)

            pool.wait_ge(S["sum_out"], 64)
            slot_steps(pool, ((4, add1),))


def kernel(**inputs):
    import numpy as np
    import concourse.bacc as bacc
    from concourse.bass_utils import run_bass_kernel_spmd as run

    a = {k: np.asarray(v) for k, v in inputs.items()}
    f = np.float32
    r = np.arange(P)
    ident = np.eye(P, dtype=f)
    bid = np.zeros((P, P + 1), f)
    bid[r, r] = 1
    bid[r, r + 1] = -1
    sel = np.zeros((P, N, P), f)
    for part in range(3):
        sel[32 * part + np.arange(N), np.arange(N), :] = 1
    cf = np.concatenate([ident, bid, np.ones((P, P), f), np.triu(np.ones((P, P), f), 1),
                         np.tile(np.arange(P, dtype=f), (P, 1)), np.arange(P, dtype=f)[:, None], sel.reshape(P, -1)], axis=1)
    gam = (1.0 - np.exp(np.linspace(np.log(1.0 / 512.0), np.log(1.0 / 32.0), HEADS))).astype(f)
    diff = np.arange(L)[None, :] - np.arange(L)[:, None]
    dec = np.where(diff >= 0, gam[:, None, None] ** np.where(diff >= 0, diff, 0).astype(f), 0).astype(f)
    head = np.repeat(np.eye(HEADS, dtype=f), HD, axis=0)
    average = (head @ head.T / HD).astype(f)
    mask = np.concatenate([np.concatenate([dec[:, 0:P, :], dec[:, P:L, P:L]], axis=2).transpose(1, 0, 2).reshape(P, -1),
                           ident - average, average], axis=1)
    unit = np.where(np.arange(ROUNDS) < 15, 1 << np.maximum(28 - 2 * np.arange(ROUNDS), 0), 0)

    def rounds(three):
        return np.tile((unit[:, None] * np.array(three))[None, :, :, None], (P, 1, 1, E0))

    z = lambda v, n: np.ascontiguousarray(v.reshape(n, P).T)
    col = np.zeros((P, 108 + HEADS), f)
    col[:, 0] = a["L0_attn_ln_g"]
    col[:, 1] = a["L0_attn_ln_b"]
    col[:, 2:4] = z(a["L0_attn_conv_b"], 2)
    col[:, 4:6] = z(a["L0_attn_b_ll"][0:DI], 2)
    col[0:N, 6] = a["L0_attn_b_ll"][DI:DI + N]
    col[0:N, 7] = a["L0_attn_b_ll"][DI + N:]
    col[:, 8] = a["L0_attn_b_down"]
    col[:, 9:41] = z(a["L0_ffn_b1"], E0 * HC)
    col[:, 41:105] = z(a["L1_ffn_b1"], E1 * HC)
    col[:, 105] = a["L1_attn_gn_w"]
    col[:, 106] = a["L1_attn_gn_b"]
    col[:, 107] = EPS
    col[:, 108:] = head

    def blocks(w):
        o = np.zeros((P, P), f)
        for h in range(HEADS):
            o[h * HD:(h + 1) * HD, h * HD:(h + 1) * HD] = w[h]
        return o

    down = lambda w, e: w.reshape(e, HC, P, P).transpose(0, 2, 1, 3).reshape(e, P, HC * P)
    arrays = dict(
        x=a["L0_attn_X"].reshape(T, P), cf=cf, mask_d=mask, bits_i=rounds((1, 2, 3)).astype(np.int32), bits_f=rounds((1, 3, 1)).astype(f),
        cols=col, conv_t=a["L0_attn_conv_w"].reshape(DI, K).T,
        w_up1=a["L0_attn_W_up1"].T, w_up2=a["L0_attn_W_up2"].T, w_ll=a["L0_attn_W_ll"].T, a_log=a["L0_attn_A_log"],
        a_log_t=a["L0_attn_A_log"].T, w_down=a["L0_attn_W_down"].T, wr0=a["L0_ffn_Wr"], w1_0=a["L0_ffn_W1"],
        w2_0=down(a["L0_ffn_W2"], E0), b2_0=a["L0_ffn_b2"], wq=blocks(a["L1_attn_Wq"]), wk=blocks(a["L1_attn_Wk"]),
        wv=blocks(a["L1_attn_Wv"]), wg=a["L1_attn_W1"], wo=a["L1_attn_W2"], wr1=a["L1_ffn_Wr"], br1=a["L1_ffn_br"].reshape(1, E1),
        w1_1=a["L1_ffn_W1"], w2_1=down(a["L1_ffn_W2"], E1),
        b_1=np.concatenate([a["L1_ffn_b1"], a["L1_ffn_b2"]], axis=1))
    arrays = {k: np.ascontiguousarray(v) for k, v in arrays.items()}
    nc = bacc.Bacc("TRN2", target_bir_lowering=False, num_devices=1)
    ins = {k: nc.dram_tensor(f"in_{k}", v.shape, mybir.dt.from_np(v.dtype), kind="ExternalInput").ap()
           for k, v in arrays.items()}
    out = nc.dram_tensor("out_x", [T, P], F32, kind="ExternalOutput").ap()
    layer_pair(nc, out=out, **{k: v for k, v in ins.items() if k != "rows"})
    res = run(nc, [{f"in_{k}": v for k, v in arrays.items()}], core_ids=[0])
    return res.results[0]["out_x"].reshape(NB, L, P)
```

```python
from contextlib import ExitStack

import concourse.bass as bass
from concourse import mybir

F32 = mybir.dt.float32
BF16 = mybir.dt.bfloat16
I32 = mybir.dt.int32
U32 = mybir.dt.uint32
ALU = mybir.AluOpType
ACT = mybir.ActivationFunctionType
AX = mybir.AxisListType

P = 128
NB, L = 8, 256
T = NB * L
NT = T // P
CH = 512
NC = T // CH
DI, N, K = 256, 16, 4
NH2 = DI // P
LP = L + K
HID = 512
HC = HID // P
E0, KTOP = 8, (T * 2) // 8
E1 = 16
SLOTT = 48
SLOTS = SLOTT * P
YLAG = 6
LAG = 3
HEADS, HD = 8, 16
SC = 384
EPS = 1e-5
ROW1 = P + 2
ROW = P + E0
PB = HID + P
ROUNDS = 16


class Chain:

    def __init__(self, eng, sem):
        self.eng, self.sem, self.n, self.calls = eng, sem, 0, 0

    def __call__(self, ins):
        ins.then_inc(self.sem, 1)
        self.n = self.n + 1
        self.calls += 1
        self.eng.wait_ge(self.sem, self.n)

    def more(self, ins):
        ins.then_inc(self.sem, 1)
        self.n = self.n + 1
        self.calls += 1

    def loop(self, i, per):
        self.start, self.per, self.calls = self.n, per, 0
        self.n = self.start + i * per

    def end(self, count):
        assert self.calls == self.per, self.calls
        self.n = self.start + count * self.per


def layer_pair(nc, x, cf, mask_d, bits_i, bits_f, cols, conv_t, w_up1, w_up2, w_ll, a_log, a_log_t, w_down,
               wr0, w1_0, w2_0, b2_0, wq, wk, wv, wg, wo, wr1, br1, w1_1, w2_1, b_1, out):
    ctx = ExitStack()
    with ctx:
        def sb(name, shape, dt=F32):
            return ctx.enter_context(nc.sbuf_tensor(name, shape, dt))

        def sem(name):
            return ctx.enter_context(nc.semaphore(name))

        bank = [ctx.enter_context(nc.psum_tensor(f"bank{i}", [P, 512], F32)) for i in range(8)]

        acc = sb("acc", [P, NT, P])
        xnw = sb("xnw", [P, NT, ROW1])
        xn = xnw[:, :, 0:P]
        xnT = sb("xnT", [P, T])
        hbuf = sb("hbuf", [P, 2, HC, CH])
        z2p = sb("z2p", [P, NB, LP])
        w1b = sb("w1b", [P, 2, HID])
        w2b = sb("w2b", [P, 2, HC, P])
        xm = sb("xm", [P, NH2, T])
        gate = sb("gate", [P, NH2, T])
        delta = sb("delta", [P, NH2, T])
        zbuf = sb("zbuf", [P, 4, 2, L])
        arena = sb("arena", [P, E1 * HID])
        abar = arena[:, 0:4096].rearrange("p (a b l) -> p a b l", a=8, b=2)
        bd = sb("bd", [P, 2, 2, N, P + 1])
        zb = arena[:, 4096:8192].rearrange("p (a b l) -> p a b l", a=8, b=2)
        hb = hbuf[:, :, :, :].rearrange("p a c t -> p (a c t)")
        xnf = xnw[:, :, :].rearrange("p t d -> p (t d)")
        xcur = hb[:, 0:1024].rearrange("p (a h l) -> p a h l", a=2, h=NH2)
        xT = xnf[:, 0:1024].rearrange("p (a c d) -> p a c d", a=2, c=2)
        bcur = sb("bcur", [N, 2, L])
        ccur = sb("ccur", [N, 2, L])
        cres = sb("cres", [N, 2, L])
        cb = sb("cb", [N, 2, L])
        cmid = sb("cmid", [N, L], BF16)
        csp = sb("csp", [P, 2, L], BF16)
        btok = sb("btok", [P, 2, 2, N])
        mcur = hb[:, 1024:2048].rearrange("p (a h l) -> p a h l", a=2, h=NH2)
        yg = xnf[:, 1024:2048].rearrange("p (a h l) -> p a h l", a=2, h=NH2)
        ident = sb("ident", [P, P])
        cfs = sb("cfs", [P, 129 + 128 + 128 + 128 + 1])
        iota_p = cfs[:, 385:513]
        iota_k = iota_p[:, 0:SLOTT]
        own_p = cfs[:, 513:514]
        bid = cfs[:, 0:129]
        ones_f = cfs[:, 129:257]
        iota_e = iota_p[:, 0:E1]
        onesb = sb("onesb", [P, P], BF16)
        ltri = sb("ltri", [P, P], BF16)
        selb = sb("selb", [P, N, P], BF16)
        NCOL = cols.shape[1]
        colv = sb("colv", [P, NCOL])
        nega = sb("nega", [P, NH2, N])
        inva = sb("inva", [P, NH2, N])
        invat = sb("invat", [N, DI])
        convb = delta[:, 1, 0:K * DI].rearrange("p (k e) -> p k e", k=K)
        wup1 = delta[:, 0, K * DI:(K + 1) * DI]
        wconv = delta[:, 0, 0:K * DI].rearrange("p (k e) -> p k e", k=K)
        wup2 = delta[:, 0, (K + 1) * DI:(K + 2) * DI]
        wll = sb("wll", [P, NH2, DI + 2 * N])
        wdn = sb("wdn", [P, NH2, P])
        wr0s = sb("wr0s", [P, E0])
        bn = sb("bn", [P, NT, 12])
        sc = sb("sc", [P, NT, E1])
        gts = sb("gts", [P, NT, E0])
        sm = sb("sm", [P, 4, NT])
        early = bd[:, 1, :, :, :].rearrange("p c n t -> p (c n t)")
        bis = early[:, 0:3 * ROUNDS * E0].bitcast(I32).rearrange("p (r c e) -> p r c e", c=3, e=E0)
        bfs = early[:, 512:512 + 3 * ROUNDS * E0].rearrange("p (r c e) -> p r c e", c=3, e=E0)
        cmp3 = early[:, 1024:1024 + 3 * P // 2].bitcast(BF16).rearrange("p (c t e) -> p c t e", c=3, e=E0)
        eqb = early[:, 1280:1280 + P // 2].bitcast(BF16).rearrange("p (t e) -> p t e", e=E0)
        cmpb = cmp3[:, 0, :, :]
        tmp8 = xT[:, :, :, :].rearrange("p a b l -> p (a b l)")[:, 0:3 * NT * E0].rearrange("p (a t e) -> p a t e", a=3, e=E0)
        thr = sb("thr", [P, E0], I32)
        cand = sb("cand", [P, 3, E0], I32)
        inc = sb("inc", [P, 3, E0], I32)
        cnt = sb("cnt", [P, 3, E0])
        need = sb("need", [P, E0])
        mx8 = sb("mx8", [P, NT, 8])
        ix8 = sb("ix8", [P, NT, 8], U32)
        ixf = sb("ixf", [P, 2, NT])
        choice, posn, quot = (early[:, 1536 + 128 * k:1664 + 128 * k].rearrange("p (t e) -> p t e", e=E0) for k in range(3))
        four = early[:, 2048:2560].rearrange("p (m q) -> p m q", q=4)
        posi, quoi, modi = (early[:, 2560 + 128 * k:2688 + 128 * k].bitcast(I32) for k in range(3))
        chb = cmp3[:, 1, :, :]
        zf = zbuf[:, :, :, :].rearrange("p a b l -> p (a b l)")
        place = zf[:, 0:P].rearrange("p (t e) -> p t e", e=E0)
        tokp = zf[:, 128:640].bitcast(BF16).rearrange("p (t e q c) -> p t e q c", t=NT, e=E0, q=4)
        b2b = zf[:, 640:640 + 2 * P].rearrange("p (a d) -> p a d", a=2)
        idx = zf[:, 896:896 + 4 * E0].bitcast(I32)
        idxf = zf[:, 896 + 4 * E0:900 + 4 * E0]
        exps = [zf[:, 1024 + CH * c:1024 + CH * (c + 1)] for c in (0, 1)] + [hb[:, CH * c:CH * (c + 1)] for c in range(2, 8)]
        logs, rests = ([arena[:, o + CH * c:o + CH * (c + 1)] for c in range(8)] for o in (4096, 0))
        xmf = xm[:, :, :].rearrange("p h t -> p (h t)")
        xg = xmf[:, 0:4 * 4 * ROW].rearrange("p (a q r) -> p a q r", a=4, q=4)
        xgT = xmf[:, 4096 - 1024:4096].rearrange("p (a s) -> p a s", a=2)
        hot = gate[:, 0, :].bitcast(BF16).rearrange("p (a t r) -> p a t r", a=2, t=NT)
        ye = gate[:, 1, 0:1024].rearrange("p (a q d) -> p a q d", a=2, q=4)
        rows = nc.dram_tensor("token_rows", [T, ROW], F32, kind="Internal").ap()
        moe = nc.dram_tensor("expert_sums", [T, P], F32, kind="Internal").ap()
        latef = delta[:, :, :].rearrange("p h t -> p (h t)")
        maskd = latef[:, 0:HEADS * SC].rearrange("p (h c) -> p h c", h=HEADS)
        centre = latef[:, HEADS * SC:HEADS * SC + P]
        average = latef[:, HEADS * SC + P:HEADS * SC + 2 * P]
        zs = z2p[:, :, :].rearrange("p b l -> p (b l)")
        wqs, wks, wvs, wgs, wos = (zs[:, k * P:(k + 1) * P] for k in (0, 1, 2, 4, 5))
        wr1s = zs[:, 3 * P:3 * P + E1]
        wvr = zs[:, 2 * P:3 * P + E1]
        br1s = zs[:, 6 * P:6 * P + E1]
        w1r = bd[:, :, :, :, :].rearrange("p a c n t -> p (a c n t)")[:, 0:E1 * HID].rearrange("p (e h) -> p e h", e=E1)
        w2r = arena[:, :].rearrange("p (e c d) -> p e c d", e=E1, c=HC)
        w1f = w1b[:, :, :].rearrange("p a h -> p (a h)")
        w2f = w2b[:, :, :, :].rearrange("p a c d -> p (a c d)")
        xs = xnT[:, 0:8 * ROW1].rearrange("p (k r) -> p k r", k=8)
        ys = w1f[:, 4 * P:8 * P].rearrange("p (k d) -> p k d", k=4)
        xsT = sb("xsT", [P, 2, P])
        hs = hbuf[:, 0, :, :].rearrange("p (a b) t -> p a (b t)", a=2)[:, :, 0:HID]
        hT = hbuf[:, 1, :, :].rearrange("p (a b) t -> p a (b t)", a=2)[:, :, 0:HID]
        bias1 = w2f[0:E1, 0:PB]
        bhi = w2f[0:E1, PB:PB + PB // 2].bitcast(BF16)
        bres = latef[0:E1, HEADS * SC + 2 * P:HEADS * SC + 2 * P + PB]
        bmid = bcur[:, :, :].rearrange("n a l -> n (a l)")[:, 0:PB // 2].bitcast(BF16)
        blo = ccur[:, :, :].rearrange("n a l -> n (a l)")[:, 0:PB // 2].bitcast(BF16)
        b1p = delta[0:3, :, :].rearrange("p h t -> p (h t)").bitcast(BF16).rearrange("p (e h) -> p e h", e=E1)
        b2p = zbuf[0:3, 0:2, :, :].rearrange("p a b l -> p (a b l)").bitcast(BF16).rearrange("p (e d) -> p e d", e=E1)
        inc8 = sb("inc8", [P, 1, E1], I32)
        ekf = sb("ekf", [P, SLOTT])
        mkb = sb("mkb", [P, NT, E1], BF16)
        slot = sb("slot", [P, 2, NT], I32)
        eidx = sb("eidx", [P, SLOTT], I32)
        esm = sb("esm", [P, 5, E1])
        xd = nc.dram_tensor("slots_in", [SLOTS, ROW1], F32, kind="Internal").ap()
        kT = w1f[:, 0:2 * L].rearrange("p (a l) -> p a l", a=2)
        qm = xm[:, :, :].rearrange("p a (h l) -> p a h l", h=HEADS)
        vmf = [zf, gate[:, 0, :]]
        vm = [v.rearrange("p (t h d) -> p t h d", t=2, h=HEADS) for v in vmf]
        pbuf = hbuf[:, 1, :, 0:SC]
        vtok = gate[:, 1, :].rearrange("p (t d) -> p t d", t=NT)
        oT = gate[:, 1, :]
        retT = hbuf[:, 0, :, :].rearrange("p c t -> p (c t)")

        C_LNG, C_LNB, C_CB, C_BD, C_BB, C_BC, C_DN, C_B10, C_GW, C_GB, C_EPS, C_HEAD = 0, 1, 2, 4, 6, 7, 8, 9, 41, 42, 43, 44

        names = ("act_past pe_past pool_past "
                 "ld_x0 ld_x1 ld_x2 ld_x3 ld_i ld_r ld_s sum_ready norm_ready norm_root shift_ready norm2_ready ld_c ld_w ld_late pe_done dve_done wconv_ready act_link dve_link pool_link "
                 "ps_ready ps_free psd_ready psd_free ab_ready ab_free dw_ready cbc_ready p_ready q_ready p_free "
                 "y_free xcur_ready rest_ready w_less_1 sp_ps sp_free pro_x pro_xe pro_bt pro_bte bd_ready csp_hi csp_r csp_mid csp_r2 csp_lo "
                 "cb_ready m_ready m_evac yg_ready dn_ready dn_evac "
                 "u_ready h_ready d_ready w1_in0 w1_in1 w2_in0 w2_in1 layer0 rows_x gates_ready rows_g moe_zero hot_ready cp_ready id_ready "
                 "xg_in0 xg_in1 xg_in2 xg_in3 xg_ps xg_sb ye_ready added moe_in0 moe_in1 moe_in2 moe_in3 "
                 "ee abs_r exp_r sm_exp ln_r cnt_in cnt_out "
                 "ld_w1 ld_b ld_bp b_split scattered xs_in0 xs_in1 xs_in2 xs_in3 xs_in4 xs_in5 xs_in6 xs_in7 xT_ps xT_sb h_ps h_sb hT_ps hT_sb y_ps y_sb "
                 "sum_out added1 "
                 "qk_ps qk_sb s_ready pm_ready pm_free r_free vm_zero gc_ready gsq_ready gv_ready groot gate_ps gate_sb").split()
        S = {n: sem(n) for n in names}

        block = ctx.enter_context(nc.Block())

        def expert_steps(stages):
            for s in range(E0 + 3):
                for lag, f in stages:
                    if 0 <= s - lag < E0:
                        f(s - lag)

        Z2_BANK = (4, 5, 6, 1)

        def slot_steps(eng, stages):
            def step(t, u):
                for lag, f in stages:
                    k = t - lag
                    if not isinstance(k, int) or 0 <= k < SLOTT:
                        f(k, (u - lag) % 8)

            for t in range(8):
                step(t, t)
            with eng.Fori(0, SLOTT // 8 - 1) as i:
                for u in range(8):
                    step(i * 8 + (8 + u), u)
            for t in range(SLOTT, SLOTT + 5):
                step(t, t % 8)

        def later(k, n):
            return not isinstance(k, int) or k >= n

        dve_at = {}

        @block.vector
        def _(dve):
            link = Chain(dve, S["dve_link"])
            V = nc.vector

            def bc(ap, n):
                return ap[:, :, None].broadcast_to([P, NT, n])

            def norm_stats(source, nth, q):
                for t in range(4 * q, 4 * q + 4):
                    link.more(V.bn_stats(bn[:, t, 0:6], source[:, t, :]))
                dve.wait_ge(S["dve_link"], link.n)
                for t in range(4 * q, 4 * q + 4):
                    link.more(V.bn_aggr(bn[:, t, 6:8], bn[:, t, 0:6]))
                dve.wait_ge(S["dve_link"], link.n)
                link(V.tensor_scalar(bn[:, 4 * q:4 * q + 4, 8], bn[:, 4 * q:4 * q + 4, 7], EPS, None, ALU.add))
                dve_at[nth, q] = link.n

            def normalize(dst, source, nth, q):
                dve.wait_ge(S["norm_root"], 4 * nth + q + 1)
                link(V.reciprocal(bn[:, 4 * q:4 * q + 4, 10], bn[:, 4 * q:4 * q + 4, 9]))
                for t in range(4 * q, 4 * q + 4):
                    link.more(V.tensor_scalar(dst[:, t, :], source[:, t, :], bn[:, t, 6:7], bn[:, t, 10:11],
                                              ALU.subtract, ALU.mult))
                dve.wait_ge(S["dve_link"], link.n)
                dve.sem_inc(S["norm_ready"], 1)

            def normalize_by(q):
                dve.wait_ge(S["norm_root"], 4 + q + 1)
                t = slice(4 * q, 4 * q + 4)
                link(V.reciprocal(bn[:, t, 10], bn[:, t, 9]))
                V.scalar_tensor_tensor(out=bn[:, t, 11], in0=bn[:, t, 6], scalar=-1.0, in1=bn[:, t, 10],
                                       op0=ALU.mult, op1=ALU.mult).then_inc(S["shift_ready"], 1)

            z2 = hbuf[:, 0, :, :].rearrange("p c (q d) -> p (c q) d", d=P)
            norms = {0: (xn, acc), 1: (z2, xn)}
            for nth, q, part in ((0, 0, 0), (0, 1, 0), (0, 0, 1), (0, 2, 0), (0, 1, 1), (0, 3, 0), (0, 2, 1), (1, 0, 0),
                                 (0, 3, 1), (1, 1, 0), (1, 0, 1), (1, 2, 0), (1, 1, 1), (1, 3, 0), (1, 2, 1), (1, 3, 1)):
                dst, source = norms[nth]
                if part and nth:
                    normalize_by(q)
                elif part:
                    normalize(dst, source, nth, q)
                else:
                    if nth == 0:
                        dve.wait_ge(S[f"ld_x{q}"], 16)
                    norm_stats(source, nth, q)
            dve.sem_inc(S["dve_done"], 2)
            def softmax_less_max(E, ready, count, ps, nth):
                s = sc[:, :, 0:E]
                dve.wait_ge(S[ready], count)
                link(V.tensor_reduce(sm[:, 0, :], ps, AX.X, ALU.max))
                link(V.tensor_tensor(s, ps, bc(sm[:, 0, :], E), ALU.subtract))
                dve_at[nth] = link.n

            def softmax_scale(E, nth):
                s = sc[:, :, 0:E]
                dve.wait_ge(S["sm_exp"], nth)
                link(V.tensor_reduce(sm[:, 1, :], s, AX.X, ALU.add))
                link(V.reciprocal(sm[:, 2, :], sm[:, 1, :]))
                link(V.tensor_tensor(s, s, bc(sm[:, 2, :], E), ALU.mult))

            softmax_less_max(E0, "pe_done", 1, bank[7][:, 0:P].rearrange("p (t e) -> p t e", t=NT), "smax0")
            softmax_scale(E0, 1)
            s0 = sc[:, :, 0:E0]

            def per_e(ap):
                return ap[:, None, :].broadcast_to([P, NT, E0])

            tot = bank[5][:, 0:P].rearrange("p (t e) -> p t e", t=NT)
            tot3 = bank[5][:, 0:3 * P].rearrange("p (c t e) -> p c t e", c=3, t=NT)
            link(V.memset(thr[:, :], 0))
            dve.wait_ge(S["ld_s"], 32)
            with dve.Fori(0, ROUNDS // 4) as j:
                link.loop(j, 28)
                for r in range(4):
                    i = j * 4 + r
                    link(V.tensor_tensor(cand[:, :, :], thr[:, None, :].broadcast_to([P, 3, E0]),
                                         bis[:, bass.ds(i, 1), :, :].rearrange("p a c e -> p (a c) e"), ALU.bitwise_or))
                    link(V.tensor_tensor(cmp3[:, :, :, :], s0[:, None, :, :].broadcast_to([P, 3, NT, E0]),
                                         cand[:, :, None, :].bitcast(F32).broadcast_to([P, 3, NT, E0]), ALU.is_ge))
                    dve.sem_inc(S["cnt_in"], 1)
                    dve.wait_ge(S["cnt_out"], i + 1)
                    link(V.tensor_reduce(cnt[:, :, :], tot3.rearrange("p c t e -> p c e t"), AX.X, ALU.add))
                    link(V.scalar_tensor_tensor(out=inc[:, :, :], in0=cnt[:, :, :], scalar=float(KTOP),
                                                in1=bfs[:, bass.ds(i, 1), :, :].rearrange("p a c e -> p (a c) e"),
                                                op0=ALU.is_ge, op1=ALU.mult))
                    for c in range(3):
                        link(V.tensor_tensor(thr[:, :], thr[:, :], inc[:, c, :], ALU.bitwise_xor))
            link.end(ROUNDS // 4)
            thf = thr[:, :].bitcast(F32)
            link(V.tensor_tensor(cmpb, s0, per_e(thf), ALU.is_gt))
            dve.sem_inc(S["cnt_in"], 1)
            link(V.tensor_tensor(eqb[:, :, :], s0, per_e(thf), ALU.is_equal))
            dve.wait_ge(S["cnt_out"], ROUNDS + 1)
            link(V.tensor_reduce(cnt[:, 0, :], tot.rearrange("p t e -> p e t"), AX.X, ALU.add))
            dve.sem_inc(S["cnt_in"], 1)
            link(V.tensor_scalar(need[:, :], cnt[:, 0, :], -1.0, float(KTOP), ALU.mult, ALU.add))
            dve.wait_ge(S["cnt_out"], ROUNDS + 2)
            def part(c):
                return delta[:, c % 2, c // 2 * CH:(c // 2 + 1) * CH]

            def positive(c):
                dve.wait_ge(S["abs_r"], c + 1)
                V.tensor_scalar(part(c), bank[c % 4][:, :], colv[:, C_BD + c % 2:C_BD + c % 2 + 1], 0.0, ALU.add, ALU.max
                                ).then_inc(S["sp_free"], 1)

            def rounded(c):
                dve.wait_ge(S["exp_r"], c + 1)
                V.tensor_scalar(rests[c], exps[c], 1.0, -1.0, ALU.add, ALU.add).then_inc(S["w_less_1"], 1)

            dve.wait_ge(S["rows_x"], 16)
            dve.wait_ge(S["sum_ready"], 1)

            def running(out_, total, within):
                link(V.memset(tmp8[:, 0, 0:1, :], 0.0))
                link(V.tensor_copy(tmp8[:, 0, 1:NT, :], total[:, 0:NT - 1, :]))
                cur = 0
                for d in (1, 2, 4, 8):
                    V.tensor_copy(tmp8[:, 1 - cur, 0:d, :], tmp8[:, cur, 0:d, :]).then_inc(S["dve_link"], 1)
                    link.n += 1
                    link(V.tensor_tensor(tmp8[:, 1 - cur, d:NT, :], tmp8[:, cur, d:NT, :], tmp8[:, cur, 0:NT - d, :], ALU.add))
                    cur = 1 - cur
                link(V.tensor_tensor(out_, tmp8[:, cur, :, :], within, ALU.add))

            own = bank[6][:, 0:P].rearrange("p (t e) -> p t e", t=NT)
            rank = tmp8[:, 2, :, :]
            running(rank, tot, own)
            link(V.tensor_tensor(rank, rank, per_e(need[:, :]), ALU.is_lt))
            link(V.tensor_tensor(rank, rank, eqb[:, :, :], ALU.mult))
            link(V.tensor_tensor(choice, rank, cmpb, ALU.add))
            link(V.tensor_copy(chb, choice))
            dve.sem_inc(S["cnt_in"], 1)
            link(V.tensor_tensor(gts[:, :, :], choice, s0, ALU.mult))
            dve.sem_inc(S["gates_ready"], 1)
            for c in range(4):
                positive(c)
                if c:
                    rounded(c - 1)
            dve.wait_ge(S["cnt_out"], ROUNDS + 3)
            running(posn, tot, own)
            dve_at["search"] = link.n
            for c in range(4, 8):
                positive(c)
                rounded(c - 1)
            rounded(7)
            flat = "p t e -> p (t e)"
            link(V.tensor_copy(posi, posn.rearrange(flat)))
            link(V.tensor_scalar(quoi, posi, 7, None, ALU.logical_shift_right))
            link(V.tensor_scalar(modi, posi, P - 1, None, ALU.bitwise_and))
            link(V.tensor_copy(quot.rearrange(flat), quoi))
            link(V.tensor_copy(place.rearrange(flat), modi))
            link(V.tensor_tensor(four, iota_p[:, None, 0:4].broadcast_to([P, P, 4]),
                                 quot.rearrange(flat)[:, :, None].broadcast_to([P, P, 4]), ALU.is_equal))
            link(V.tensor_tensor(four, four, choice.rearrange(flat)[:, :, None].broadcast_to([P, P, 4]), ALU.mult))
            link(V.scalar_tensor_tensor(out=tokp[:, :, :, :, 0].rearrange("p t e q -> p t (e q)"),
                                        in0=four.rearrange("p (t e) q -> p t (e q)", t=NT), scalar=float(P),
                                        in1=iota_e[:, :, None].broadcast_to([P, NT, 4 * E0]), op0=ALU.mult, op1=ALU.mult))
            link(V.tensor_scalar(tokp[:, :, :, :, 1].rearrange("p t e q -> p (t e q)"), four.rearrange("p m q -> p (m q)"), own_p, None, ALU.mult))
            dve.wait_ge(S["act_link"], 4)
            link(V.tensor_scalar(nega[:, :, :], nega[:, :, :], -1.0, None, ALU.mult))
            link(V.tensor_scalar(invat[:, :], invat[:, :], -1.0, None, ALU.mult))
            link(V.reciprocal(inva[:, :, :], nega[:, :, :]))
            link(V.reciprocal(invat[:, :], invat[:, :]))
            dve_at["inva"] = link.n
            dve.wait_ge(S["sp_free"], 8)
            for c in range(8):
                dve.wait_ge(S["rest_ready"], c + 1)
                link.more(V.tensor_tensor(part(c), part(c), rests[c], ALU.subtract))
            dve.wait_ge(S["dve_link"], link.n)
            for c in range(8):
                dve.wait_ge(S["ln_r"], c + 1)
                link.more(V.tensor_tensor(part(c), part(c), logs[c], ALU.add))
            dve.wait_ge(S["dve_link"], link.n)
            dve_at["delta"] = link.n

            def mult(b, s):
                n2, h = s // 2, s % 2
                dve.wait_ge(S["cbc_ready"], b * 8 + n2 + 1)
                dve.wait_ge(S["ab_free"], b * 16 + (s + 9))
                for r in range(2):
                    n = 2 * n2 + r
                    m = V.scalar_tensor_tensor(out=zb[:, s % 8, r, :], in0=zb[:, s % 8, r, :], scalar=inva[:, h, n:n + 1],
                                               in1=bank[4][:, r * L:(r + 1) * L], op0=ALU.mult, op1=ALU.mult)
                m.then_inc(S["p_ready"], 1)

            def finish(b, par):
                dve.wait_ge(S["m_evac"], b + 1)
                if later(b, 2):
                    dve.wait_ge(S["dn_ready"], b + 1)
                link(V.tensor_tensor(yg[:, par, :, :], xm[:, :, bass.ds(b * L, L)], mcur[:, par, :, :], ALU.mult))
                dve.wait_ge(S["p_free"], b * 16 + (16 + 8))
                yf = yg[:, par, :, :].rearrange("p h l -> p (h l)")
                link(V.tensor_tensor(yf, bank[5][:, :], yf, ALU.subtract))
                dve.sem_inc(S["y_free"], 1)
                V.tensor_tensor(yg[:, par, :, :], yg[:, par, :, :], gate[:, :, bass.ds(b * L, L)], ALU.mult).then_inc(S["yg_ready"], 1)

            def main(b, par):
                for s in range(16):
                    dve.wait_ge(S["ab_ready"], b * 16 + s + 1)
                    dve.wait_ge(S["dw_ready"], b * 16 + s + 1)
                    dve.wait_ge(S["p_free"], b * 16 + s + 1)
                    for r in range(2):
                        m = V.tensor_tensor_scan(zb[:, s % 8, r, :], bank[s % 4][:, r * L:(r + 1) * L], abar[:, s % 8, r, :],
                                                 0.0, ALU.add, ALU.mult)
                    m.then_inc(S["ab_free"], 1)
                    if s >= 1:
                        mult(b, s - 1)
                    elif later(b, 1):
                        mult(b - 1, 15)
                    if s == 4 and later(b, 1):
                        finish(b - 1, 1 - par)

            main(0, 0)
            with dve.Fori(0, 3) as i:
                link.loop(i, 4)
                main(i * 2 + 1, 1)
                main(i * 2 + 2, 0)
            link.end(3)
            main(7, 1)
            mult(7, 15)
            finish(7, 1)
            dve.sem_inc(S["dve_done"], 1)
            for q in range(4):
                dve.wait_ge(S["pe_done"], q + 2)
                t = acc[:, 4 * q:4 * q + 4, :].rearrange("p t d -> p (t d)")
                V.tensor_tensor(t, t, bank[q % 2][:, :], ALU.add).then_inc(S["dve_done"], 1)


            def one_hot(e):
                if e > 1:
                    dve.wait_ge(S["cp_ready"], e - 1)
                V.tensor_tensor(hot[:, e % 2, :, :], iota_p[:, None, :].broadcast_to([P, NT, P]),
                                place[:, :, e:e + 1].broadcast_to([P, NT, P]), ALU.is_equal).then_inc(S["hot_ready"], 1)

            def indices(e):
                dve.wait_ge(S["cp_ready"], e + 1)
                pair = bank[7][:, 0:8].rearrange("p (q c) -> p q c", c=2)
                link(V.tensor_reduce(idxf, pair, AX.X, ALU.add))
                V.tensor_copy(idx[:, 4 * e:4 * e + 4], idxf).then_inc(S["id_ready"], 1)

            def gated(e):
                dve.wait_ge(S["d_ready"], e + 1)
                if e > 1:
                    dve.wait_ge(S["added"], 64 * (e - 1))
                y = ye[:, e % 2, :, :]
                link(V.tensor_tensor(y, bank[4 + e % 2][:, :].rearrange("p (q d) -> p q d", q=4),
                                     b2b[:, e % 2, None, :].broadcast_to([P, 4, P]), ALU.add))
                V.tensor_tensor(y, y, xg[:, e % 4, :, P + e:P + e + 1].broadcast_to([P, 4, P]), ALU.mult).then_inc(S["ye_ready"], 1)

            expert_steps(((0, one_hot), (0, indices), (3, gated)))
            dve.sem_inc(S["layer0"], 1)

            def layer0_sum(q):
                dve.wait_ge(S[f"moe_in{q}"], 16)
                link(V.tensor_tensor(acc[:, 4 * q:4 * q + 4, :], acc[:, 4 * q:4 * q + 4, :], xn[:, 4 * q:4 * q + 4, :], ALU.add))

            for q in range(5):
                if q < 4:
                    layer0_sum(q)
                    norm_stats(acc, 2, q)
                if q:
                    normalize(xn, acc, 2, q - 1)
            link(V.tensor_scalar(xnw[:, :, P].bitcast(I32), iota_e, float(P), own_p, ALU.mult, ALU.add))
            dve.sem_inc(S["dve_done"], 1)
            dve.wait_ge(S["act_link"], 6)
            dve.wait_ge(S["ld_late"], 8 * 16)
            link(V.tensor_tensor(sc[:, :, :], sc[:, :, :], br1s[:, None, :].broadcast_to([P, NT, E1]), ALU.add))
            softmax_less_max(E1, "act_link", 6, sc[:, :, :], "smax1")
            oh = [zs[:, 1024 + 256 * w:1280 + 256 * w].rearrange("p (t e) -> p t e", t=NT) for w in range(2)]
            pre = [zs[:, 1536 + 256 * w:1792 + 256 * w].rearrange("p (t e) -> p t e", t=NT) for w in range(2)]
            ek = selb[:, :, :].rearrange("p n m -> p (n m)").bitcast(F32)[:, 0:SLOTT * E1].rearrange("p (k e) -> p k e", e=E1)
            within = bank[5][:, 0:NT * E1].rearrange("p (t e) -> p t e", t=NT)
            total = bank[5][:, NT * E1:2 * NT * E1].rearrange("p (t e) -> p t e", t=NT)

            def best(half):
                for t in range(8 * half, 8 * half + 8):
                    link.more(V.max(mx8[:, t, :], sc[:, t, :]))
                dve.wait_ge(S["dve_link"], link.n)

            def best_index(half):
                for t in range(8 * half, 8 * half + 8):
                    link.more(V.max_index(ix8[:, t, :], mx8[:, t, :], sc[:, t, :]))
                dve.wait_ge(S["dve_link"], link.n)

            def chosen(w):
                link(V.tensor_copy(ixf[:, w, :], ix8[:, :, w]))
                link(V.tensor_tensor(oh[w], iota_e[:, None, :].broadcast_to([P, NT, E1]),
                                     ixf[:, w, :, None].broadcast_to([P, NT, E1]), ALU.is_equal))

            def either():
                link(V.tensor_tensor(mkb[:, :, :], oh[0], oh[1], ALU.add))
                dve.sem_inc(S["dve_done"], 1)

            def before():
                dve.wait_ge(S["pe_done"], 12)
                link(V.memset(pre[0][:, 0:1, :], 0.0))
                link(V.tensor_copy(pre[0][:, 1:NT, :], total[:, 0:NT - 1, :]))

            def double(cur, d):
                link(V.tensor_copy(pre[1 - cur][:, 0:d, :], pre[cur][:, 0:d, :]))
                link(V.tensor_tensor(pre[1 - cur][:, d:NT, :], pre[cur][:, d:NT, :], pre[cur][:, 0:NT - d, :], ALU.add))

            ti = inc8[:, 0, :]

            def tiles():
                link(V.tensor_tensor(esm[:, 0, :], pre[0][:, NT - 1, :], total[:, NT - 1, :], ALU.add))
                link(V.tensor_scalar(ti, esm[:, 0, :], float(P - 1), None, ALU.add))
                link(V.tensor_scalar(ti, ti, 7, None, ALU.logical_shift_right))
                link(V.tensor_copy(esm[:, 1, :], ti))
                link(V.memset(esm[:, 2, :], 1.0))

            def tile_sums():
                link(V.tensor_tensor_scan(esm[:, 3, :], esm[:, 2, :], esm[:, 1, :], 0.0, ALU.mult, ALU.add))
                link(V.tensor_tensor(esm[:, 4, :], esm[:, 3, :], esm[:, 1, :], ALU.subtract))
                link(V.tensor_scalar(esm[:, 4, :], esm[:, 4, :], float(P), None, ALU.mult))

            def slot_numbers():
                link(V.tensor_tensor(pre[0], pre[0], within, ALU.add))
                link(V.tensor_tensor(pre[0], pre[0], esm[:, 4, None, :].broadcast_to([P, NT, E1]), ALU.add))

            def slots(w):
                link(V.tensor_tensor(oh[w], oh[w], pre[0], ALU.mult))
                link(V.tensor_reduce(ixf[:, w, :], oh[w], AX.X, ALU.add))
                link(V.tensor_copy(slot[:, w, :], ixf[:, w, :]))

            def tile_experts():
                link(V.tensor_tensor(ek, iota_k[:, :, None].broadcast_to([P, SLOTT, E1]),
                                     esm[:, 3, None, :].broadcast_to([P, SLOTT, E1]), ALU.is_ge))

            def tile_experts2():
                link(V.tensor_reduce(ekf[:, :], ek, AX.X, ALU.add))
                link(V.tensor_scalar(eidx[:, :], ekf[:, :], float(E1 - 1), None, ALU.min))
                dve.sem_inc(S["dve_done"], 1)

            def route(b, h):
                if b == 0:
                    if h == 1:
                        softmax_scale(E1, 2)
                    if h in (3, 4):
                        best(h - 3)
                    if h in (5, 6):
                        best_index(h - 5)
                    if h == 7:
                        chosen(0)
                if b == 1:
                    if h == 0:
                        chosen(1)
                    if h == 1:
                        either()
                    if h == 5:
                        before()
                    if h == 6:
                        double(0, 1)
                    if h == 7:
                        double(1, 2)
                if b == 2:
                    if h == 0:
                        double(0, 4)
                    if h == 1:
                        double(1, 8)
                    if h == 2:
                        tiles()
                    if h == 3:
                        tile_sums()
                    if h == 4:
                        slot_numbers()
                    if h in (5, 6):
                        slots(h - 5)
                    if h == 7:
                        dve.sem_inc(S["dve_done"], 1)
                        tile_experts()
                if b == 3 and h == 0:
                    tile_experts2()


            def decay(b, h):
                dve.wait_ge(S["s_ready"], b * 8 + (h + 1))
                dve.wait_ge(S["pm_free"], b * 8 + (h + 5))
                V.tensor_tensor(pbuf[:, h % 4, :], bank[h % 4][:, 0:SC], maskd[:, h, :], ALU.mult).then_inc(S["pm_ready"], 1)

            for b in range(4):
                for h in range(HEADS):
                    decay(b, h)
                    route(b, h)
            with dve.Fori(0, NB - 4) as i:
                for h in range(HEADS):
                    decay(i + 4, h)
            dve.sem_inc(S["dve_done"], 1)
            for q in range(4):
                o = slice(q * CH, (q + 1) * CH)
                rt = hbuf[:, 1, 2 + q % 2, :]
                dve.wait_ge(S["gate_sb"], q + 1)
                link.more(V.tensor_scalar(oT[:, o], oT[:, o], colv[:, C_GB:C_GB + 1], None, ALU.add))
                dve.wait_ge(S["groot"], q + 1)
                link(V.reciprocal(rt, rt))
                link(V.tensor_tensor(rt, bank[q][:, :], rt, ALU.mult))
                V.scalar_tensor_tensor(out=oT[:, o], in0=rt, scalar=colv[:, C_GW:C_GW + 1], in1=oT[:, o],
                                       op0=ALU.mult, op1=ALU.add).then_inc(S["dve_done"], 1)
            for q in range(4):
                dve.wait_ge(S["pe_done"], 13 + q)
                t = acc[:, 4 * q:4 * q + 4, :].rearrange("p t d -> p (t d)")
                V.tensor_tensor(t, t, bank[q][:, :], ALU.add).then_inc(S["dve_done"], 1)

            def h_out(k, u):
                dve.wait_ge(S["hT_ps"], k + 1)
                if later(k, 2):
                    dve.wait_ge(S["y_ps"], k - 1)
                V.tensor_copy(hT[:, u % 2, :], bank[2 + u % 2][:, :]).then_inc(S["hT_sb"], 1)

            def y_out(k, u):
                dve.wait_ge(S["y_ps"], k + 1)
                if later(k, 4):
                    dve.wait_ge(S["added1"], k * 16 - 48)
                V.tensor_scalar(ys[:, u % 4, :], bank[6 + u % 2][:, 0:P], xs[:, u, P + 1:P + 2], None, ALU.mult).then_inc(S["y_sb"], 1)

            slot_steps(dve, ((2, h_out), (LAG, y_out)))

        @block.sync
        def _(sp):
            xv = x.rearrange("(t p) d -> p t d", p=P)
            for q in range(4):
                sp.dma_start(acc[:, 4 * q:4 * q + 4, :], xv[:, 4 * q:4 * q + 4, :]).then_inc(S[f"ld_x{q}"], 16)
            sp.dma_start(ident[:, :], cf[:, 0:P]).then_inc(S["ld_i"], 16)
            sp.dma_start(wr0s[:, :], wr0).then_inc(S["ld_r"], 16)
            for dst, src in ((bis[:, :, :, :], bits_i), (bfs[:, :, :, :], bits_f)):
                sp.dma_start(dst, src).then_inc(S["ld_s"], 16)
            for dst, src in ((colv[:, :], cols), (cfs[:, :], cf[:, P:P + 514]),
                             (abar[:, 0:4, :, :].rearrange("p a b l -> p (a b l)"), cf[:, P + 514:])):
                sp.dma_start(dst, src).then_inc(S["ld_c"], 16)
            for k in range(K):
                sp.dma_start(convb[:, k, :], conv_t[k, :].partition_broadcast(P)).then_inc(S["ld_w"], 16)
            for dst, src in ((wup1, w_up1), (wup2, w_up2),
                             (wll[:, :, :], w_ll.rearrange("(h p) e -> p h e", p=P)),
                             (wdn[:, :, :], w_down.rearrange("(h p) e -> p h e", p=P)),
                             (nega[:, :, :], a_log.rearrange("(h p) n -> p h n", p=P)),
                             (invat[:, :], a_log_t)):
                sp.dma_start(dst, src).then_inc(S["ld_w"], 16)
            def weights1(e):
                if e > 1:
                    sp.wait_ge(S["u_ready"], (e - 1) * HC)
                sp.dma_start(w1b[:, e % 2, :], w1_0[e, :, :]).then_inc(S[f"w1_in{e % 2}"], 16)

            def weights2(e):
                if e > 1:
                    sp.wait_ge(S["ye_ready"], e - 1)
                for dst, src in ((w2b[:, e % 2, :, :].rearrange("p c d -> p (c d)"), w2_0[e, :, :]),
                                 (b2b[:, e % 2, :], b2_0[e, :].partition_broadcast(P))):
                    sp.dma_start(dst, src).then_inc(S[f"w2_in{e % 2}"], 16)

            for e in range(2):
                weights1(e)
                weights2(e)
            sp.wait_ge(S["norm_ready"], 4)
            sp.dma_start(rows.rearrange("(t p) r -> p t r", p=P)[:, :, 0:P], xn[:, :, :]).then_inc(S["rows_x"], 16)
            sp.wait_ge(S["gates_ready"], 1)
            sp.dma_start(rows.rearrange("(t p) r -> p t r", p=P)[:, :, P:ROW], gts[:, :, :]).then_inc(S["rows_g"], 16)
            sp.wait_ge(S["dve_done"], 7)
            for dst, src in ((latef[:, 0:HEADS * SC + 2 * P], mask_d), (wqs, wq), (wks, wk), (wvs, wv), (wgs, wg), (wos, wo),
                             (wr1s, wr1), (br1s, br1[0, :].partition_broadcast(P))):
                sp.dma_start(dst, src).then_inc(S["ld_late"], 16)

            def resident(q):
                e = slice(4 * q, 4 * q + 4)
                sp.dma_start(w1r[:, e, :], w1_1.rearrange("e p h -> p e h")[:, e, :]).then_inc(S["ld_w1"], 16)
                sp.dma_start(w2r[:, e, :, :].rearrange("p e c d -> p e (c d)"),
                             w2_1.rearrange("e p h -> p e h")[:, e, :]).then_inc(S["ld_w1"], 16)

            weights1(2)
            for e in range(2, E0):
                if e + 1 < E0:
                    weights1(e + 1)
                weights2(e)
                if e < 6:
                    resident(e - 2)
            sp.wait_ge(S["added"], 64 * E0)
            for q in range(4):
                sp.dma_start(xn[:, 4 * q:4 * q + 4, :], moe.rearrange("(t p) d -> p t d", p=P)[:, 4 * q:4 * q + 4, :]
                             ).then_inc(S[f"moe_in{q}"], 16)
            sp.wait_ge(S["layer0"], 1)
            sp.dma_start(bias1, b_1).then_inc(S["ld_b"], 16)
            sp.wait_ge(S["b_split"], 1)
            sp.wait_ge(S["gv_ready"], 4)
            for part, src in enumerate((bhi, bmid, blo)):
                sp.dma_start(b1p[part:part + 1, :, :], src[:, 0:HID]).then_inc(S["ld_bp"], 16)
                sp.dma_start(b2p[part:part + 1, :, :], src[:, HID:PB]).then_inc(S["ld_bp"], 16)
            sp.wait_ge(S["scattered"], 33 * 16)

            sp.wait_ge(S["gate_ps"], 4)

            def load(k, u):
                if not isinstance(k, int):
                    sp.wait_ge(S["added1"], k * 16 - 112)
                sp.dma_start(xs[:, u, :], xd[bass.ds(k * P, P), :]).then_inc(S[f"xs_in{u}"], 16)

            for u in range(8):
                load(u, u)
            for q in range(4):
                sp.wait_ge(S["dve_done"], 17 + q)
                sp.dma_start(out.rearrange("(t p) d -> p t d", p=P)[:, 4 * q:4 * q + 4, :], acc[:, 4 * q:4 * q + 4, :]
                             ).then_inc(S["sum_out"], 16)
            with sp.Fori(0, SLOTT // 8 - 1) as i:
                for u in range(8):
                    load(i * 8 + (8 + u), u)
            sp.wait_ge(S["added1"], SLOTT * 16)
            sp.wait_ge(S["sum_out"], 64)

        @block.tensor
        def _(pe):
            pe.wait_ge(S["ld_i"], 16)

            def transpose_norm(src, ready, first, quarters=range(4)):
                for q in quarters:
                    pe.wait_ge(S["norm_ready"], ready + q + 1)
                    for r in range(4):
                        m = pe.transpose(bank[first + q][:, r * P:(r + 1) * P], src[:, 4 * q + r, :], ident[:, :])
                    m.then_inc(S["ps_ready"], 1)

            for q in range(5):
                if q < 4:
                    transpose_norm(xn, 0, 0, (q,))
                if q:
                    pe.wait_ge(S["ps_free"], q)
                    if q == 1:
                        pe.wait_ge(S["ld_r"], 16)
                    for t in range(4 * q - 4, 4 * q):
                        m = pe.matmul(bank[7][:, t * E0:(t + 1) * E0], xnT[:, t * P:(t + 1) * P], wr0s[:, :], start=True, stop=True)
            m.then_inc(S["pe_done"], 1)
            z2 = hbuf[:, 0, :, :].rearrange("p c (q d) -> p (c q) d", d=P)
            for q in range(4):
                pe.wait_ge(S["norm2_ready"], q + 1)
                for r in range(4):
                    m = pe.transpose(bank[Z2_BANK[q]][:, r * P:(r + 1) * P], z2[:, 4 * q + r, :], ident[:, :])
                m.then_inc(S["ps_ready"], 1)

            pe.wait_ge(S["ld_w"], 10 * 16)
            pe.wait_ge(S["wconv_ready"], 1)
            pe.wait_ge(S["ps_free"], 8)
            def count(i):
                pe.wait_ge(S["cnt_in"], i + 1)
                pe.matmul(bank[5][:, 0:3 * P], onesb[:, :], cmp3[:, :, :, :].rearrange("p c t e -> p (c t e)"),
                          start=True, stop=True).then_inc(S["cnt_out"], 1)

            def count_ties(k):
                pe.wait_ge(S["cnt_in"], ROUNDS + 1 + k)
                if k == 0:
                    pe.matmul(bank[5][:, 0:P], onesb[:, :], cmpb, start=True, stop=True).then_inc(S["cnt_out"], 1)
                else:
                    of = eqb[:, :, :] if k == 1 else chb
                    pe.matmul(bank[5][:, 0:P], onesb[:, :], of, start=True, stop=True)
                    pe.matmul(bank[6][:, 0:P], ltri[:, :], of, start=True, stop=True).then_inc(S["cnt_out"], 1)

            with pe.Fori(0, NC) as j:
                for q in range(4):
                    pe.wait_ge(S["psd_free"], j * 4 + q + 1)
                    h = q % 2
                    if q < 2:
                        for k in range(K):
                            if q * K + k in (0, 2, 5, 7):
                                count(j * 4 + (0, 2, 5, 7).index(q * K + k))
                            m = pe.matmul(bank[q][:, :], wconv[:, k, h * P:(h + 1) * P],
                                          z2p[:, bass.ds(j * 2, 2), k:k + L], start=(k == 0), stop=(k == K - 1))
                    else:
                        m = pe.matmul(bank[q][:, :], wup2[:, h * P:(h + 1) * P],
                                      z2p[:, bass.ds(j * 2, 2), K - 1:K - 1 + L], start=True, stop=True)
                    m.then_inc(S["psd_ready"], 1)
            pe.wait_ge(S["psd_free"], 4 * NC + 4)
            for c in range(8):
                j, h = c // 2, c % 2
                if c > 3:
                    pe.wait_ge(S["sp_free"], c - 3)
                for kh in range(NH2):
                    m = pe.matmul(bank[c % 4][:, :], wll[:, kh, h * P:(h + 1) * P], xm[:, kh, j * CH:(j + 1) * CH],
                                  start=(kh == 0), stop=(kh == NH2 - 1))
                m.then_inc(S["sp_ps"], 1)
                if 0 < c < 4:
                    count_ties(c - 1)

            DW, CB_, Y, M0, M1 = bank[0:4], bank[4], bank[5], bank[6], bank[7]

            def pro1(b, par):
                pe.wait_ge(S["xcur_ready"], b + 1)
                if not (isinstance(b, int) and b == 0):
                    pe.wait_ge(S["m_evac"], b)
                    pe.wait_ge(S["pro_bte"], b)
                    pe.wait_ge(S["dn_evac"], b - 1) if not (isinstance(b, int) and b == 1) else None
                for c in range(2):
                    for h in range(NH2):
                        pe.transpose(M0[:, c * DI + h * P:c * DI + (h + 1) * P], xcur[:, par, h, c * P:(c + 1) * P], ident[:, :])
                for w in range(2):
                    for h in range(NH2):
                        m = pe.matmul(M1[0:N, w * L:(w + 1) * L], wll[:, h, DI + w * N:DI + (w + 1) * N],
                                      xcur[:, par, h, :], start=(h == 0), stop=(h == NH2 - 1))
                m.then_inc(S["pro_x"], 1)

            def pro2(b, par):
                pe.wait_ge(S["pro_xe"], b + 1)
                pe.sem_inc(S["pe_past"], 1)
                for c in range(2):
                    m = pe.transpose(M0[:, c * N:(c + 1) * N], bcur[:, par, c * P:(c + 1) * P], ident[0:N, 0:N])
                m.then_inc(S["pro_bt"], 1)

            def pro3(b, par):
                pe.wait_ge(S["cb_ready"], b + 1)
                for h in range(NH2):
                    m = pe.matmul(M1[:, h * L:(h + 1) * L], invat[:, h * P:(h + 1) * P], cb[:, par, :], start=True, stop=True)
                m.then_inc(S["m_ready"], 1)

            def down(b, par, last):
                pe.wait_ge(S["yg_ready"], b + 1)
                pe.wait_ge(S["pro_bte"], 8 if last else b + 3)
                for h in range(NH2):
                    m = pe.matmul(M0[:, 0:L], wdn[:, h, :], yg[:, par, h, :], start=(h == 0), stop=(h == NH2 - 1))
                m.then_inc(S["dn_ready"], 1)

            def y_sum(b, s):
                n2, h = s // 2, s % 2
                pe.wait_ge(S["q_ready"], b * 16 + s + 1)
                if s == 0:
                    pe.wait_ge(S["y_free"], b + 1)
                pe.matmul(Y[:, h * L:(h + 1) * L], ident[:, :], zb[:, s % 8, 0, :], start=(s == 0), stop=(s == 15),
                          skip_group_check=True).then_inc(S["p_free"], 1)

            def c_rows(b, par, n2):
                pe.wait_ge(S["p_ready"], b * 16 + 2 * n2 + 2)
                for r in range(2):
                    m = pe.matmul(CB_[:, r * L:(r + 1) * L], selb[:, 2 * n2 + r, :], csp[:, par, :], start=True, stop=True)
                m.then_inc(S["cbc_ready"], 1)

            def main(b, par, more):
                first = isinstance(b, int) and b == 0
                pe.wait_ge(S["csp_lo"], b + 1)
                for s in range(16):
                    n2, h = s // 2, s % 2
                    if h == 0:
                        pe.wait_ge(S["bd_ready"], b * 8 + n2 + 1)
                    pe.wait_ge(S["ab_free"], b * 16 + s + 5)
                    o = DW[s % 4][:, :].rearrange("p (n t) -> p n t", n=2)
                    pe.matmul(o[:, :, 0:P + 1], xT[:, par, 0, h * P:(h + 1) * P], bd[:, par, 0, 2 * n2:2 * n2 + 2, :],
                              start=True, stop=False, skip_group_check=True)
                    pe.matmul(o[:, :, P:L], xT[:, par, 1, h * P:(h + 1) * P], bd[:, par, 1, 2 * n2:2 * n2 + 2, 0:P],
                              start=False, stop=True, skip_group_check=True).then_inc(S["dw_ready"], 1)
                    if h == 1 and s > 1:
                        c_rows(b, par, n2 - 1)
                    elif h == 1 and not first:
                        c_rows(b - 1, 1 - par, 7)
                    if s >= YLAG:
                        y_sum(b, s - YLAG)
                    elif not first:
                        y_sum(b - 1, s + 16 - YLAG)
                    if more:
                        if s == 1:
                            pro1(b + 1, 1 - par)
                        if s == 4:
                            pro2(b + 1, 1 - par)
                        if s == 8:
                            pro3(b + 1, 1 - par)
                    if s == 10 and not first:
                        down(b - 1, 1 - par, not more)

            pe.wait_ge(S["dve_link"], dve_at["search"])
            pro1(0, 0)
            pro2(0, 0)
            pe.wait_ge(S["dve_link"], dve_at["inva"])
            pro3(0, 0)
            pe.wait_ge(S["sp_free"], 8)
            main(0, 0, True)
            with pe.Fori(0, 3) as i:
                main(i * 2 + 1, 1, True)
                main(i * 2 + 2, 0, True)
            main(7, 1, False)
            c_rows(7, 1, 7)
            for s in range(16 - YLAG, 16):
                y_sum(7, s)
            pe.wait_ge(S["dn_evac"], 8)
            pe.wait_ge(S["yg_ready"], 8)
            for h in range(NH2):
                m = pe.matmul(M0[:, 0:L], wdn[:, h, :], yg[:, 1, h, :], start=(h == 0), stop=(h == NH2 - 1))
            m.then_inc(S["dn_ready"], 1)
            pe.wait_ge(S["dn_evac"], 9)
            ymt = z2p[:, :, :].rearrange("p b l -> p (b l)")
            for q in range(4):
                pe.wait_ge(S["dve_done"], 3 if q < 2 else 2 + q)
                for r in range(4):
                    t = 4 * q + r
                    m = pe.transpose(bank[q % 2][:, r * P:(r + 1) * P], ymt[:, t * P:(t + 1) * P], ident[:, :])
                m.then_inc(S["pe_done"], 1)

            def compact(e):
                pe.wait_ge(S["hot_ready"], e + 1)
                if e:
                    pe.wait_ge(S["id_ready"], e)
                else:
                    pe.wait_ge(S["dn_evac"], 9)
                for t in range(NT):
                    m = pe.matmul(bank[7][:, 0:8], hot[:, e % 2, t, :], tokp[:, t, e, :, :], start=(t == 0), stop=(t == NT - 1))
                m.then_inc(S["cp_ready"], 1)

            def turn_rows(e):
                pe.wait_ge(S[f"xg_in{e % 4}"], 64 * (e // 4 + 1))
                if e:
                    pe.wait_ge(S["xg_sb"], e)
                for q in range(4):
                    m = pe.transpose(bank[6][:, q * P:(q + 1) * P], xg[:, e % 4, q, 0:P], ident[:, :])
                m.then_inc(S["xg_ps"], 1)

            def up0(e):
                pe.wait_ge(S[f"w1_in{e % 2}"], 16 * (e // 2 + 1))
                pe.wait_ge(S["xg_sb"], e + 1)
                for c in range(HC):
                    if e:
                        pe.wait_ge(S["h_ready"], (e - 1) * HC + c + 1)
                    else:
                        pe.wait_ge(S["dve_done"], 7)
                    pe.matmul(bank[c][:, :], w1b[:, e % 2, c * P:(c + 1) * P], xgT[:, e % 2, :], start=True, stop=True
                              ).then_inc(S["u_ready"], 1)

            def down0(e):
                pe.wait_ge(S[f"w2_in{e % 2}"], 32 * (e // 2 + 1))
                pe.wait_ge(S["h_ready"], (e + 1) * HC)
                if e > 1:
                    pe.wait_ge(S["ye_ready"], e - 1)
                for q in range(4):
                    for c in range(HC):
                        m = pe.matmul(bank[4 + e % 2][:, q * P:(q + 1) * P], hbuf[:, e % 2, c, q * P:(q + 1) * P],
                                      w2b[:, e % 2, c, :], start=(c == 0), stop=(c == HC - 1))
                m.then_inc(S["d_ready"], 1)

            expert_steps(((2, up0), (0, compact), (1, turn_rows), (3, down0)))

            pe.wait_ge(S["ld_late"], 8 * 16)
            for q in range(5):
                if q < 4:
                    transpose_norm(xn, 4, 0, (q,))
                if q:
                    for t in range(4 * q - 4, 4 * q):
                        pe.wait_ge(S["ps_free"], 9 + min(t // 3, 3))
                        m = pe.matmul(bank[t // 3][:, t % 3 * (P + E1):(t % 3 + 1) * (P + E1)], xnT[:, t * P:(t + 1) * P], wvr,
                                      start=True, stop=True)
                        if t % 3 == 2 or t == NT - 1:
                            m.then_inc(S["pe_done"], 1)
            pe.wait_ge(S["act_link"], 6)

            def choices():
                pe.wait_ge(S["dve_done"], 9)
                pe.matmul(bank[5][:, 0:NT * E1], ltri[:, :], mkb[:, :, :], start=True, stop=True)
                pe.matmul(bank[5][:, NT * E1:2 * NT * E1], onesb[:, :], mkb[:, :, :], start=True, stop=True
                          ).then_inc(S["pe_done"], 1)

            def project(b, par):
                if not (isinstance(b, int) and b == 0):
                    pe.wait_ge(S["qk_sb"], b)
                pe.sem_inc(S["pe_past"], 1)
                for w, o in ((wqs, 0), (wks, L)):
                    m = pe.matmul(bank[4][:, o:o + L], w, xnT[:, bass.ds(b * L, L)], start=True, stop=True)
                m.then_inc(S["qk_ps"], 1)

            def scores(b, par, h):
                if h == 0:
                    pe.wait_ge(S["qk_sb"], b + 1)
                pe.wait_ge(S["pm_ready"], b * 8 + (h + 1))
                pe.matmul(bank[h % 4][:, 0:L], kT[:, par, 0:P], qm[:, par, h, :], start=True, stop=True)
                pe.matmul(bank[h % 4][:, L:SC], kT[:, par, P:L], qm[:, par, h, P:L], start=True, stop=True
                          ).then_inc(S["s_ready"], 1)

            def retain(b, par, h):
                if h == 0:
                    pe.wait_ge(S["r_free"], b + 1)
                pe.wait_ge(S["pm_ready"], b * 8 + (h + 5))
                o = bank[6 + par]
                pe.matmul(o[:, 0:L], vm[par][:, 0, h, :], pbuf[:, h % 4, 0:L], start=(h == 0), stop=False, skip_group_check=True)
                pe.matmul(o[:, P:L], vm[par][:, 1, h, :], pbuf[:, h % 4, L:SC], start=False, stop=(h == HEADS - 1),
                          skip_group_check=True).then_inc(S["pm_free"], 1)

            def attend(b, par, more):
                for h in range(HEADS):
                    scores(b, par, h)
                    if h >= 3:
                        retain(b, par, h - 3)
                    elif not (isinstance(b, int) and b == 0):
                        retain(b - 1, 1 - par, h + 5)
                    if h == 4 and more:
                        project(b + 1, 1 - par)
                    if h == 4 and isinstance(b, int) and b == 1:
                        choices()

            project(0, 0)
            for b in range(3):
                attend(b, b % 2, True)
            with pe.Fori(0, 2) as i:
                attend(i * 2 + 3, 1, True)
                attend(i * 2 + 4, 0, True)
            attend(7, 1, False)
            for h in range(5, HEADS):
                retain(7, 1, h)
            def gate_in(q):
                if q > 1:
                    pe.wait_ge(S["gate_sb"], q - 1)
                else:
                    pe.wait_ge(S["r_free"], NB + 2)
                pe.matmul(bank[6 + q % 2][:, :], wgs, xnT[:, q * CH:(q + 1) * CH], start=True, stop=True).then_inc(S["gate_ps"], 1)

            def variance(q):
                pe.wait_ge(S["gsq_ready"], q + 1)
                if q > 1:
                    pe.wait_ge(S["groot"], q - 1)
                pe.matmul(bank[4 + q % 2][:, :], average, hbuf[:, 1, q % 2, :], start=True, stop=True).then_inc(S["gv_ready"], 1)

            gate_in(0)
            gate_in(1)
            for q in range(4):
                pe.matmul(bank[q][:, :], centre, retT[:, q * CH:(q + 1) * CH], start=True, stop=True).then_inc(S["gc_ready"], 1)
            gate_in(2)
            gate_in(3)
            for q in range(4):
                variance(q)
            for q in range(4):
                pe.wait_ge(S["dve_done"], 13 + q)
                for r in range(4):
                    t = 4 * q + r
                    m = pe.matmul(bank[q][:, r * P:(r + 1) * P], oT[:, t * P:(t + 1) * P], wos, start=True, stop=True)
                m.then_inc(S["pe_done"], 1)
            pe.wait_ge(S["dve_done"], 20)
            pe.wait_ge(S["ld_w1"], 8 * 16)
            pe.wait_ge(S["ld_bp"], 6 * 16)

            def expert(k):
                return pe.value_load(eidx[0:1, bass.ds(k, 1)], min_val=0, max_val=E1 - 1)

            def turn_x(k, u):
                pe.wait_ge(S[f"xs_in{u}"], (k - u) * 2 + 16)
                if later(k, 2):
                    pe.wait_ge(S["xT_sb"], k - 1)
                pe.transpose(bank[4 + u % 2][:, 0:P], xs[:, u, 0:P], ident[:, :]).then_inc(S["xT_ps"], 1)

            held = {}

            def fetch(k, u):
                held["up"] = expert(k)

            def up(k, u):
                e = held["up"]
                if later(k, 2):
                    pe.wait_ge(S["h_sb"], k - 1)
                pe.wait_ge(S["xT_sb"], k + 1)
                pe.sem_inc(S["pe_past"], 1)
                pe.matmul(bank[u % 2][:, :], onesb[0:3, :], b1p[:, bass.ds(e, 1), :], start=True, stop=False)
                pe.matmul(bank[u % 2][:, :], xsT[:, u % 2, :], w1r[:, bass.ds(e, 1), :], start=False, stop=True
                          ).then_inc(S["h_ps"], 1)

            def turn_h(k, u):
                pe.wait_ge(S["h_sb"], k + 1)
                if later(k, 2):
                    pe.wait_ge(S["hT_sb"], k - 1)
                for c in range(HC):
                    m = pe.transpose(bank[2 + u % 2][:, c * P:(c + 1) * P], hs[:, u % 2, c * P:(c + 1) * P], ident[:, :])
                m.then_inc(S["hT_ps"], 1)

            def down(k, u):
                e = expert(k)
                if later(k, 2):
                    pe.wait_ge(S["y_sb"], k - 1)
                pe.wait_ge(S["hT_sb"], k + 1)
                pe.sem_inc(S["pe_past"], 1)
                pe.matmul(bank[6 + u % 2][:, 0:P], onesb[0:3, :], b2p[:, bass.ds(e, 1), :], start=True, stop=False)
                for c in range(HC):
                    m = pe.matmul(bank[6 + u % 2][:, 0:P], hT[:, u % 2, c * P:(c + 1) * P], w2r[:, bass.ds(e, 1), c, :],
                                  start=False, stop=(c == HC - 1))
                m.then_inc(S["y_ps"], 1)

            slot_steps(pe, ((1, fetch), (0, turn_x), (1, up), (2, turn_h), (LAG, down)))

        @block.scalar
        def _(act):
            link = Chain(act, S["act_link"])

            def norm_root(nth, q):
                act.wait_ge(S["dve_link"], dve_at[nth, q])
                nc.scalar.activation(bn[:, 4 * q:4 * q + 4, 9], bn[:, 4 * q:4 * q + 4, 8], ACT.Sqrt).then_inc(S["norm_root"], 1)

            def turned_out(q, first):
                act.wait_ge(S["ps_ready"], first + q + 1)
                nc.scalar.activation(xnT[:, q * CH:(q + 1) * CH], bank[q][:, :], ACT.Copy).then_inc(S["ps_free"], 1)

            def turned2_out(q):
                act.wait_ge(S["ps_ready"], 4 + q + 1)
                nc.scalar.activation(z2p[:, 2 * q:2 * q + 2, K - 1:K - 1 + L], bank[Z2_BANK[q]][:, :].rearrange("p (b l) -> p b l", b=2),
                                     ACT.Identity, scale=colv[:, C_LNG:C_LNG + 1], bias=colv[:, C_LNB:C_LNB + 1]
                                     ).then_inc(S["ps_free"], 1)

            def second_norm(q):
                act.wait_ge(S["shift_ready"], q + 1)
                for t in range(4 * q, 4 * q + 4):
                    m = nc.scalar.activation(z2[:, t, :], xn[:, t, :], ACT.Identity, scale=bn[:, t, 10:11], bias=bn[:, t, 11:12])
                m.then_inc(S["norm2_ready"], 1)

            z2 = hbuf[:, 0, :, :].rearrange("p c (q d) -> p (c q) d", d=P)
            for q in range(4):
                norm_root(0, q)
            for q in range(2):
                turned_out(q, 0)
            for q in range(4):
                norm_root(1, q)
                if q < 2:
                    turned_out(q + 2, 0)
                if q:
                    second_norm(q - 1)
            second_norm(3)
            act.wait_ge(S["ld_c"], 48)
            link.more(nc.scalar.activation(onesb[:, :], ones_f, ACT.Copy))
            link(nc.scalar.activation(ltri[:, :], cfs[:, 257:385], ACT.Copy))
            act.wait_ge(S["dve_link"], dve_at["smax0"])
            nc.scalar.activation(sc[:, :, 0:E0], sc[:, :, 0:E0], ACT.Exp).then_inc(S["sm_exp"], 1)
            for q in range(4):
                turned2_out(q)
            act.wait_ge(S["ld_w"], 10 * 16)
            link.more(nc.scalar.activation(nega[:, :, :], nega[:, :, :], ACT.Exp))
            link.more(nc.scalar.activation(invat[:, :], invat[:, :], ACT.Exp))
            link.more(nc.scalar.activation(selb[:, :, :].rearrange("p n m -> p (n m)"),
                                           abar[:, 0:4, :, :].rearrange("p a b l -> p (a b l)"), ACT.Copy))
            with act.Fori(0, NC) as j:
                for q in range(4):
                    h = q % 2
                    act.wait_ge(S["psd_ready"], j * 4 + q + 1)
                    act.sem_inc(S["act_past"], 1)
                    if q < 2:
                        nc.scalar.activation(xm[:, h, bass.ts(j, CH)], bank[q][:, :], ACT.Silu,
                                             bias=colv[:, C_CB + h:C_CB + h + 1]).then_inc(S["psd_free"], 1)
                    else:
                        nc.scalar.activation(gate[:, h, bass.ts(j, CH)], bank[q][:, :], ACT.Silu).then_inc(S["psd_free"], 1)
            for c in range(9):
                if c < 8:
                    act.wait_ge(S["sp_ps"], c + 1)
                    nc.scalar.activation(exps[c], bank[c % 4][:, :], ACT.Abs, bias=colv[:, C_BD + c % 2:C_BD + c % 2 + 1]
                                         ).then_inc(S["abs_r"], 1)
                if c:
                    act.wait_ge(S["abs_r"], c)
                    nc.scalar.activation(exps[c - 1], exps[c - 1], ACT.Exp, scale=-1.0).then_inc(S["exp_r"], 1)

            def pro_a(b, par):
                act.wait_ge(S["pro_x"], b + 1)
                if not (isinstance(b, int) and b < 2):
                    act.wait_ge(S["dw_ready"], b * 16 - 16)
                    act.wait_ge(S["cb_ready"], b - 1)
                    act.wait_ge(S["cbc_ready"], b * 8 - 8)
                nc.scalar.activation(xT[:, par, :, :].rearrange("p c d -> p (c d)"), bank[6][:, :], ACT.Copy).then_inc(S["ee"], 1)
                nc.scalar.activation(bcur[:, par, :], bank[7][0:N, 0:L], ACT.Identity, bias=colv[0:N, C_BB:C_BB + 1]
                                     ).then_inc(S["ee"], 1)
                nc.scalar.activation(ccur[:, par, :], bank[7][0:N, L:2 * L], ACT.Identity, bias=colv[0:N, C_BC:C_BC + 1]
                                     ).then_inc(S["ee"], 1)
                act.wait_ge(S["ee"], b * 3 + 3)
                nc.scalar.activation(csp[0:N, par, :], ccur[:, par, :], ACT.Copy).then_inc(S["pro_xe"], 1)
                act.wait_ge(S["pro_xe"], b + 1)
                act.sem_inc(S["csp_hi"], 1)

            def pro_b(b, par):
                act.wait_ge(S["pro_bt"], b + 1)
                if not (isinstance(b, int) and b < 2):
                    act.wait_ge(S["bd_ready"], b * 8 - 8)
                nc.scalar.activation(btok[:, par, :, :].rearrange("p c n -> p (c n)"), bank[6][:, 0:2 * N], ACT.Copy
                                     ).then_inc(S["pro_bte"], 1)
                act.wait_ge(S["csp_r"], b + 1)
                nc.scalar.activation(csp[32:32 + N, par, :], cres[:, 0, :], ACT.Copy).then_inc(S["csp_mid"], 1)
                act.wait_ge(S["csp_r2"], b + 1)
                nc.scalar.activation(csp[64:64 + N, par, :], cres[:, 1, :], ACT.Copy).then_inc(S["csp_lo"], 1)

            def pro_c(b, par):
                act.wait_ge(S["m_ready"], b + 1)
                if not (isinstance(b, int) and b < 2):
                    act.wait_ge(S["yg_ready"], b - 1)
                nc.scalar.activation(mcur[:, par, :, :].rearrange("p h l -> p (h l)"), bank[7][:, :], ACT.Copy
                                     ).then_inc(S["m_evac"], 1)

            ymt = z2p[:, :, :].rearrange("p b l -> p (b l)")

            def down_a(b, par):
                act.wait_ge(S["dn_ready"], b + 3)
                act.sem_inc(S["act_past"], 1)
                nc.scalar.activation(ymt[:, bass.ds(b * L, L)], bank[6][:, 0:L], ACT.Identity,
                                     bias=colv[:, C_DN:C_DN + 1]).then_inc(S["dn_evac"], 1)

            def main(b, par, more):
                for s in range(16):
                    n2, h = s // 2, s % 2
                    act.wait_ge(S["ab_free"], b * 16 + s + 1)
                    act.sem_inc(S["act_past"], 1)
                    for r in range(2):
                        n = 2 * n2 + r
                        m = nc.scalar.activation(abar[:, s % 8, r, :], delta[:, h, bass.ds(b * L, L)], ACT.Exp,
                                                 scale=negs[:, h, n:n + 1])
                    m.then_inc(S["ab_ready"], 1)
                    if s == 0 and not (isinstance(b, int) and b == 0):
                        pro_c(b, par)
                    if s == 2 and not (isinstance(b, int) and b < 2):
                        down_a(b - 2, par)
                    if more:
                        if s == 5:
                            pro_a(b + 1, 1 - par)
                        if s == 10:
                            pro_b(b + 1, 1 - par)

            negs = nega
            pro_a(0, 0)
            act.wait_ge(S["exp_r"], 8)
            for c in range(8):
                nc.scalar.activation(logs[c], exps[c], ACT.Ln, bias=1.0).then_inc(S["ln_r"], 1)
            pro_b(0, 0)
            pro_c(0, 0)
            act.wait_ge(S["dve_link"], dve_at["delta"])
            main(0, 0, True)
            main(1, 1, True)
            with act.Fori(0, 2) as i:
                main(i * 2 + 2, 0, True)
                main(i * 2 + 3, 1, True)
            main(6, 0, True)
            main(7, 1, False)
            down_a(6, 0)
            down_a(7, 1)


            def gelus(e):
                if e > 1:
                    act.wait_ge(S["d_ready"], e - 1)
                for c in range(HC):
                    act.wait_ge(S["u_ready"], e * HC + c + 1)
                    k = C_B10 + e * HC + c
                    nc.scalar.activation(hbuf[:, e % 2, c, :], bank[c][:, :], ACT.Gelu, bias=colv[:, k:k + 1]
                                         ).then_inc(S["h_ready"], 1)

            def rows_out(e):
                act.wait_ge(S["xg_ps"], e + 1)
                if e > 1:
                    act.wait_ge(S["u_ready"], (e - 1) * HC)
                nc.scalar.activation(xgT[:, e % 2, :], bank[6][:, :], ACT.Copy).then_inc(S["xg_sb"], 1)

            expert_steps(((2, gelus), (1, rows_out)))
            for q in range(4):
                norm_root(2, q)
            for q in range(4):
                turned_out(q, 8)
            for k in range(6):
                act.wait_ge(S["pe_done"], 6 + k)
                t = slice(3 * k, min(3 * k + 3, NT))
                o = bank[k][:, 0:(t.stop - t.start) * (P + E1)].rearrange("p (t c) -> p t c", c=P + E1)
                nc.scalar.activation(vtok[:, t, :], o[:, :, 0:P], ACT.Copy)
                m = nc.scalar.activation(sc[:, t, :], o[:, :, P:P + E1], ACT.Copy)
            m.then_inc(S["act_link"], 1)
            def qk_out(b, par):
                act.wait_ge(S["qk_ps"], b + 1)
                if not (isinstance(b, int) and b < 2):
                    act.wait_ge(S["pm_free"], b * 8)
                act.sem_inc(S["act_past"], 1)
                nc.scalar.activation(kT[:, par, :], bank[4][:, L:2 * L], ACT.Copy)
                for h in range(HEADS):
                    nc.scalar.activation(qm[:, par, h, :], bank[4][:, 0:L], ACT.Copy, scale=colv[:, C_HEAD + h:C_HEAD + h + 1])
                v4 = vtok[:, bass.ds(b * 2, 2), :].rearrange("p t (h d) -> p t h d", h=HEADS)
                out4 = vmf[par].rearrange("p (t r) -> p t r", t=2)
                step = P + HD
                nc.scalar.activation(out4[:, :, 0:7 * step].rearrange("p t (h r) -> p t h r", r=step)[:, :, :, 0:HD],
                                     v4[:, :, 0:7, :], ACT.Copy)
                nc.scalar.activation(out4[:, :, 7 * step:7 * step + HD], v4[:, :, 7, :], ACT.Copy).then_inc(S["qk_sb"], 1)

            def ret_out(b, par):
                act.wait_ge(S["pm_free"], b * 8 + 16)
                act.sem_inc(S["act_past"], 1)
                nc.scalar.activation(retT[:, bass.ds(b * L, L)], bank[6 + par][:, 0:L], ACT.Copy).then_inc(S["r_free"], 1)

            act.wait_ge(S["vm_zero"], 1)
            qk_out(0, 0)
            act.wait_ge(S["dve_link"], dve_at["smax1"])
            nc.scalar.activation(sc[:, :, :], sc[:, :, :], ACT.Exp).then_inc(S["sm_exp"], 1)
            qk_out(1, 1)
            with act.Fori(0, 3) as i:
                ret_out(i * 2, 0)
                qk_out(i * 2 + 2, 0)
                ret_out(i * 2 + 1, 1)
                qk_out(i * 2 + 3, 1)
            ret_out(6, 0)
            ret_out(7, 1)
            for q in range(4):
                act.wait_ge(S["gate_ps"], q + 1)
                nc.scalar.activation(oT[:, q * CH:(q + 1) * CH], bank[6 + q % 2][:, :], ACT.Silu).then_inc(S["gate_sb"], 1)

            def square(q):
                act.wait_ge(S["gc_ready"], q + 1)
                if q > 1:
                    act.wait_ge(S["gv_ready"], q - 1)
                nc.scalar.activation(hbuf[:, 1, q % 2, :], bank[q][:, :], ACT.Square).then_inc(S["gsq_ready"], 1)

            def root(q):
                act.wait_ge(S["gv_ready"], q + 1)
                if q > 1:
                    act.wait_ge(S["dve_done"], 11 + q)
                nc.scalar.activation(hbuf[:, 1, 2 + q % 2, :], bank[4 + q % 2][:, :], ACT.Sqrt, bias=colv[:, C_EPS:C_EPS + 1]
                                     ).then_inc(S["groot"], 1)

            square(0)
            square(1)
            for q in range(4):
                root(q)
                if q < 2:
                    square(q + 2)

            def x_out(k, u):
                act.wait_ge(S["xT_ps"], k + 1)
                if later(k, 2):
                    act.wait_ge(S["h_ps"], k - 1)
                nc.scalar.activation(xsT[:, u % 2, :], bank[4 + u % 2][:, 0:P], ACT.Copy).then_inc(S["xT_sb"], 1)

            def relu(k, u):
                act.wait_ge(S["h_ps"], k + 1)
                if later(k, 2):
                    act.wait_ge(S["hT_ps"], k - 1)
                nc.scalar.activation(hs[:, u % 2, :], bank[u % 2][:, :], ACT.Relu).then_inc(S["h_sb"], 1)

            slot_steps(act, ((0, x_out), (1, relu)))

        @block.gpsimd
        def _(pool):
            link = Chain(pool, S["pool_link"])
            for name, n in (("psd_free", 4), ("ab_free", 8), ("p_ready", 2), ("y_free", 1), ("p_free", 8), ("dn_evac", 1), ("dn_ready", 2),
                            ("pm_free", 8), ("pm_ready", 4),
                            ("r_free", 2)):
                pool.sem_inc(S[name], n)
            link(nc.gpsimd.memset(z2p[:, :, 0:K - 1], 0.0))
            link(nc.gpsimd.memset(csp[:, :, :], 0.0))
            blank = bd[:, 0, 0, :, :].rearrange("p n t -> p (n t)")
            link(nc.gpsimd.memset(blank[:, 0:ROW1], 0.0))
            link(nc.gpsimd.memset(blank[:, P:P + 1].bitcast(I32), T))
            nc.gpsimd.dma_start(xd.rearrange("(p k) d -> p k d", p=P), blank[:, None, 0:ROW1].broadcast_to([P, SLOTT, ROW1])
                                ).then_inc(S["scattered"], 16)
            nc.gpsimd.dma_start(moe.rearrange("(p k) d -> p k d", p=P), blank[:, None, 0:P].broadcast_to([P, NT, P])
                                ).then_inc(S["moe_zero"], 16)
            pool.wait_ge(S["ld_w"], 10 * 16)
            for k in range(K):
                m = nc.gpsimd.tensor_tensor(wconv[:, k, :], wup1, convb[:, k, :], ALU.mult)
            m.then_inc(S["wconv_ready"], 1)
            pool.wait_ge(S["norm_ready"], 4)
            nc.gpsimd.tensor_tensor(acc[:, :, :], acc[:, :, :], xn[:, :, :], ALU.add).then_inc(S["sum_ready"], 1)

            pool.wait_ge(S["psd_free"], 4 + 4 * NC)
            pool.wait_ge(S["scattered"], 16)
            pool.wait_ge(S["moe_zero"], 16)

            def pro_x(b, par):
                if not (isinstance(b, int) and b < 2):
                    pool.wait_ge(S["pro_x"], b - 1)
                pool.sem_inc(S["pool_past"], 1)
                nc.gpsimd.tensor_copy(xcur[:, par, :, :], xm[:, :, bass.ds(b * L, L)]).then_inc(S["xcur_ready"], 1)

            def pro_c(b, par):
                pool.wait_ge(S["csp_hi"], b + 1)
                if not (isinstance(b, int) and b == 0):
                    pool.wait_ge(S["csp_lo"], b)
                nc.gpsimd.tensor_tensor(cres[:, 0, :], ccur[:, par, :], csp[0:N, par, :], ALU.subtract).then_inc(S["csp_r"], 1)
                if not (isinstance(b, int) and b == 0):
                    pool.wait_ge(S["m_ready"], b)
                nc.gpsimd.tensor_tensor(cb[:, par, :], ccur[:, par, :], bcur[:, par, :], ALU.mult).then_inc(S["cb_ready"], 1)

            def pro_m(b, par):
                pool.wait_ge(S["csp_mid"], b + 1)
                pool.sem_inc(S["pool_past"], 1)
                nc.gpsimd.tensor_copy(cmid[:, :], cres[:, 0, :]).then_inc(S["pool_link"], 1)
                pool.wait_ge(S["pool_link"], b + link.n + 1)
                nc.gpsimd.tensor_tensor(cres[:, 1, :], cres[:, 0, :], cmid[:, :], ALU.subtract).then_inc(S["csp_r2"], 1)

            def pro_bd(b, par, n2):
                if n2 == 0:
                    pool.wait_ge(S["pro_bte"], b + 1)
                    if not (isinstance(b, int) and b < 2):
                        pool.wait_ge(S["dw_ready"], b * 16 - 16)
                n = slice(2 * n2, 2 * n2 + 2)
                for c in range(2):
                    m = nc.gpsimd.tensor_tensor(bd[:, par, c, n, :], bid[:, None, :].broadcast_to([P, 2, P + 1]),
                                                btok[:, par, c, n, None].broadcast_to([P, 2, P + 1]), ALU.mult)
                m.then_inc(S["bd_ready"], 1)

            def main(b, par, more):
                for s in range(16):
                    pool.wait_ge(S["p_ready"], b * 16 + s + 3)
                    nc.gpsimd.tensor_tensor(zb[:, s % 8, 0, :], zb[:, s % 8, 0, :], zb[:, s % 8, 1, :], ALU.add
                                            ).then_inc(S["q_ready"], 1)
                    if more:
                        if s == 3:
                            pro_c(b + 1, 1 - par)
                        if s == 5:
                            pro_m(b + 1, 1 - par)
                        if s == 8 and not (isinstance(b, int) and b == 6):
                            pro_x(b + 2, par)
                        if s >= 7 and s % 2:
                            pro_bd(b + 1, 1 - par, (s - 7) // 2)
                    if s in (1, 3, 5):
                        pro_bd(b, par, 5 + s // 2)

            pro_x(0, 0)
            pro_x(1, 1)
            for c in range(8):
                pool.wait_ge(S["w_less_1"], c + 1)
                nc.gpsimd.tensor_tensor(rests[c], rests[c], exps[c], ALU.subtract).then_inc(S["rest_ready"], 1)
            pro_c(0, 0)
            pro_m(0, 0)
            for n2 in range(5):
                pro_bd(0, 0, n2)
            main(0, 0, True)
            with pool.Fori(0, 2) as i:
                main(i * 2 + 1, 1, True)
                main(i * 2 + 2, 0, True)
            main(5, 1, True)
            main(6, 0, True)
            main(7, 1, False)

            pool.wait_ge(S["rows_g"], 16)

            def gather(e):
                pool.wait_ge(S["id_ready"], e + 1)
                if e > 3:
                    pool.wait_ge(S["ye_ready"], e - 3)
                for q in range(4):
                    nc.gpsimd.indirect_dma_start(
                        out=xg[:, e % 4, q, :], out_offset=None, in_=rows,
                        in_offset=bass.IndirectOffsetOnAxis(ap=idx[:, 4 * e + q:4 * e + q + 1], axis=0)
                        ).then_inc(S[f"xg_in{e % 4}"], 16)

            def add(e):
                pool.wait_ge(S["ye_ready"], e + 1)
                if e:
                    pool.wait_ge(S["added"], 64 * e)
                for q in range(4):
                    nc.gpsimd.indirect_dma_start(
                        out=moe, out_offset=bass.IndirectOffsetOnAxis(ap=idx[:, 4 * e + q:4 * e + q + 1], axis=0),
                        in_=ye[:, e % 2, q, :], in_offset=None, compute_op=ALU.add).then_inc(S["added"], 16)

            expert_steps(((0, gather), (3, add)))
            pool.wait_ge(S["added"], 64 * E0)
            for v in vmf:
                m = nc.gpsimd.memset(v, 0.0)
            m.then_inc(S["vm_zero"], 1)
            pool.wait_ge(S["ld_b"], 16)
            pool.wait_ge(S["dve_done"], 10)
            link.n = link.n + NB
            link(nc.gpsimd.tensor_copy(bhi, bias1))
            link(nc.gpsimd.tensor_tensor(bres, bias1, bhi, ALU.subtract))
            link(nc.gpsimd.tensor_copy(bmid, bres))
            link(nc.gpsimd.tensor_tensor(bres, bres, bmid, ALU.subtract))
            link(nc.gpsimd.tensor_copy(blo, bres))
            pool.sem_inc(S["b_split"], 1)
            pool.wait_ge(S["scattered"], 16)
            for w in range(2):
                pool.wait_ge(S["scattered"], (1 + w * NT) * 16)
                link(nc.gpsimd.tensor_copy(xnw[:, :, P + 1], mx8[:, :, w]))
                for t in range(NT):
                    nc.gpsimd.indirect_dma_start(
                        out=xd, out_offset=bass.IndirectOffsetOnAxis(ap=slot[:, w, t:t + 1], axis=0),
                        in_=xnw[:, t, :], in_offset=None).then_inc(S["scattered"], 16)

            def add1(k, u):
                pool.wait_ge(S["y_sb"], k + 1)
                if later(k, 1):
                    pool.wait_ge(S["added1"], k * 16)
                pool.sem_inc(S["pool_past"], 1)
                nc.gpsimd.indirect_dma_start(
                    out=out, out_offset=bass.IndirectOffsetOnAxis(ap=xs[:, u, P:P + 1].bitcast(I32), axis=0),
                    in_=ys[:, u % 4, :], in_offset=None, compute_op=ALU.add, bounds_check=T - 1, oob_is_err=False
                    ).then_inc(S["added1"], 16)

            pool.wait_ge(S["sum_out"], 64)
            slot_steps(pool, ((4, add1),))


def kernel(**inputs):
    import numpy as np
    import concourse.bacc as bacc
    from concourse.bass_utils import run_bass_kernel_spmd as run

    a = {k: np.asarray(v) for k, v in inputs.items()}
    f = np.float32
    r = np.arange(P)
    ident = np.eye(P, dtype=f)
    bid = np.zeros((P, P + 1), f)
    bid[r, r] = 1
    bid[r, r + 1] = -1
    sel = np.zeros((P, N, P), f)
    for part in range(3):
        sel[32 * part + np.arange(N), np.arange(N), :] = 1
    cf = np.concatenate([ident, bid, np.ones((P, P), f), np.triu(np.ones((P, P), f), 1),
                         np.tile(np.arange(P, dtype=f), (P, 1)), np.arange(P, dtype=f)[:, None], sel.reshape(P, -1)], axis=1)
    gam = (1.0 - np.exp(np.linspace(np.log(1.0 / 512.0), np.log(1.0 / 32.0), HEADS))).astype(f)
    diff = np.arange(L)[None, :] - np.arange(L)[:, None]
    dec = np.where(diff >= 0, gam[:, None, None] ** np.where(diff >= 0, diff, 0).astype(f), 0).astype(f)
    head = np.repeat(np.eye(HEADS, dtype=f), HD, axis=0)
    average = (head @ head.T / HD).astype(f)
    mask = np.concatenate([np.concatenate([dec[:, 0:P, :], dec[:, P:L, P:L]], axis=2).transpose(1, 0, 2).reshape(P, -1),
                           ident - average, average], axis=1)
    unit = np.where(np.arange(ROUNDS) < 15, 1 << np.maximum(28 - 2 * np.arange(ROUNDS), 0), 0)

    def rounds(three):
        return np.tile((unit[:, None] * np.array(three))[None, :, :, None], (P, 1, 1, E0))

    z = lambda v, n: np.ascontiguousarray(v.reshape(n, P).T)
    col = np.zeros((P, 44 + HEADS), f)
    col[:, 0] = a["L0_attn_ln_g"]
    col[:, 1] = a["L0_attn_ln_b"]
    col[:, 2:4] = z(a["L0_attn_conv_b"], 2)
    col[:, 4:6] = z(a["L0_attn_b_ll"][0:DI], 2)
    col[0:N, 6] = a["L0_attn_b_ll"][DI:DI + N]
    col[0:N, 7] = a["L0_attn_b_ll"][DI + N:]
    col[:, 8] = a["L0_attn_b_down"]
    col[:, 9:41] = z(a["L0_ffn_b1"], E0 * HC)
    col[:, 41] = a["L1_attn_gn_w"]
    col[:, 42] = a["L1_attn_gn_b"]
    col[:, 43] = EPS
    col[:, 44:] = head

    def blocks(w):
        o = np.zeros((P, P), f)
        for h in range(HEADS):
            o[h * HD:(h + 1) * HD, h * HD:(h + 1) * HD] = w[h]
        return o

    down = lambda w, e: w.reshape(e, HC, P, P).transpose(0, 2, 1, 3).reshape(e, P, HC * P)
    arrays = dict(
        x=a["L0_attn_X"].reshape(T, P), cf=cf, mask_d=mask, bits_i=rounds((1, 2, 3)).astype(np.int32), bits_f=rounds((1, 3, 1)).astype(f),
        cols=col, conv_t=a["L0_attn_conv_w"].reshape(DI, K).T,
        w_up1=a["L0_attn_W_up1"].T, w_up2=a["L0_attn_W_up2"].T, w_ll=a["L0_attn_W_ll"].T, a_log=a["L0_attn_A_log"],
        a_log_t=a["L0_attn_A_log"].T, w_down=a["L0_attn_W_down"].T, wr0=a["L0_ffn_Wr"], w1_0=a["L0_ffn_W1"],
        w2_0=down(a["L0_ffn_W2"], E0), b2_0=a["L0_ffn_b2"], wq=blocks(a["L1_attn_Wq"]), wk=blocks(a["L1_attn_Wk"]),
        wv=blocks(a["L1_attn_Wv"]), wg=a["L1_attn_W1"], wo=a["L1_attn_W2"], wr1=a["L1_ffn_Wr"], br1=a["L1_ffn_br"].reshape(1, E1),
        w1_1=a["L1_ffn_W1"], w2_1=down(a["L1_ffn_W2"], E1),
        b_1=np.concatenate([a["L1_ffn_b1"], a["L1_ffn_b2"]], axis=1))
    arrays = {k: np.ascontiguousarray(v) for k, v in arrays.items()}
    nc = bacc.Bacc("TRN2", target_bir_lowering=False, num_devices=1)
    ins = {k: nc.dram_tensor(f"in_{k}", v.shape, mybir.dt.from_np(v.dtype), kind="ExternalInput").ap()
           for k, v in arrays.items()}
    out = nc.dram_tensor("out_x", [T, P], F32, kind="ExternalOutput").ap()
    layer_pair(nc, out=out, **ins)
    res = run(nc, [{f"in_{k}": v for k, v in arrays.items()}], core_ids=[0])
    return res.results[0]["out_x"].reshape(NB, L, P)
```
